# Optimizing a Trainium2 kernel written in Bass

```python
import numpy as np
import jax
import jax.numpy as jnp

def _softmax(x, axis=-1):
    return jax.nn.softmax(x, axis=axis)

def _gelu(x):
    return jax.nn.gelu(x, approximate=True)

def _silu(x):
    return jax.nn.silu(x)

def _sigmoid(x):
    return jax.nn.sigmoid(x)

def _layernorm(x, axis=-1, eps=1e-05):
    m = jnp.mean(x, axis=axis, keepdims=True)
    v = jnp.var(x, axis=axis, keepdims=True)
    return (x - m) / jnp.sqrt(v + eps)

def _scatter_add(tgt, idx, src, axis=0):
    return tgt.at[idx].add(src)

def _segment_sum(src, seg, n):
    return jax.ops.segment_sum(src, seg, n)
kernel_name = 'mk_gnn_ffn_d1_gnn_r8_d94f2d'

def setup_inputs(seed: int=0):
    np.random.seed(seed)
    _w = jnp.asarray

    def _rec_inputs():
        import jax
        import jax.numpy as jnp
        _gk = jax.random.key(seed)
        x = -0.0003713 + 1 * jax.random.normal(jax.random.fold_in(_gk, 1), (6250, 256), jnp.float32)
        src = jax.random.randint(jax.random.fold_in(_gk, 2), (100000,), 0, 6250, jnp.int32)
        dst = jnp.minimum((6250 * jax.random.uniform(jax.random.fold_in(_gk, 3), (100000,)) ** 2.0).astype(jnp.int32), 49999)
        _o = jnp.argsort(dst, stable=True)
        src = src[_o]
        dst = dst[_o]
        return (x, src, dst)
    x, src, dst = _rec_inputs()

    def _L0_gnn_setup():
        import jax, jax.numpy as jnp
        import numpy as np
        N = 6250
        E = 100000
        DIN = 256
        DOUT = 256
        K = 3
        key = jax.random.key(seed)
        k1, k2, k3 = jax.random.split(key, 3)
        x = jax.random.normal(k1, (N, DIN), dtype=jnp.float32)
        edge_index = jax.random.randint(k2, (2, E), 0, N, dtype=jnp.int32)
        limit = float(np.sqrt(6.0 / (DIN + DOUT)))
        weight = jax.random.uniform(k3, (K + 1, DIN, DOUT), dtype=jnp.float32, minval=-limit, maxval=limit)
        bias = jnp.zeros((DOUT,), dtype=jnp.float32)
        return {'x': x, 'edge_index': edge_index, 'weight': weight, 'bias': bias}
    _L0_gnn_all = _L0_gnn_setup()
    _L0_gnn_in = {k: v for k, v in _L0_gnn_all.items() if k in ('weight', 'bias')}
    del _L0_gnn_all

    def _L0_ffn_setup():
        import jax, jax.numpy as jnp
        import numpy as np
        C = 256
        HID = 1024
        E = 8
        TEMP = 1.0
        key = jax.random.key(seed)
        ks = jax.random.split(key, 7)
        x = jax.random.normal(ks[0], (8, 2048, C), dtype=jnp.float32)
        W1 = jax.random.normal(ks[1], (C, HID), dtype=jnp.float32) * 0.02
        b1 = jnp.zeros((HID,), dtype=jnp.float32)
        Wg = jax.random.normal(ks[2], (HID, E), dtype=jnp.float32) * 0.02
        bg = jnp.zeros((E,), dtype=jnp.float32)
        Wd = jax.random.normal(ks[3], (E, HID, C), dtype=jnp.float32) * 0.02
        bd = jnp.zeros((E, C), dtype=jnp.float32)
        return {'x': x, 'W1': W1, 'b1': b1, 'Wg': Wg, 'bg': bg, 'Wd': Wd, 'bd': bd}
    _L0_ffn_all = _L0_ffn_setup()
    _L0_ffn_in = {k: v for k, v in _L0_ffn_all.items() if k in ('W1', 'b1', 'Wg', 'bg', 'Wd', 'bd')}
    del _L0_ffn_all
    return {'x': x, 'src': src, 'dst': dst, 'L0_gnn_weight': _L0_gnn_in['weight'], 'L0_gnn_bias': _L0_gnn_in['bias'], 'L0_ffn_W1': _L0_ffn_in['W1'], 'L0_ffn_b1': _L0_ffn_in['b1'], 'L0_ffn_Wg': _L0_ffn_in['Wg'], 'L0_ffn_bg': _L0_ffn_in['bg'], 'L0_ffn_Wd': _L0_ffn_in['Wd'], 'L0_ffn_bd': _L0_ffn_in['bd']}

def reference(x, src, dst, L0_gnn_weight, L0_gnn_bias, L0_ffn_W1, L0_ffn_b1, L0_ffn_Wg, L0_ffn_bg, L0_ffn_Wd, L0_ffn_bd):
    import jax
    import jax.numpy as jnp

    def _L0_gnn_ref(x, edge_index, weight, bias):
        import jax, jax.numpy as jnp
        import numpy as np
        N = 6250
        E = 100000
        DIN = 256
        DOUT = 256
        K = 3
        num_nodes = x.shape[0]
        loops = jnp.arange(num_nodes, dtype=edge_index.dtype)
        row = jnp.concatenate([edge_index[0], loops])
        col = jnp.concatenate([edge_index[1], loops])
        deg = jax.ops.segment_sum(jnp.ones_like(row, dtype=x.dtype), row, num_segments=num_nodes)
        deg_inv_sqrt = jnp.where(deg > 0, jax.lax.rsqrt(jnp.maximum(deg, 1e-30)), 0.0)
        Lvals = -deg_inv_sqrt[row] * deg_inv_sqrt[col]
        Lvals = jnp.where(row == col, Lvals + 1.0, Lvals)

        def spmm(v):
            return jax.ops.segment_sum(Lvals[:, None] * v[col], row, num_segments=num_nodes)
        out = jnp.matmul(x, weight[0])
        Tx_0 = x
        Tx_1 = spmm(x)
        out = out + jnp.matmul(Tx_1, weight[1])
        for k in range(2, K + 1):
            Tx_2 = 2.0 * spmm(Tx_1) - Tx_0
            out = out + jnp.matmul(Tx_2, weight[k])
            Tx_0, Tx_1 = (Tx_1, Tx_2)
        return out + bias

    def _L0_ffn_ref(x, W1, b1, Wg, bg, Wd, bd):
        import jax, jax.numpy as jnp
        import numpy as np
        C = 256
        HID = 1024
        E = 8
        TEMP = 1.0
        orig_shape = x.shape
        xf = x.reshape(-1, orig_shape[-1])
        H = jax.nn.gelu(xf @ W1 + b1, approximate=False)
        probs = jax.nn.softmax((H @ Wg + bg) / TEMP, axis=-1)
        assign = jnp.argmax(probs, axis=-1)
        out = jnp.zeros_like(xf)
        for e in range(Wd.shape[0]):
            y = H @ Wd[e] + bd[e]
            sel = (assign == e)[:, None]
            out = out + jnp.where(sel, probs[:, e:e + 1] * y, 0.0)
        return out.reshape(orig_shape)
    edge_index = jnp.stack([src, dst])
    x = x + _L0_gnn_ref(_layernorm(x, axis=-1), edge_index, L0_gnn_weight, L0_gnn_bias)
    x = x + _L0_ffn_ref(_layernorm(x, axis=-1)[None], L0_ffn_W1, L0_ffn_b1, L0_ffn_Wg, L0_ffn_bg, L0_ffn_Wd, L0_ffn_bd)[0]
    return x

_drawn_inputs = setup_inputs


def setup_inputs(seed=0):
    import zlib

    import numpy as np

    out = dict(_drawn_inputs(seed))
    spreads = {'L0_gnn_bias': (0.0, 0.1),
     'L0_ffn_b1': (0.0, 0.8),
     'L0_ffn_bg': (0.0, 0.8),
     'L0_ffn_bd': (0.0, 0.8)}
    factors = {'L0_ffn_W1': 8.0, 'L0_ffn_Wg': 8.0, 'L0_ffn_Wd': 8.0}
    for name, (base, spread) in spreads.items():
        noise = np.random.default_rng([zlib.crc32(name.encode()), seed]).standard_normal(out[name].shape)
        drawn = base * np.exp(spread * noise) if base else spread * noise
        out[name] = jnp.asarray(drawn.astype(out[name].dtype))
    for name, factor in factors.items():
        out[name] = (out[name] * factor).astype(out[name].dtype)
    return out
```

```python
from contextlib import ExitStack

import concourse.bass as bass
from concourse import mybir

F32 = mybir.dt.float32
BF16 = mybir.dt.bfloat16
I32 = mybir.dt.int32
U32 = mybir.dt.uint32
ALU = mybir.AluOpType
ACT = mybir.ActivationFunctionType
AX = mybir.AxisListType.X
DVE = mybir.EngineType.DVE
PEE = mybir.EngineType.PE

P = 128
MOMENTS = 5
UNROLL = 8
BOUNDED = "bounded by how the numbers are built"


def moments(dve, stats, mean, var, done, count):
    half = 128.0
    even, odd = stats[:, :, 1], stats[:, :, 4]
    dve.tensor_tensor(mean[:], even, odd, ALU.subtract).then_inc(done, 1)
    dve.wait_ge(done, count + 1)
    dve.scalar_tensor_tensor(var[:], mean[:], 0.25, mean[:], ALU.mult, ALU.mult).then_inc(done, 1)
    dve.wait_ge(done, count + 2)
    for q in (2, 5):
        dve.scalar_tensor_tensor(var[:], stats[:, :, q], 0.5 / half, var[:], ALU.mult, ALU.add).then_inc(done, 1)
        dve.wait_ge(done, count + (3 if q == 2 else 4))
    dve.tensor_tensor(mean[:], even, odd, ALU.add).then_inc(done, 1)
    dve.wait_ge(done, count + 5)


def in_turn(engine, total, steps):
    first, last = -min(lead for lead, _ in steps), total - max(lead for lead, _ in steps)
    rounds = (last - first) // UNROLL

    def one(n):
        for lead, f in steps:
            if 0 <= n + lead < total:
                f(n + lead, (n + lead) % UNROLL, (n + lead) // UNROLL)
    for n in range(-max(lead for lead, _ in steps), first):
        one(n)
    with engine.Fori(0, rounds) as i:
        for j in range(UNROLL):
            for lead, f in steps:
                m = first + j + lead
                f(i * UNROLL + m, m % UNROLL, i + m // UNROLL)
    for n in range(first + rounds * UNROLL, total - min(lead for lead, _ in steps)):
        one(n)


def gnn_ffn_kernel(nc, x, src, dst, gw, gb, w1, b1, wg, bg, wd, bd, out):
    NP, D = x.shape
    TILES = NP // P
    E = src.shape[0]
    KC = D // P
    CHUNKS = -(-E // P)
    SB = 8
    SN = SB * P
    J = 16
    ROUNDS = -(-(CHUNKS + TILES - 1) // J)
    ITEMS = ROUNDS * J
    HALF = ITEMS // 2
    WB = -(-ITEMS // P)
    AHEAD = 4
    COLBITS = 13
    COLMASK = (1 << COLBITS) - 1
    NORMAL = 1 << 29
    EPS = 1e-5
    HID = w1.shape[1]
    HC = HID // P
    NE = wd.shape[0]
    ETILES = TILES + NE - 1
    ROW = 260
    ESRC, EW = 125, 800
    G = 7
    assert ESRC * EW == E and EW <= SN and SN * P >= E and NP <= COLMASK + 1
    assert CHUNKS <= SB * P and TILES == G * G and ETILES % G == 0 and D == 2 * P

    xnT_d = nc.dram_tensor("xnT", [TILES, P, D], F32, kind="Internal").ap()
    table = [nc.dram_tensor(f"table{k}", [NP, D], F32, kind="Internal").ap() for k in range(3)]
    placed = nc.dram_tensor("placed", [ETILES * P, ROW], F32, kind="Internal").ap()

    outer = ExitStack()
    with outer:
        def sb(ctx, name, shape, dt=F32):
            return ctx.enter_context(nc.sbuf_tensor(name, shape, dt))

        def pb(ctx, name, shape, dt=F32):
            return ctx.enter_context(nc.psum_tensor(name, shape, dt))

        def sem(name):
            return outer.enter_context(nc.semaphore(name))

        ident = sb(outer, "ident", [P, P])
        lanes = sb(outer, "lanes", [P, P])
        ones = sb(outer, "ones", [P, P])
        bufA = sb(outer, "bufA", [P, TILES, ROW])

        graph = ExitStack()
        bufB = sb(graph, "bufB", [P, TILES, D])
        rel = sb(graph, "rel", [P, ITEMS + AHEAD])
        col = sb(graph, "col", [P, ITEMS], U32)
        tile_of = sb(graph, "tile_of", [1, ITEMS], I32)
        wk = sb(graph, "wk", [P, 4, KC, D])
        gbrow = sb(graph, "gbrow", [1, D])
        dis = sb(graph, "dis", [P, TILES])
        sc1 = sb(graph, "sc1", [P, TILES])
        sc2 = sb(graph, "sc2", [P, TILES])
        nd1 = sb(graph, "nd1", [P, TILES])
        nd2 = sb(graph, "nd2", [P, TILES])

        with ExitStack() as s1:
            edges = sb(s1, "edges", [P, 2, SN], I32)
            keys = [sb(s1, f"keys{i}", [P, SN]) for i in range(2)]
            sign0 = sb(s1, "sign0", [P, 1])
            lane_i = sb(s1, "lane_i", [P, P], I32)
            gray = sb(s1, "gray", [P, P], I32)
            bits = sb(s1, "bits", [P, P], I32)
            bitsf = sb(s1, "bitsf", [P, P])
            turn = sb(s1, "turn", [P, 7, P])
            part_i = sb(s1, "part_i", [P, 1], I32)
            chunk = sb(s1, "chunk", [P, SB])
            chunk1 = sb(s1, "chunk1", [P, SB, P])
            iw = sb(s1, "iw", [P, ITEMS])
            tmp = sb(s1, "tmp", [P, ITEMS])
            lohi_i = sb(s1, "lohi_i", [P, 2, SB], I32)
            lohi = sb(s1, "lohi", [P, 2, SB])
            pick = sb(s1, "pick", [P, SB * ITEMS])
            twf = sb(s1, "twf", [P, WB * P])
            relb = sb(s1, "relb", [P, ITEMS], BF16)
            lanesb = sb(s1, "lanesb", [P, P], BF16)
            pairs = sb(s1, "pairs", [P, ITEMS, 2], BF16)
            tile_hot = sb(s1, "tile_hot", [P, WB, TILES])
            deg = sb(s1, "deg", [P, TILES])
            stats = sb(s1, "stats", [P, TILES, 6])
            mean = sb(s1, "mean", [P, TILES])
            var = sb(s1, "var", [P, TILES])
            rstd = sb(s1, "rstd", [P, TILES])
            shift = sb(s1, "shift", [P, TILES])
            xn = sb(s1, "xn", [P, 3, D])
            half_neg = sb(s1, "half_neg", [P, TILES])
            xT = sb(s1, "xT", [P, G, D])
            psN = pb(s1, "psN", [P, 2, 512])
            psW = pb(s1, "psW", [P, 2, 2 * D])
            psS = pb(s1, "psS", [P, 2, 512])
            psI = pb(s1, "psI", [P, 2, 512])
            psM = psN[:, 0, :]

            edges_in, wk_in = sem("edges_in"), sem("wk_in")
            x_in = [sem(f"x_in{g}") for g in range(G)]
            consts = sem("consts")
            edges_set = sem("edges_set")
            rstd_done, normed = sem("rstd_done"), sem("normed")
            ln_seq, pool_seq = sem("ln_seq"), sem("pool_seq")
            turned, xT_set, mm_done, mm_out = sem("turned"), sem("xT_set"), sem("mm_done"), sem("mm_out")
            xT_out = [sem(f"xT_out{j}") for j in range(G)]
            seq = sem("seq")
            sort_T = sem("sort_T")
            quant_ready, item_sum, item_out = sem("quant_ready"), sem("item_sum"), sem("item_out")
            tw_ready, twT_done = sem("tw_ready"), sem("twT_done")
            level_sorted = sem("level_sorted")
            hot_ready, hist_mm, hist_out = sem("hot_ready"), sem("hist_mm"), sem("hist_out")
            cnt_turned, cnt_set, deg_done = sem("cnt_turned"), sem("cnt_set"), sem("deg_done")
            deg_set, dis_done = sem("deg_set"), sem("dis_done")

            at, source = (1 + 55) % 2, {}
            for k in range(1, 8):
                for way in range(2):
                    source[k, way] = at
                    at = (at + 1 + (k if way == 0 else 10)) % 2
            srt = keys[at][:].bitcast(I32)
            rowf, colf = keys[1 - at], keys[at]
            selff = edges[:, 0, :].bitcast(F32)
            picks = pick[:].rearrange("p (b w) -> p b w", b=SB)
            counts = pick[:, 0:WB * P * 2].rearrange("p (w s) -> p w s", s=2)
            countsT = pick[:, WB * P * 2:WB * P * 4].rearrange("p (m r) -> p m r", r=P)
            hot = pick[:, WB * P * 4:WB * P * 4 + J * P].bitcast(BF16).rearrange("p (h j r) -> p h j r", h=2, j=J)

            block = s1.enter_context(nc.Block())

            @block.sync
            def _(sp):
                sp.wait_ge(edges_set, 1)
                sp.dma_start(edges[0:ESRC, 0, 0:EW], src.rearrange("(p f) -> p f", f=EW)).then_inc(edges_in, 16)
                sp.dma_start(edges[0:ESRC, 1, 0:EW], dst.rearrange("(p f) -> p f", f=EW)).then_inc(edges_in, 16)
                for g in range(G):
                    sp.dma_start(bufA[:, g * G:(g + 1) * G, 0:D],
                                 x[g * G * P:(g + 1) * G * P, :].rearrange("(t p) f -> p t f", p=P)).then_inc(x_in[g], 16)
                for k in range(4):
                    sp.dma_start(wk[:, k, :, :], gw[k].rearrange("(c f) o -> f c o", f=P)).then_inc(wk_in, 16)
                sp.dma_start(gbrow[:], gb.rearrange("(a o) -> a o", a=1)).then_inc(wk_in, 16)
                def store(i):
                    for j in range(G):
                        sp.wait_ge(xT_set, i * G + (j + 1))
                        sp.dma_start(xnT_d[bass.ds(i * G + j, 1)].rearrange("a p f -> p (a f)"), xT[:, j, :]).then_inc(xT_out[j], 16)
                store(0)
                with sp.Fori(1, G) as i:
                    store(i)
                for j in range(G):
                    sp.wait_ge(xT_out[j], 16 * G)

            @block.gpsimd
            def _(pool):
                pool.memset(edges[:, 0, :], NP - 1).then_inc(pool_seq, 1)
                pool.memset(edges[:, 1, :], 0).then_inc(pool_seq, 1)
                pool.wait_ge(pool_seq, 2)
                pool.sem_inc(edges_set, 1)
                pool.iota(lane_i[:], [[1, P]], base=0, channel_multiplier=0).then_inc(consts, 1)
                pool.iota(part_i[:], [[0, 1]], base=0, channel_multiplier=1).then_inc(consts, 1)
                pool.iota(lanes[:], [[1, P]], base=0, channel_multiplier=0, allow_small_or_imprecise_dtypes=True).then_inc(consts, 1)
                pool.iota(iw[:], [[1, ITEMS]], base=0, channel_multiplier=0, allow_small_or_imprecise_dtypes=True).then_inc(consts, 1)
                pool.iota(chunk[:], [[1, SB]], base=0, channel_multiplier=SB, allow_small_or_imprecise_dtypes=True).then_inc(consts, 1)
                pool.iota(chunk1[:], [[1, SB], [0, P]], base=1, channel_multiplier=SB, allow_small_or_imprecise_dtypes=True).then_inc(consts, 1)
                pool.memset(ident[:], 0.0).then_inc(pool_seq, 1)
                pool.memset(ones[:], 1.0).then_inc(consts, 1)
                pool.memset(half_neg[:], -0.5).then_inc(pool_seq, 1)
                pool.wait_ge(pool_seq, 4)
                pool.affine_select(out=ident[:], in_=ident[:], compare_op=ALU.not_equal, fill=1.0, base=0,
                                   pattern=[[-1, P]], channel_multiplier=1).then_inc(consts, 1)
                pool.wait_ge(ln_seq, TILES + MOMENTS)
                pool.tensor_scalar(rstd[:], var[:], EPS, None, ALU.add).then_inc(pool_seq, 1)
                pool.wait_ge(pool_seq, 5)
                pool.tensor_tensor(rstd[:], rstd[:], half_neg[:], ALU.pow).then_inc(pool_seq, 1)
                pool.wait_ge(pool_seq, 6)
                pool.tensor_tensor(shift[:], mean[:], rstd[:], ALU.mult).then_inc(pool_seq, 1)
                pool.wait_ge(pool_seq, 7)
                pool.tensor_scalar(shift[:], shift[:], -0.5, None, ALU.mult).then_inc(rstd_done, 1)
                pool.wait_ge(deg_set, 1)
                pool.tensor_tensor(dis[:], deg[:], half_neg[:], ALU.pow).then_inc(dis_done, 1)

            @block.scalar
            def _(act):
                def norm(i, j):
                    act.activation(xn[:, j % 3, :], bufA[:, bass.ds(i * G + j, 1), 0:D].rearrange("p a f -> p (a f)"), ACT.Identity,
                                   bias=shift[:, bass.ds(i * G + j, 1)], scale=rstd[:, bass.ds(i * G + j, 1)]).then_inc(normed, 1)

                def xT_evac(i, j, first):
                    act.wait_ge(turned, i * G + (j + 1))
                    if not first:
                        act.wait_ge(xT_out[j], i * 16)
                    act.copy(xT[:, j, :], psN[:, j % 2, 0:D]).then_inc(xT_set, 1)

                def mm_evac(i, j):
                    act.wait_ge(rstd_done, 1)
                    act.wait_ge(mm_done, i * G + (j + 1))
                    act.copy(bufA[:, bass.ds(i * G + j, 1), 0:D].rearrange("p a f -> p (a f)"), psW[:, j % 2, 0:D])
                    act.copy(bufB[:, bass.ds(i * G + j, 1), :].rearrange("p a f -> p (a f)"), psW[:, j % 2, D:2 * D]).then_inc(mm_out, 1)

                def group(i, first):
                    norm(i, 0)
                    norm(i, 1)
                    xT_evac(i, 0, first)
                    for j in range(G):
                        if j + 2 < G:
                            norm(i, j + 2)
                        if j + 1 < G:
                            xT_evac(i, j + 1, first)
                        mm_evac(i, j)
                act.wait_ge(rstd_done, 1)
                group(0, True)
                with act.Fori(1, G) as i:
                    group(i, False)

                with act.Fori(0, ROUNDS // 2) as i:
                    for h in range(2):
                        act.wait_ge(rstd_done, 1)
                        act.wait_ge(hist_mm, i * 2 + (h + 1))
                        act.copy(counts[:, bass.ds(i * (2 * J) + h * J, J), :], psW[:, h, 0:2 * J].rearrange("p (j s) -> p j s", s=2)).then_inc(hist_out, 1)

            @block.tensor
            def _(pe):
                pe.wait_ge(consts, 8)

                def turn_tile(i, j, first):
                    pe.wait_ge(normed, i * G + (j + 1))
                    if not (first and j == 0) and j != 1:
                        pe.wait_ge(xT_set, i * G + max(j - 1, 0))
                    for c in range(KC):
                        last = pe.transpose(psN[:, j % 2, c * P:(c + 1) * P],
                                            xn[:, j % 3, c * P:(c + 1) * P], ident[:])
                    last.then_inc(turned, 1)

                def mm_tile(i, j, first):
                    pe.wait_ge(xT_set, i * G + (j + 1))
                    if not (first and j == 0) and j != 1:
                        pe.wait_ge(mm_out, i * G + max(j - 1, 0))
                    for q, k in enumerate((3, 2)):
                        for c in range(KC):
                            last = pe.matmul(psW[:, j % 2, q * D:(q + 1) * D], xT[:, j, c * P:(c + 1) * P], wk[:, k, c, :],
                                             start=(c == 0), stop=(c == KC - 1))
                    last.then_inc(mm_done, 1)

                def group(i, first):
                    turn_tile(i, 0, first)
                    for j in range(G):
                        if j + 1 < G:
                            turn_tile(i, j + 1, first)
                        mm_tile(i, j, first)
                pe.wait_ge(wk_in, 16 * 5)
                group(0, True)
                with pe.Fori(1, G) as i:
                    group(i, False)

                for k in range(1, 8):
                    for way in range(2):
                        pe.wait_ge(level_sorted, 2 * (k - 1) + way + 1)
                        for b in range(SB):
                            last = pe.transpose(psS[:, b // 4, (b % 4) * P:(b % 4 + 1) * P],
                                                keys[source[k, way]][:, b * P:(b + 1) * P], ident[:])
                            if b % 4 == 3:
                                last.then_inc(sort_T, 1)

                pe.wait_ge(quant_ready, 1)
                for q, quant in enumerate((rowf, colf, selff, None)):
                    ps = (psS, psI)[q % 2]
                    if q >= 2:
                        pe.wait_ge(item_out, q - 1)
                    for h in range(2):
                        for b in range(SB):
                            lhs = chunk1[:, b, :] if quant is None else quant[:, b * P:(b + 1) * P]
                            last = pe.matmul(ps[:, h, 0:HALF], lhs, picks[:, b, h * HALF:(h + 1) * HALF],
                                             start=(b == 0), stop=(b == SB - 1))
                    last.then_inc(item_sum, 1)
                pe.wait_ge(tw_ready, 1)
                for q in range(WB):
                    last = pe.matmul(psM[:, q:q + 1], twf[:, q * P:(q + 1) * P], ident[:, 0:1], start=True, stop=True)
                last.then_inc(twT_done, 1)

                def count_round(i, h, first):
                    pe.wait_ge(hot_ready, i * 2 + (h + 1))
                    if first:
                        pe.wait_ge(mm_out, TILES)
                    else:
                        pe.wait_ge(hist_out, i * 2 + (h - 1))
                    for j in range(J):
                        last = pe.matmul(psW[:, h, 2 * j:2 * j + 2], hot[:, h, j, :],
                                         pairs[:, bass.ds(i * (2 * J) + (h * J + j), 1), :].rearrange("p a s -> p (a s)"), start=True, stop=True)
                    last.then_inc(hist_mm, 1)
                for h in range(2):
                    count_round(0, h, True)
                with pe.Fori(1, ROUNDS // 2) as i:
                    for h in range(2):
                        count_round(i, h, False)
                pe.wait_ge(hist_out, ROUNDS)
                pe.wait_ge(item_out, 4)
                for m in range(2 * WB):
                    ps = psS if m < 8 else psI
                    last = pe.transpose(ps[:, m % 8 // 4, m % 4 * P:(m % 4 + 1) * P], counts[:, m // 2 * P:(m // 2 + 1) * P, m % 2], ident[:])
                last.then_inc(cnt_turned, 1)
                pe.wait_ge(cnt_set, 1)
                for s in range(2):
                    for q in range(WB):
                        last = pe.matmul(psM[:, s * P:s * P + TILES], countsT[:, 2 * q + s, :], tile_hot[:, q, :],
                                         start=(q == 0), stop=(q == WB - 1))
                last.then_inc(deg_done, 1)

            @block.vector
            def _(dve):
                count = [0]

                def step(ins):
                    count[0] += 1
                    ins.then_inc(seq, 1)

                def settle():
                    dve.wait_ge(seq, count[0])

                for g in range(G):
                    dve.wait_ge(x_in[g], 16)
                with dve.Fori(0, TILES) as t:
                    dve.bn_stats(stats[:, bass.ds(t, 1), :].rearrange("p a f -> p (a f)"),
                                 bufA[:, bass.ds(t, 1), 0:D].rearrange("p a f -> p (a f)")).then_inc(ln_seq, 1)
                dve.wait_ge(ln_seq, TILES)
                moments(dve, stats, mean, var, ln_seq, TILES)

                dve.wait_ge(edges_in, 32)
                dve.wait_ge(consts, 8)
                e_row, e_col = edges[:, 0, :], edges[:, 1, :]
                step(dve.tensor_scalar(e_row, e_row, COLBITS, NORMAL, ALU.logical_shift_left, ALU.bitwise_or))
                step(dve.tensor_scalar(part_i[:], part_i[:], 1, None, ALU.bitwise_and))
                settle()
                step(dve.tensor_tensor(keys[0][:].bitcast(I32), e_row, e_col, ALU.bitwise_or))
                step(dve.tensor_copy(sign0[:], part_i[:]))
                step(dve.tensor_scalar(bits[:], lane_i[:], 1, None, ALU.logical_shift_right))
                settle()
                step(dve.tensor_scalar(sign0[:], sign0[:], -2.0, 1.0, ALU.mult, ALU.add))
                step(dve.tensor_tensor(gray[:], lane_i[:], bits[:], ALU.bitwise_xor))
                settle()
                for k in range(7):
                    step(dve.tensor_scalar(bits[:], gray[:], k, 1, ALU.logical_shift_right, ALU.bitwise_and))
                    settle()
                    step(dve.tensor_copy(bitsf[:], bits[:]))
                    settle()
                    step(dve.tensor_scalar(turn[:, k, :], bitsf[:], -2.0, 1.0, ALU.mult, ALU.add))
                    settle()
                step(dve.tensor_scalar(keys[1][:], keys[0][:], sign0[:, 0:1], None, ALU.mult))

                buf = 1

                def compare(dist, flip):
                    nonlocal buf
                    a = keys[buf][:].rearrange("p (n two d) -> p n two d", two=2, d=dist)
                    o = keys[1 - buf][:].rearrange("p (n two d) -> p n two d", two=2, d=dist)
                    hi = a[:, :, 1, ::-1] if flip else a[:, :, 1, :]
                    settle()
                    step(dve.tensor_tensor(o[:, :, 0, :], a[:, :, 0, :], hi, ALU.min))
                    step(dve.tensor_tensor(o[:, :, 1, :], a[:, :, 0, :], hi, ALU.max))
                    buf = 1 - buf

                for k in range(10):
                    compare(1 << k, flip=k > 0)
                    for d in reversed(range(k)):
                        compare(1 << d, flip=False)
                moves = 0
                for k in range(1, 8):
                    for way in range(2):
                        settle()
                        dve.sem_inc(level_sorted, 1)
                        assert source[k, way] == buf
                        for h in range(2):
                            moves += 1
                            dve.wait_ge(sort_T, moves)
                            o = keys[1 - buf][:, h * 512:(h + 1) * 512]
                            if way == 0:
                                step(dve.tensor_tensor(o.rearrange("p (b l) -> p b l", l=P), psS[:, h, :].rearrange("p (b l) -> p b l", l=P),
                                                       turn[:, k - 1:k, :].to_broadcast([P, 4, P]), ALU.mult))
                            else:
                                step(dve.tensor_copy(o, psS[:, h, :]))
                        buf = 1 - buf
                        for d in reversed(range(k if way == 0 else 10)):
                            compare(1 << d, flip=False)
                settle()
                step(dve.tensor_scalar(edges[:, 0, :], srt, COLBITS, COLMASK, ALU.logical_shift_right, ALU.bitwise_and))
                step(dve.tensor_scalar(edges[:, 1, :], srt, COLMASK, None, ALU.bitwise_and))
                settle()
                blocks = edges[:, 0, :].rearrange("p (b l) -> p b l", l=P)
                step(dve.tensor_scalar(lohi_i[:, 0, :], blocks[:, :, 0], 7, None, ALU.logical_shift_right))
                step(dve.tensor_scalar(lohi_i[:, 1, :], blocks[:, :, P - 1], 7, None, ALU.logical_shift_right))
                step(dve.tensor_copy(rowf[:], edges[:, 0, :]))
                step(dve.tensor_copy(colf[:], edges[:, 1, :]))
                settle()
                step(dve.tensor_copy(lohi[:], lohi_i[:]))
                step(dve.tensor_tensor(selff, rowf[:], colf[:], ALU.is_equal))
                settle()
                for s in range(2):
                    step(dve.tensor_tensor(lohi[:, s, :], lohi[:, s, :], chunk[:], ALU.add))
                settle()
                step(dve.scalar_tensor_tensor(rowf[:], chunk1[:].rearrange("p b l -> p (b l)"), float(P), rowf[:], ALU.mult, ALU.add))
                for b in range(SB):
                    step(dve.tensor_scalar(tmp[:], iw[:], lohi[:, 0, b:b + 1], None, ALU.is_ge))
                    settle()
                    step(dve.scalar_tensor_tensor(picks[:, b, :], iw[:], lohi[:, 1, b:b + 1], tmp[:], ALU.is_le, ALU.mult))
                    settle()
                step(dve.memset(rel[:, ITEMS:ITEMS + AHEAD], -1.0))
                step(dve.memset(twf[:, ITEMS:WB * P], -1.0))
                step(dve.memset(pairs[:], 1.0))
                step(dve.tensor_copy(lanesb[:], lanes[:]))
                step(dve.tensor_scalar(tmp[:], iw[:], float(P), float(P), ALU.mult, ALU.add))
                settle()
                dve.sem_inc(quant_ready, 1)

                def halves(t):
                    return t[:, 0:ITEMS].rearrange("p (h w) -> p h w", h=2)
                dve.wait_ge(item_sum, 1)
                dve.tensor_tensor(halves(rel), psS[:, :, 0:HALF], halves(tmp), ALU.subtract).then_inc(item_out, 1)
                dve.wait_ge(item_sum, 2)
                dve.tensor_copy(halves(col), psI[:, :, 0:HALF]).then_inc(item_out, 1)
                dve.wait_ge(item_out, 2)
                step(dve.tensor_copy(relb[:], rel[:, 0:ITEMS]))
                dve.wait_ge(item_sum, 3)
                dve.tensor_copy(pairs[:, :, 1].rearrange("p (h w) -> p h w", h=2), psS[:, :, 0:HALF]).then_inc(item_out, 1)
                dve.wait_ge(item_sum, 4)
                dve.scalar_tensor_tensor(halves(tmp), halves(iw), 1.0, psI[:, :, 0:HALF], ALU.add, ALU.subtract).then_inc(item_out, 1)
                dve.wait_ge(item_out, 4)
                step(dve.tensor_scalar(twf[:, 0:ITEMS], tmp[:], float(TILES - 1), None, ALU.min))
                step(dve.memset(counts[:, ITEMS:WB * P, :], 0.0))
                settle()
                step(dve.tensor_copy(tile_of[:], twf[0:1, 0:ITEMS]))
                dve.sem_inc(tw_ready, 1)

                def hot_round(i, h, first):
                    if not first:
                        dve.wait_ge(hist_mm, i * 2 + (h - 1))
                    dve.tensor_tensor(hot[:, h, :, :], lanesb[:].unsqueeze(1).to_broadcast([P, J, P]),
                                      relb[:, bass.ds(i * (2 * J) + h * J, J)].unsqueeze(2).to_broadcast([P, J, P]),
                                      ALU.is_equal).then_inc(hot_ready, 1)
                for h in range(2):
                    hot_round(0, h, True)
                with dve.Fori(1, ROUNDS // 2) as i:
                    for h in range(2):
                        hot_round(i, h, False)
                dve.wait_ge(twT_done, 1)
                for q in range(WB):
                    step(dve.tensor_scalar(tile_hot[:, q, :], lanes[:, 0:TILES], psM[:, q:q + 1], None, ALU.is_equal))
                dve.wait_ge(cnt_turned, 1)
                step(dve.tensor_copy(countsT[:, 0:8, :], psS[:].rearrange("p h (m r) -> p (h m) r", r=P)))
                step(dve.tensor_copy(countsT[:, 8:2 * WB, :], psI[:].rearrange("p h (m r) -> p (h m) r", r=P)[:, 0:2 * WB - 8, :]))
                settle()
                dve.sem_inc(cnt_set, 1)
                dve.wait_ge(deg_done, 1)
                dve.tensor_scalar(deg[:], psM[:, 0:TILES], 1.0, None, ALU.add).then_inc(deg_set, 1)
                dve.wait_ge(dis_done, 1)
                step(dve.tensor_tensor(sc2[:], dis[:], dis[:], ALU.mult))
                settle()
                step(dve.scalar_tensor_tensor(sc1[:], psM[:, P:P + TILES], 1.0, sc2[:], ALU.add, ALU.subtract))
                settle()
                step(dve.tensor_scalar(sc2[:], sc1[:], 2.0, None, ALU.mult))
                step(dve.tensor_scalar(nd1[:], dis[:], -1.0, None, ALU.mult))
                step(dve.tensor_scalar(nd2[:], dis[:], -2.0, None, ALU.mult))
                settle()
        with ExitStack() as s2:
            bufC = sb(s2, "bufC", [P, TILES, D])
            gath = sb(s2, "gath", [P, J, D])
            idx = sb(s2, "idx", [P, J], U32)
            hot = sb(s2, "hot_r", [P, AHEAD, P])
            xnT = sb(s2, "xnT_s", [P, D])
            xr = sb(s2, "xr", [P, D])
            empty = sb(s2, "empty", [P, ROW])
            psP = pb(s2, "psP", [P, AHEAD, 512])
            psX = pb(s2, "psX", [P, 512])

            PASSES = ((2, bufB, bufA, bufC, bufC, sc2, nd2),
                      (1, bufC, bufB, bufA, bufA, sc2, nd2),
                      (0, bufA, bufC, None, bufB, sc1, nd1))
            u_set = sem("u_set")
            u_out = [[sem(f"u_out{n}_{g}") for g in range(G)] for n in range(3)]
            landed = [sem(f"landed{j}") for j in range(J)]
            gathering = sem("gathering")
            idx_set, hot_set, item_mm, item_added = sem("idx_set"), sem("hot_set"), sem("item_mm"), sem("item_added")
            xnT_load, xr_load = sem("xnT_load"), sem("xr_load")
            next_mm, next_diff, next_set = sem("next_mm"), sem("next_diff"), sem("next_set")
            b_set = sem("b_set")
            empty_set, empty_out = sem("empty_set"), sem("empty_out")

            def tile(buf, t):
                return buf[:, bass.ds(t, 1), 0:D].rearrange("p a f -> p (a f)")

            block = s2.enter_context(nc.Block())

            @block.sync
            def _(sp):
                sp.wait_ge(empty_set, 2)
                sp.dma_start(placed.rearrange("(t p) f -> p t f", p=P),
                             empty[:].unsqueeze(1).to_broadcast([P, ETILES, ROW])).then_inc(empty_out, 16)
                for n, (k, _, _, nxt, staging, _, _) in enumerate(PASSES):
                    for g in range(G):
                        sp.wait_ge(u_set, n * TILES + (g + 1) * G)
                        sp.dma_start(table[n][g * G * P:(g + 1) * G * P, :].rearrange("(t p) f -> p t f", p=P),
                                     staging[:, g * G:(g + 1) * G, 0:D]).then_inc(u_out[n][g], 16)
                    if nxt is None:
                        break

                    def load(t, first):
                        if not first:
                            sp.wait_ge(next_set, t + n * TILES)
                        sp.dma_start(xnT[:], xnT_d[bass.ds(t, 1)].rearrange("a p f -> p (a f)")).then_inc(xnT_load, 16)
                        if k == 1:
                            sp.dma_start(xr[:], x[bass.ds(t * P, P), :]).then_inc(xr_load, 16)
                    load(0, n == 0)
                    with sp.Fori(1, TILES) as t:
                        load(t, False)
                sp.wait_ge(empty_out, 16)

            @block.gpsimd
            def _(pool):
                pool.memset(empty[:], 0.0).then_inc(empty_set, 1)
                pool.wait_ge(empty_set, 1)
                pool.memset(empty[:].bitcast(I32)[:, D + 1:D + 2], NP).then_inc(empty_set, 1)
                for n in range(3):
                    for g in range(G):
                        pool.wait_ge(u_out[n][g], 16)
                    with pool.Fori(0, ROUNDS) as i:
                        for j in range(J):
                            if j % (J // 2) == 0:
                                pool.wait_ge(idx_set, i * 2 + (n * 2 * ROUNDS + j // (J // 2) + 1))
                                pool.sem_inc(gathering, 1)
                            pool.indirect_dma_start(out=gath[:, j, :], out_offset=None, in_=table[n],
                                                    in_offset=bass.IndirectOffsetOnAxis(ap=idx[:, j:j + 1], axis=0)).then_inc(landed[j], 16)

            @block.scalar
            def _(act):
                for n, (_, _, _, _, staging, _, _) in enumerate(PASSES):
                    before = bufA if n == 0 else PASSES[n - 1][1]
                    with act.Fori(0, TILES) as t:
                        if n > 0:
                            act.wait_ge(empty_set, 1)
                            act.wait_ge(b_set, t + ((n - 1) * TILES + 1))
                        act.mul(tile(staging, t), tile(before, t), dis[:, bass.ds(t, 1)]).then_inc(u_set, 1)

                    def refresh(i, h, first):
                        c = h * (J // 2)
                        if not first:
                            act.wait_ge(empty_set, 1)
                            act.wait_ge(item_mm, i * J + (n * ITEMS - J + c + J // 2))
                        act.copy(idx[:, c:c + J // 2], col[:, bass.ds(i * J + c, J // 2)]).then_inc(idx_set, 1)
                    for h in range(2):
                        refresh(0, h, True)
                    with act.Fori(1, ROUNDS) as i:
                        for h in range(2):
                            refresh(i, h, False)

            @block.vector
            def _(dve):
                dve.wait_ge(empty_set, 1)
                for n, (k, acc, prev, nxt, staging, factor, minus) in enumerate(PASSES):
                    def one_hot(i, j):
                        dve.tensor_scalar(hot[:, j % AHEAD, :], lanes[:], rel[:, bass.ds(i * J + j, 1)], None, ALU.is_equal).then_inc(hot_set, 1)

                    def items(i, first):
                        _, ts = nc.values_load_multi_w_load_instructions(
                            tile_of[0:1, bass.ds(i * J, J)], engines=[DVE], min_val=0, max_val=TILES - 1, skip_runtime_bounds_check_because=BOUNDED)
                        for j in range(J):
                            if not (first and j == 0):
                                dve.wait_ge(item_added, i * J + (n * ITEMS + j))
                            dve.wait_ge(item_mm, i * J + (n * ITEMS + j + 1))
                            dve.scalar_tensor_tensor(out=tile(acc, ts[j]), in0=psP[:, j % AHEAD, 0:D], scalar=minus[:, bass.ds(ts[j], 1)],
                                                     in1=tile(acc, ts[j]), op0=ALU.mult, op1=ALU.add).then_inc(item_added, 1)
                            one_hot(i, j + AHEAD)

                    def prepare(t):
                        dve.wait_ge(next_mm, t + (n * TILES + 1))
                        if k == 2:
                            dve.tensor_tensor(tile(nxt, t), psX[:, 0:D], tile(prev, t), ALU.subtract).then_inc(next_set, 1)
                        else:
                            dve.tensor_tensor(tile(nxt, t), psX[:, 0:D], tile(prev, t), ALU.subtract).then_inc(next_diff, 1)
                            dve.wait_ge(next_diff, t + 1)
                            dve.wait_ge(xr_load, (t + 1) * 16)
                            dve.tensor_tensor(tile(nxt, t), tile(nxt, t), xr[:], ALU.add).then_inc(next_set, 1)

                    if n > 0:
                        dve.wait_ge(hot_set, n * (ITEMS + AHEAD))
                    for j in range(AHEAD):
                        one_hot(0, j)
                    if nxt is None:
                        with dve.Fori(0, ROUNDS) as i:
                            items(i, False)
                    else:
                        items(0, n == 0)
                        for g in range(G):
                            dve.wait_ge(u_out[n][g], 16)
                        prepare(0)
                        with dve.Fori(1, TILES) as i:
                            items(i, False)
                            prepare(i)
                        with dve.Fori(TILES, ROUNDS) as i:
                            items(i, False)
                    dve.wait_ge(item_added, (n + 1) * ITEMS)
                    if nxt is None:
                        for g in range(G):
                            dve.wait_ge(u_out[n][g], 16)
                    with dve.Fori(0, TILES) as t:
                        dve.scalar_tensor_tensor(out=tile(acc, t), in0=tile(prev, t), scalar=factor[:, bass.ds(t, 1)], in1=tile(acc, t),
                                                 op0=ALU.mult, op1=ALU.add).then_inc(b_set, 1)
                dve.wait_ge(b_set, 3 * TILES)

            @block.tensor
            def _(pe):
                for n, (k, _, _, nxt, _, _, _) in enumerate(PASSES):
                    def items(i, first):
                        for j in range(J):
                            pe.wait_ge(landed[j], (i + (n * ROUNDS + 1)) * 16)
                            pe.wait_ge(hot_set, i * J + (n * (ITEMS + AHEAD) + j + 1))
                            if not (first and j < AHEAD):
                                pe.wait_ge(item_added, i * J + (n * ITEMS + j + 1 - AHEAD))
                            pe.matmul(psP[:, j % AHEAD, 0:D], hot[:, j % AHEAD, :], gath[:, j, :], start=True, stop=True).then_inc(item_mm, 1)

                    def prepare(t, first):
                        pe.wait_ge(xnT_load, (t + (n * TILES + 1)) * 16)
                        if not first:
                            pe.wait_ge(next_set, t + n * TILES)
                        for c in range(KC):
                            last = pe.matmul(psX[:, 0:D], xnT[:, c * P:(c + 1) * P], wk[:, k - 1, c, :], start=(c == 0),
                                             stop=(c == KC - 1 and k == 2))
                        if k == 1:
                            last = pe.matmul(psX[:, 0:D], ones[0:1, :], gbrow[:], start=False, stop=True)
                        last.then_inc(next_mm, 1)

                    if nxt is None:
                        with pe.Fori(0, ROUNDS) as i:
                            items(i, False)
                    else:
                        items(0, n == 0)
                        prepare(0, n == 0)
                        with pe.Fori(1, TILES) as i:
                            items(i, False)
                            prepare(i, False)
                        with pe.Fori(TILES, ROUNDS) as i:
                            items(i, False)
        graph.close()

        ffn = ExitStack()
        w1_s = sb(ffn, "w1_s", [P, KC, HID])
        b1_s = sb(ffn, "b1_s", [P, HC])
        wd_s = sb(ffn, "wd_s", [P, NE, HC, D])
        bd_s = sb(ffn, "bd_s", [1, NE, D])
        z = sb(ffn, "z", [P, 4, D])
        zT = sb(ffn, "zT", [P, 2, D])
        hT = sb(ffn, "hT", [P, 2, HC, P])
        expert = sb(ffn, "expert", [1, ETILES], I32)
        minus_half = sb(ffn, "minus_half", [P, TILES])
        eps = sb(ffn, "eps", [P, 1])
        psT = pb(ffn, "psT", [P, 2, 512])
        psH = pb(ffn, "psH", [P, 2, 2, 512])
        psO = pb(ffn, "psO", [P, 2, 512])
        w1_in, wd_in = sem("w1_in"), sem("wd_in")

        def ffn_turn(pe, z_set, turned, zT_set):
            def f(n, m, _):
                pe.wait_ge(zT_set, n + 1)
                pe.wait_ge(z_set, n + 1)
                for c in range(KC):
                    last = pe.transpose(psT[:, m % 2, c * P:(c + 1) * P], z[:, m % 4, c * P:(c + 1) * P], ident[:])
                last.then_inc(turned, 1)
            return f

        def ffn_hidden(pe, zT_set, hid, gelus):
            def f(n, m, _):
                pe.wait_ge(zT_set, n + 3)
                for h in range(2):
                    pe.wait_ge(gelus, n * 2 + (h + 1))
                    for q in range(HC // 2):
                        hc = h * (HC // 2) + q
                        for c in range(KC):
                            last = pe.matmul(psH[:, m % 2, h, q * P:(q + 1) * P], w1_s[:, c, hc * P:(hc + 1) * P], zT[:, m % 2, c * P:(c + 1) * P],
                                             start=(c == 0), stop=(c == KC - 1))
                    last.then_inc(hid, 1)
            return f

        def ffn_gelu(act, hid, gelus, tails):
            def f(n, m, _):
                act.wait_ge(tails, n + 1)
                for h in range(2):
                    act.wait_ge(hid, n * 2 + (h + 1))
                    for q in range(HC // 2):
                        hc = h * (HC // 2) + q
                        last = act.activation(hT[:, m % 2, hc, :], psH[:, m % 2, h, q * P:(q + 1) * P], ACT.Gelu, bias=b1_s[:, hc:hc + 1])
                    last.then_inc(gelus, 1)
            return f

        def ffn_zT(dve, turned, zT_set):
            def f(n, m, _):
                dve.wait_ge(turned, n + 1)
                dve.tensor_copy(zT[:, m % 2, :], psT[:, m % 2, 0:D]).then_inc(zT_set, 1)
            return f

        with ExitStack() as s3:
            wg_s = sb(s3, "wg_s", [P, HC, NE])
            bg_s = sb(s3, "bg_s", [1, NE])
            stats = sb(s3, "stats3", [P, TILES, 6])
            mean = sb(s3, "mean3", [P, TILES])
            var = sb(s3, "var3", [P, TILES])
            rstd = sb(s3, "rstd3", [P, TILES])
            shift = sb(s3, "shift3", [P, TILES])
            part = sb(s3, "part", [P, 1])
            before = sb(s3, "before", [P, P])
            falling = sb(s3, "falling", [P, NE])
            etile = sb(s3, "etile", [P, ETILES])
            logit = sb(s3, "logit", [P, TILES, NE])
            prob = sb(s3, "prob", [P, TILES, NE])
            mine = sb(s3, "mine", [P, TILES, NE])
            most = sb(s3, "most", [P, TILES])
            total = sb(s3, "total", [P, TILES])
            per_tile = sb(s3, "per_tile", [P, NE, TILES])
            upto = sb(s3, "upto", [P, NE, TILES])
            need = sb(s3, "need", [P, NE])
            need_i = sb(s3, "need_i", [P, NE], I32)
            start = sb(s3, "start", [P, NE])
            exf = sb(s3, "exf", [P, ETILES])
            pos = sb(s3, "pos", [P, TILES], U32)

            ln3, rstd3_seq, c3 = sem("ln3"), sem("rstd3_seq"), sem("c3")
            wg_in = sem("wg_in")
            z_set, turned, zT_set, hid, gelus, tails, outs = (sem(f"{a}_3") for a in ("z_set", "turned", "zT_set", "hid", "gelus", "tails", "outs"))
            route, exp_in, exp_out = sem("route"), sem("exp_in"), sem("exp_out")
            mine_set, ranked, pos_set, scattered = sem("mine_set"), sem("ranked"), sem("pos_set"), sem("scattered")

            block = s3.enter_context(nc.Block())

            @block.sync
            def _(sp):
                sp.dma_start(w1_s[:], w1.rearrange("(c f) h -> f c h", f=P)).then_inc(w1_in, 16)
                sp.dma_start(b1_s[:], b1.rearrange("(c h) -> h c", h=P), allow_slow_non_contiguous=True).then_inc(w1_in, 16)
                sp.dma_start(wg_s[:], wg.rearrange("(c h) e -> h c e", h=P)).then_inc(wg_in, 16)
                sp.dma_start(bg_s[:], bg.rearrange("(a e) -> a e", a=1)).then_inc(wg_in, 16)
                sp.dma_start(bd_s[:], bd.rearrange("(a e) o -> a e o", a=1)).then_inc(wd_in, 16)
                for e in range(NE):
                    sp.dma_start(wd_s[:, e, :, :], wd[e].rearrange("(c h) o -> h c o", h=P)).then_inc(wd_in, 16)

            @block.gpsimd
            def _(pool):
                pool.memset(eps[:], EPS)
                pool.memset(minus_half[:], -0.5).then_inc(c3, 1)
                pool.memset(bufA[:, :, D:ROW], 0.0).then_inc(c3, 1)
                pool.iota(part[:], [[0, 1]], base=0, channel_multiplier=1, allow_small_or_imprecise_dtypes=True).then_inc(c3, 1)
                pool.iota(falling[:], [[-1, NE]], base=NE, channel_multiplier=0, allow_small_or_imprecise_dtypes=True).then_inc(c3, 1)
                pool.iota(etile[:], [[1, ETILES]], base=0, channel_multiplier=0, allow_small_or_imprecise_dtypes=True).then_inc(c3, 1)
                pool.wait_ge(c3, 5)
                pool.iota(bufA[:].bitcast(I32)[:, :, D + 1], [[P, TILES]], base=0, channel_multiplier=1).then_inc(c3, 1)
                pool.wait_ge(ln3, TILES + MOMENTS)
                pool.tensor_scalar(rstd[:], var[:], EPS, None, ALU.add).then_inc(rstd3_seq, 1)
                pool.wait_ge(rstd3_seq, 1)
                pool.tensor_tensor(rstd[:], rstd[:], minus_half[:], ALU.pow).then_inc(rstd3_seq, 1)
                pool.wait_ge(rstd3_seq, 2)
                pool.tensor_tensor(shift[:], mean[:], rstd[:], ALU.mult).then_inc(rstd3_seq, 1)
                pool.wait_ge(rstd3_seq, 3)
                pool.tensor_scalar(shift[:], shift[:], -0.5, None, ALU.mult).then_inc(rstd3_seq, 1)
                pool.wait_ge(pos_set, 1)
                for t in range(TILES):
                    pool.indirect_dma_start(out=placed, out_offset=bass.IndirectOffsetOnAxis(ap=pos[:, t:t + 1], axis=0),
                                            in_=bufA[:, t, :], in_offset=None).then_inc(scattered, 16)
                pool.wait_ge(scattered, 16 * TILES)

            @block.scalar
            def _(act):
                act.wait_ge(rstd3_seq, 4)
                act.wait_ge(w1_in, 32)
                act.sem_inc(gelus, 4)

                def norm(n, m, _):
                    act.activation(z[:, m % 4, :], bufA[:, bass.ds(n, 1), 0:D].rearrange("p a f -> p (a f)"), ACT.Identity,
                                   bias=shift[:, bass.ds(n, 1)], scale=rstd[:, bass.ds(n, 1)]).then_inc(z_set, 1)
                in_turn(act, TILES, [(2, norm), (0, ffn_gelu(act, hid, gelus, tails))])
                act.wait_ge(exp_in, 1)
                act.activation(prob[:], logit[:], ACT.Exp).then_inc(exp_out, 1)

            @block.vector
            def _(dve):
                with dve.Fori(0, TILES) as t:
                    dve.bn_stats(stats[:, bass.ds(t, 1), :].rearrange("p a f -> p (a f)"),
                                 bufA[:, bass.ds(t, 1), 0:D].rearrange("p a f -> p (a f)")).then_inc(ln3, 1)
                dve.wait_ge(ln3, TILES)
                moments(dve, stats, mean, var, ln3, TILES)
                dve.wait_ge(c3, 6)
                dve.sem_inc(zT_set, 2)
                dve.sem_inc(outs, 2)

                def keep_logits(n, m, _):
                    dve.wait_ge(c3, 6)
                    dve.wait_ge(tails, n + 3)
                    dve.tensor_copy(logit[:, bass.ds(n, 1), :].rearrange("p a e -> p (a e)"), psO[:, m % 2, 0:NE]).then_inc(outs, 1)
                in_turn(dve, TILES, [(1, ffn_zT(dve, turned, zT_set)), (-1, keep_logits)])
                dve.wait_ge(outs, TILES + 2)

                count = [0]

                def step(ins):
                    count[0] += 1
                    ins.then_inc(route, 1)
                    dve.wait_ge(route, count[0])

                def over_experts(t):
                    return t[:].unsqueeze(2).to_broadcast([P, TILES, NE])
                step(dve.tensor_reduce(most[:], logit[:], AX, ALU.max))
                step(dve.tensor_tensor(logit[:], logit[:], over_experts(most), ALU.subtract))
                dve.sem_inc(exp_in, 1)
                step(dve.tensor_scalar(before[:], lanes[:], part[:, 0:1], None, ALU.is_gt))
                dve.wait_ge(exp_out, 1)
                step(dve.tensor_reduce(total[:], prob[:], AX, ALU.add))
                step(dve.reciprocal(total[:], total[:]))
                step(dve.tensor_tensor(prob[:], prob[:], over_experts(total), ALU.mult))
                step(dve.tensor_reduce(most[:], prob[:], AX, ALU.max))
                step(dve.tensor_copy(bufA[:, :, D], most[:]))
                step(dve.tensor_tensor(mine[:], prob[:], over_experts(most), ALU.is_equal))
                step(dve.tensor_tensor(mine[:], mine[:], falling[:].unsqueeze(1).to_broadcast([P, TILES, NE]), ALU.mult))
                step(dve.tensor_reduce(most[:], mine[:], AX, ALU.max))
                step(dve.tensor_tensor(mine[:], mine[:], over_experts(most), ALU.is_equal))
                dve.sem_inc(mine_set, 1)
                dve.wait_ge(ranked, 1)
                step(dve.tensor_copy(per_tile[:], psO[:, 1, 0:TILES * NE].rearrange("p (t e) -> p e t", e=NE)))
                for e in range(NE):
                    step(dve.tensor_tensor_scan(upto[:, e, :], ones[:, 0:TILES], per_tile[:, e, :], 0.0, ALU.mult, ALU.add))
                step(dve.tensor_scalar(need[:], upto[:, :, TILES - 1], float(P - 1), None, ALU.add))
                step(dve.tensor_copy(need_i[:], need[:]))
                step(dve.tensor_scalar(need_i[:], need_i[:], 7, None, ALU.logical_shift_right))
                step(dve.tensor_copy(need[:], need_i[:]))
                step(dve.tensor_tensor_scan(start[:], ones[:, 0:NE], need[:], 0.0, ALU.mult, ALU.add))
                step(dve.tensor_tensor(start[:], start[:], need[:], ALU.subtract))
                step(dve.tensor_tensor(upto[:], upto[:], per_tile[:], ALU.subtract))
                step(dve.scalar_tensor_tensor(upto[:], start[:].unsqueeze(2).to_broadcast([P, NE, TILES]), float(P), upto[:], ALU.mult, ALU.add))
                step(dve.tensor_tensor(prob[:], psO[:, 0, 0:TILES * NE].rearrange("p (t e) -> p t e", e=NE), upto[:].rearrange("p e t -> p t e"), ALU.add))
                step(dve.tensor_tensor(prob[:], prob[:], mine[:], ALU.mult))
                step(dve.tensor_reduce(most[:], prob[:], AX, ALU.add))
                step(dve.tensor_copy(pos[:], most[:]))
                dve.sem_inc(pos_set, 1)
                step(dve.tensor_scalar(exf[:], etile[:], start[:, 1:2], None, ALU.is_ge))
                for e in range(2, NE):
                    step(dve.scalar_tensor_tensor(exf[:], etile[:], start[:, e:e + 1], exf[:], ALU.is_ge, ALU.add))
                step(dve.tensor_copy(expert[:], exf[0:1, :]))

            @block.tensor
            def _(pe):
                pe.wait_ge(wg_in, 32)
                pe.wait_ge(w1_in, 32)
                pe.sem_inc(tails, 2)

                def gate(n, m, _):
                    pe.wait_ge(gelus, n * 2 + 6)
                    pe.wait_ge(outs, n + 1)
                    for c in range(HC):
                        pe.matmul(psO[:, m % 2, 0:NE], hT[:, m % 2, c, :], wg_s[:, c, :], start=(c == 0), stop=False)
                    pe.matmul(psO[:, m % 2, 0:NE], ones[0:1, :], bg_s[:], start=False, stop=True).then_inc(tails, 1)
                in_turn(pe, TILES, [(1, ffn_turn(pe, z_set, turned, zT_set)), (0, ffn_hidden(pe, zT_set, hid, gelus)), (-1, gate)])
                pe.wait_ge(mine_set, 1)
                flat = mine[:].rearrange("p t e -> p (t e)")
                pe.matmul(psO[:, 0, 0:TILES * NE], before[:], flat, start=True, stop=True)
                pe.matmul(psO[:, 1, 0:TILES * NE], ones[:], flat, start=True, stop=True).then_inc(ranked, 1)

        with ExitStack() as s4:
            rows = sb(s4, "rows", [P, UNROLL, ROW])
            result = sb(s4, "result", [P, UNROLL, D])
            stats = sb(s4, "stats4", [P, 4, 6])
            mv = sb(s4, "mv4", [P, 4, 2])
            rstd = sb(s4, "rstd4", [P, 4, 2])

            row_in = [sem(f"row_in{j}") for j in range(UNROLL)]
            row_out = [sem(f"row_out{j}") for j in range(UNROLL)]
            stat4, stat4_seen, mv_set, eps_set, rstd_set, scatters = sem("stat4"), sem("stat4_seen"), sem("mv_set"), sem("eps_set"), sem("rstd_set"), sem("scatters")
            z_set, turned, zT_set, hid, gelus, tails, outs = (sem(f"{a}_4") for a in ("z_set", "turned", "zT_set", "hid", "gelus", "tails", "outs"))

            block = s4.enter_context(nc.Block())

            @block.sync
            def _(sp):
                def load(i, j, first):
                    if not first:
                        sp.wait_ge(row_out[j], i * 16)
                    n = i * UNROLL + j
                    sp.dma_start(rows[:, j, :], placed[bass.ds(n * P, P), :]).then_inc(row_in[j], 16)
                for j in range(UNROLL):
                    load(0, j, True)
                with sp.Fori(1, ETILES // UNROLL) as i:
                    for j in range(UNROLL):
                        load(i, j, False)
                for j in range(UNROLL):
                    sp.wait_ge(row_out[j], 16 * (ETILES // UNROLL))

            @block.gpsimd
            def _(pool):
                def root(n, m, _):
                    pool.wait_ge(mv_set, n + 1)
                    pool.tensor_tensor(rstd[:, m % 4, 0:1], mv[:, m % 4, 1:2], eps[:], ALU.add).then_inc(eps_set, 1)
                    pool.wait_ge(eps_set, n + 1)
                    pool.tensor_tensor(rstd[:, m % 4, 1:2], rstd[:, m % 4, 0:1], minus_half[:, 0:1], ALU.pow).then_inc(rstd_set, 1)

                def scatter(n, m, _):
                    pool.wait_ge(outs, n + 3)
                    pool.sem_inc(scatters, 1)
                    pool.indirect_dma_start(out=out, out_offset=bass.IndirectOffsetOnAxis(ap=rows[:].bitcast(U32)[:, m, D + 1:D + 2], axis=0),
                                            in_=result[:, m, :], in_offset=None, bounds_check=NP - 1, oob_is_err=False).then_inc(row_out[m], 16)
                in_turn(pool, ETILES, [(3, root), (-1, scatter)])

            @block.scalar
            def _(act):
                act.sem_inc(gelus, 4)
                in_turn(act, ETILES, [(0, ffn_gelu(act, hid, gelus, tails))])

            @block.vector
            def _(dve):
                dve.sem_inc(zT_set, 2)
                dve.sem_inc(outs, 2)

                def statistics(n, m, turn):
                    dve.wait_ge(row_in[m], (turn + 1) * 16)
                    dve.bn_stats(stats[:, m % 4, :], rows[:, m, 0:D]).then_inc(stat4, 1)
                    dve.wait_ge(stat4, n + 1)
                    dve.sem_inc(stat4_seen, 1)
                    dve.bn_aggr(mv[:, m % 4, :], stats[:, m % 4, :]).then_inc(mv_set, 1)

                def norm(n, m, _):
                    dve.wait_ge(rstd_set, n + 1)
                    dve.tensor_scalar(z[:, m % 4, :], rows[:, m, 0:D], mv[:, m % 4, 0:1], rstd[:, m % 4, 1:2], ALU.subtract, ALU.mult).then_inc(z_set, 1)

                def finish(n, m, _):
                    dve.wait_ge(tails, n + 3)
                    dve.scalar_tensor_tensor(out=result[:, m, :], in0=psO[:, m % 2, 0:D], scalar=rows[:, m, D:D + 1], in1=rows[:, m, 0:D],
                                             op0=ALU.mult, op1=ALU.add).then_inc(outs, 1)
                in_turn(dve, ETILES, [(3, statistics), (2, norm), (1, ffn_zT(dve, turned, zT_set)), (-1, finish)])

            @block.tensor
            def _(pe):
                pe.wait_ge(wd_in, 16 * (NE + 1))
                pe.sem_inc(tails, 2)

                def product(n, m, _):
                    _, (e,) = nc.values_load_multi_w_load_instructions(
                        expert[0:1, bass.ds(n, 1)], engines=[PEE], min_val=0, max_val=NE - 1, skip_runtime_bounds_check_because=BOUNDED)
                    pe.wait_ge(gelus, n * 2 + 6)
                    pe.wait_ge(outs, n + 1)
                    for c in range(HC):
                        pe.matmul(psO[:, m % 2, 0:D], hT[:, m % 2, c, :], wd_s[:, bass.ds(e, 1), c, :].rearrange("p a o -> p (a o)"), start=(c == 0), stop=False)
                    pe.matmul(psO[:, m % 2, 0:D], ones[0:1, :], bd_s[:, bass.ds(e, 1), :].rearrange("p a o -> p (a o)"), start=False, stop=True).then_inc(tails, 1)
                in_turn(pe, ETILES, [(1, ffn_turn(pe, z_set, turned, zT_set)), (0, ffn_hidden(pe, zT_set, hid, gelus)), (-1, product)])
        ffn.close()


_INS = ["x", "src", "dst", "L0_gnn_weight", "L0_gnn_bias", "L0_ffn_W1", "L0_ffn_b1", "L0_ffn_Wg", "L0_ffn_bg", "L0_ffn_Wd", "L0_ffn_bd"]


def kernel(**inputs):
    import numpy as np
    import concourse.bacc as bacc
    from concourse.bass_utils import run_bass_kernel_spmd

    nodes, features = inputs["x"].shape
    padded = -(-nodes // P) * P
    nc = bacc.Bacc("TRN2", target_bir_lowering=False, num_devices=1)
    arrays, args = {}, []
    for name in _INS:
        a = np.ascontiguousarray(inputs[name])
        if name == "x":
            a = np.pad(a, ((0, padded - nodes), (0, 0)))
        arrays[f"in_{name}"] = a
        args.append(nc.dram_tensor(f"in_{name}", a.shape, mybir.dt.from_np(a.dtype), kind="ExternalInput").ap())
    out = nc.dram_tensor("out", (padded, features), F32, kind="ExternalOutput").ap()
    gnn_ffn_kernel(nc, *args, out)
    r = run_bass_kernel_spmd(nc, [arrays], core_ids=[0])
    return r.results[0]["out"][:nodes]
```

```python
from contextlib import ExitStack

import concourse.bass as bass
from concourse import mybir

F32 = mybir.dt.float32
BF16 = mybir.dt.bfloat16
I32 = mybir.dt.int32
U32 = mybir.dt.uint32
ALU = mybir.AluOpType
ACT = mybir.ActivationFunctionType
AX = mybir.AxisListType.X
DVE = mybir.EngineType.DVE
PEE = mybir.EngineType.PE

P = 128
MOMENTS = 5
UNROLL = 8
BOUNDED = "bounded by how the numbers are built"


def moments(dve, stats, mean, var, done, count):
    half = 128.0
    even, odd = stats[:, :, 1], stats[:, :, 4]
    dve.tensor_tensor(mean[:], even, odd, ALU.subtract).then_inc(done, 1)
    dve.wait_ge(done, count + 1)
    dve.scalar_tensor_tensor(var[:], mean[:], 0.25, mean[:], ALU.mult, ALU.mult).then_inc(done, 1)
    dve.wait_ge(done, count + 2)
    for q in (2, 5):
        dve.scalar_tensor_tensor(var[:], stats[:, :, q], 0.5 / half, var[:], ALU.mult, ALU.add).then_inc(done, 1)
        dve.wait_ge(done, count + (3 if q == 2 else 4))
    dve.tensor_tensor(mean[:], even, odd, ALU.add).then_inc(done, 1)
    dve.wait_ge(done, count + 5)


def in_turn(engine, total, steps):
    first, last = -min(lead for lead, _ in steps), total - max(lead for lead, _ in steps)
    rounds = (last - first) // UNROLL

    def one(n):
        for lead, f in steps:
            if 0 <= n + lead < total:
                f(n + lead, (n + lead) % UNROLL, (n + lead) // UNROLL)
    for n in range(-max(lead for lead, _ in steps), first):
        one(n)
    with engine.Fori(0, rounds) as i:
        for j in range(UNROLL):
            for lead, f in steps:
                m = first + j + lead
                f(i * UNROLL + m, m % UNROLL, i + m // UNROLL)
    for n in range(first + rounds * UNROLL, total - min(lead for lead, _ in steps)):
        one(n)


def gnn_ffn_kernel(nc, x, src, dst, gw, gb, w1, b1, wg, bg, wd, bd, out):
    NP, D = x.shape
    TILES = NP // P
    E = src.shape[0]
    KC = D // P
    CHUNKS = -(-E // P)
    SB = 8
    SN = SB * P
    J = 16
    ROUNDS = -(-(CHUNKS + TILES - 1) // J)
    ITEMS = ROUNDS * J
    HALF = ITEMS // 2
    WB = -(-ITEMS // P)
    AHEAD = 4
    COLBITS = 13
    COLMASK = (1 << COLBITS) - 1
    NORMAL = 1 << 29
    EPS = 1e-5
    HID = w1.shape[1]
    HC = HID // P
    NE = wd.shape[0]
    ETILES = TILES + NE - 1
    ROW = 260
    EARLY = 4
    MEET = 3
    ESRC, EW = 125, 800
    G = 7
    LAG = 4
    READ = 12
    assert J == 16 and READ < J
    assert ESRC * EW == E and EW <= SN and SN * P >= E and NP <= COLMASK + 1
    assert CHUNKS <= SB * P and TILES == G * G and ETILES % G == 0 and D == 2 * P

    xnT_d = nc.dram_tensor("xnT", [TILES, P, D], F32, kind="Internal").ap()
    table = [nc.dram_tensor(f"table{k}", [NP, D], F32, kind="Internal").ap() for k in range(3)]
    placed = nc.dram_tensor("placed", [ETILES * P, ROW], F32, kind="Internal").ap()

    outer = ExitStack()
    with outer:
        def sb(ctx, name, shape, dt=F32):
            return ctx.enter_context(nc.sbuf_tensor(name, shape, dt))

        def pb(ctx, name, shape, dt=F32):
            return ctx.enter_context(nc.psum_tensor(name, shape, dt))

        def sem(name):
            return outer.enter_context(nc.semaphore(name))

        ident = sb(outer, "ident", [P, P])
        lanes = sb(outer, "lanes", [P, P])
        ones = sb(outer, "ones", [P, P])
        bufA = sb(outer, "bufA", [P, TILES, ROW])

        bufB = sb(outer, "bufB", [P, TILES, D])
        redo = sb(outer, "redo", [1, 1], I32)

        taken = [0]

        def take(*shape):
            size = 1
            for n in shape:
                size *= n
            flat = bufB[:].rearrange("p t f -> p (t f)")[:, taken[0]:taken[0] + size]
            taken[0] += size
            assert taken[0] <= TILES * D
            names = "abc"[:len(shape)]
            return flat.rearrange(f"p ({' '.join(names)}) -> p {' '.join(names)}", **dict(zip(names, shape)))
        w1_s = take(KC, HID)
        b1_s = take(1, HC)
        wg_s = take(HC, NE)
        bg_s = take(1, NE)
        z = take(4, D)
        zT = take(2, D)
        hT = take(2, HC, P)
        logit = take(TILES, NE)
        minus_half = take(1, 1)
        eps = take(1, 1)

        graph = ExitStack()
        rel = sb(graph, "rel", [P, ITEMS + AHEAD])
        col = sb(graph, "col", [P, ITEMS], U32)
        tile_of = sb(graph, "tile_of", [1, ITEMS], I32)
        wk = sb(graph, "wk", [P, 4, KC, D])
        gbrow = sb(graph, "gbrow", [1, D])
        dis = sb(graph, "dis", [P, TILES])
        sc1 = sb(graph, "sc1", [P, TILES])
        sc2 = sb(graph, "sc2", [P, TILES])
        nd1 = sb(graph, "nd1", [P, TILES])
        nd2 = sb(graph, "nd2", [P, TILES])

        with ExitStack() as s1:
            edges = sb(s1, "edges", [P, 2, SN], I32)
            keys = [sb(s1, f"keys{i}", [P, SN]) for i in range(2)]
            sign0 = sb(s1, "sign0", [P, 1])
            lane_i = sb(s1, "lane_i", [P, P], I32)
            gray = sb(s1, "gray", [P, P], I32)
            bits = sb(s1, "bits", [P, P], I32)
            bitsf = sb(s1, "bitsf", [P, P])
            turn = sb(s1, "turn", [P, 7, P])
            part_i = sb(s1, "part_i", [P, 1], I32)
            chunk = sb(s1, "chunk", [P, SB])
            latest = sb(s1, "latest", [P, 1])
            chunk1 = sb(s1, "chunk1", [P, SB, P])
            iw = sb(s1, "iw", [P, ITEMS])
            tmp = sb(s1, "tmp", [P, ITEMS])
            lohi_i = sb(s1, "lohi_i", [P, 2, SB], I32)
            lohi = sb(s1, "lohi", [P, 2, SB])
            pick = sb(s1, "pick", [P, SB * ITEMS])
            twf = sb(s1, "twf", [P, WB * P])
            relb = sb(s1, "relb", [P, ITEMS], BF16)
            lanesb = sb(s1, "lanesb", [P, P], BF16)
            pairs = sb(s1, "pairs", [P, ITEMS, 2], BF16)
            tile_hot = sb(s1, "tile_hot", [P, WB, TILES])
            deg = sb(s1, "deg", [P, TILES])
            stats = sb(s1, "stats", [P, TILES, 6])
            mean = sb(s1, "mean", [P, TILES])
            var = sb(s1, "var", [P, TILES])
            rstd = sb(s1, "rstd", [P, TILES])
            shift = sb(s1, "shift", [P, TILES])
            xn = sb(s1, "xn", [P, 3, D])
            half_neg = sb(s1, "half_neg", [P, TILES])
            xT = sb(s1, "xT", [P, G, D])
            psN = pb(s1, "psN", [P, 2, 512])
            psW = pb(s1, "psW", [P, 2, 2 * D])
            psS = pb(s1, "psS", [P, 2, 512])
            psI = pb(s1, "psI", [P, 2, 512])
            psM = psN[:, 0, :]

            edges_in, wk_in = sem("edges_in"), sem("wk_in")
            x_in = [sem(f"x_in{g}") for g in range(G)]
            consts = sem("consts")
            edges_set = sem("edges_set")
            rstd_done, normed = sem("rstd_done"), sem("normed")
            ln_seq, pool_seq = sem("ln_seq"), sem("pool_seq")
            turned, xT_set, mm_done, mm_out = sem("turned"), sem("xT_set"), sem("mm_done"), sem("mm_out")
            xT_out = [sem(f"xT_out{j}") for j in range(G)]
            seq = sem("seq")
            sort_T = sem("sort_T")
            quant_ready, item_sum, item_out = sem("quant_ready"), sem("item_sum"), sem("item_out")
            tw_ready, twT_done = sem("tw_ready"), sem("twT_done")
            level_sorted = sem("level_sorted")
            hot_ready, hist_mm, hist_out = sem("hot_ready"), sem("hist_mm"), sem("hist_out")
            cnt_turned, cnt_set, deg_done = sem("cnt_turned"), sem("cnt_set"), sem("deg_done")
            deg_set, dis_done = sem("deg_set"), sem("dis_done")

            at, source = (1 + 55) % 2, {}
            for k in range(1, 8):
                for way in range(2):
                    source[k, way] = at
                    at = (at + 1 + (k if way == 0 else 10)) % 2
            srt = keys[at][:].bitcast(I32)
            rowf, colf = keys[1 - at], keys[at]
            selff = edges[:, 0, :].bitcast(F32)
            picks = pick[:].rearrange("p (b w) -> p b w", b=SB)
            counts = pick[:, 0:WB * P * 2].rearrange("p (w s) -> p w s", s=2)
            countsT = pick[:, WB * P * 2:WB * P * 4].rearrange("p (m r) -> p m r", r=P)
            hot = pick[:, WB * P * 4:WB * P * 4 + J * P].bitcast(BF16).rearrange("p (h j r) -> p h j r", h=2, j=J)

            block = s1.enter_context(nc.Block())

            @block.sync
            def _(sp):
                sp.wait_ge(edges_set, 1)
                sp.dma_start(edges[0:ESRC, 0, 0:EW], src.rearrange("(p f) -> p f", f=EW)).then_inc(edges_in, 16)
                sp.dma_start(edges[0:ESRC, 1, 0:EW], dst.rearrange("(p f) -> p f", f=EW)).then_inc(edges_in, 16)
                for g in range(G):
                    sp.dma_start(bufA[:, g * G:(g + 1) * G, 0:D],
                                 x[g * G * P:(g + 1) * G * P, :].rearrange("(t p) f -> p t f", p=P)).then_inc(x_in[g], 16)
                for k in range(4):
                    sp.dma_start(wk[:, k, :, :], gw[k].rearrange("(c f) o -> f c o", f=P)).then_inc(wk_in, 16)
                sp.dma_start(gbrow[:], gb.rearrange("(a o) -> a o", a=1)).then_inc(wk_in, 16)
                def store(i):
                    for j in range(G):
                        sp.wait_ge(xT_set, i * G + (j + 1))
                        sp.dma_start(xnT_d[bass.ds(i * G + j, 1)].rearrange("a p f -> p (a f)"), xT[:, j, :]).then_inc(xT_out[j], 16)
                store(0)
                with sp.Fori(1, G) as i:
                    store(i)
                for j in range(G):
                    sp.wait_ge(xT_out[j], 16 * G)

            @block.gpsimd
            def _(pool):
                pool.memset(edges[:, 0, :], NP - 1).then_inc(pool_seq, 1)
                pool.memset(edges[:, 1, :], 0).then_inc(pool_seq, 1)
                pool.wait_ge(pool_seq, 2)
                pool.sem_inc(edges_set, 1)
                pool.iota(lane_i[:], [[1, P]], base=0, channel_multiplier=0).then_inc(consts, 1)
                pool.iota(part_i[:], [[0, 1]], base=0, channel_multiplier=1).then_inc(consts, 1)
                pool.iota(lanes[:], [[1, P]], base=0, channel_multiplier=0, allow_small_or_imprecise_dtypes=True).then_inc(consts, 1)
                pool.iota(iw[:], [[1, ITEMS]], base=0, channel_multiplier=0, allow_small_or_imprecise_dtypes=True).then_inc(consts, 1)
                pool.iota(chunk[:], [[1, SB]], base=0, channel_multiplier=SB, allow_small_or_imprecise_dtypes=True).then_inc(consts, 1)
                pool.iota(chunk1[:], [[1, SB], [0, P]], base=1, channel_multiplier=SB, allow_small_or_imprecise_dtypes=True).then_inc(consts, 1)
                pool.memset(ident[:], 0.0).then_inc(pool_seq, 1)
                pool.memset(ones[:], 1.0).then_inc(consts, 1)
                pool.memset(half_neg[:], -0.5).then_inc(pool_seq, 1)
                pool.wait_ge(pool_seq, 4)
                pool.affine_select(out=ident[:], in_=ident[:], compare_op=ALU.not_equal, fill=1.0, base=0,
                                   pattern=[[-1, P]], channel_multiplier=1).then_inc(consts, 1)
                pool.wait_ge(ln_seq, TILES + MOMENTS)
                pool.tensor_scalar(rstd[:], var[:], EPS, None, ALU.add).then_inc(pool_seq, 1)
                pool.wait_ge(pool_seq, 5)
                pool.tensor_tensor(rstd[:], rstd[:], half_neg[:], ALU.pow).then_inc(pool_seq, 1)
                pool.wait_ge(pool_seq, 6)
                pool.tensor_tensor(shift[:], mean[:], rstd[:], ALU.mult).then_inc(pool_seq, 1)
                pool.wait_ge(pool_seq, 7)
                pool.tensor_scalar(shift[:], shift[:], -0.5, None, ALU.mult).then_inc(rstd_done, 1)
                pool.wait_ge(deg_set, 1)
                pool.tensor_tensor(dis[:], deg[:], half_neg[:], ALU.pow).then_inc(dis_done, 1)

            @block.scalar
            def _(act):
                def norm(i, j):
                    act.activation(xn[:, j % 3, :], bufA[:, bass.ds(i * G + j, 1), 0:D].rearrange("p a f -> p (a f)"), ACT.Identity,
                                   bias=shift[:, bass.ds(i * G + j, 1)], scale=rstd[:, bass.ds(i * G + j, 1)]).then_inc(normed, 1)

                def xT_evac(i, j, first):
                    act.wait_ge(turned, i * G + (j + 1))
                    if not first:
                        act.wait_ge(xT_out[j], i * 16)
                    act.copy(xT[:, j, :], psN[:, j % 2, 0:D]).then_inc(xT_set, 1)

                def mm_evac(i, j):
                    act.wait_ge(rstd_done, 1)
                    act.wait_ge(mm_done, i * G + (j + 1))
                    act.copy(bufA[:, bass.ds(i * G + j, 1), 0:D].rearrange("p a f -> p (a f)"), psW[:, j % 2, 0:D])
                    act.copy(bufB[:, bass.ds(i * G + j, 1), :].rearrange("p a f -> p (a f)"), psW[:, j % 2, D:2 * D]).then_inc(mm_out, 1)

                def group(i, first):
                    norm(i, 0)
                    norm(i, 1)
                    xT_evac(i, 0, first)
                    for j in range(G):
                        if j + 2 < G:
                            norm(i, j + 2)
                        if j + 1 < G:
                            xT_evac(i, j + 1, first)
                        mm_evac(i, j)
                act.wait_ge(rstd_done, 1)
                group(0, True)
                with act.Fori(1, G) as i:
                    group(i, False)

                with act.Fori(0, ROUNDS // 2) as i:
                    for h in range(2):
                        act.wait_ge(rstd_done, 1)
                        act.wait_ge(hist_mm, i * 2 + (h + 1))
                        act.copy(counts[:, bass.ds(i * (2 * J) + h * J, J), :], psW[:, h, 0:2 * J].rearrange("p (j s) -> p j s", s=2)).then_inc(hist_out, 1)

            @block.tensor
            def _(pe):
                pe.wait_ge(consts, 8)

                def turn_tile(i, j, first):
                    pe.wait_ge(normed, i * G + (j + 1))
                    if not (first and j == 0) and j != 1:
                        pe.wait_ge(xT_set, i * G + max(j - 1, 0))
                    for c in range(KC):
                        last = pe.transpose(psN[:, j % 2, c * P:(c + 1) * P],
                                            xn[:, j % 3, c * P:(c + 1) * P], ident[:])
                    last.then_inc(turned, 1)

                def mm_tile(i, j, first):
                    pe.wait_ge(xT_set, i * G + (j + 1))
                    if not (first and j == 0) and j != 1:
                        pe.wait_ge(mm_out, i * G + max(j - 1, 0))
                    for q, k in enumerate((3, 2)):
                        for c in range(KC):
                            last = pe.matmul(psW[:, j % 2, q * D:(q + 1) * D], xT[:, j, c * P:(c + 1) * P], wk[:, k, c, :],
                                             start=(c == 0), stop=(c == KC - 1))
                    last.then_inc(mm_done, 1)

                def group(i, first):
                    turn_tile(i, 0, first)
                    for j in range(G):
                        if j + 1 < G:
                            turn_tile(i, j + 1, first)
                        mm_tile(i, j, first)

                def sort_level(k):
                    for way in range(2):
                        pe.wait_ge(level_sorted, 2 * (k - 1) + way + 1)
                        for b in range(SB):
                            last = pe.transpose(psS[:, b // 4, (b % 4) * P:(b % 4 + 1) * P],
                                                keys[source[k, way]][:, b * P:(b + 1) * P], ident[:])
                            if b % 4 == 3:
                                last.then_inc(sort_T, 1)

                pe.wait_ge(wk_in, 16 * 5)
                group(0, True)
                with pe.Fori(1, MEET) as i:
                    group(i, False)
                for k in range(1, 8):
                    sort_level(k)
                    if MEET + k - 1 < G:
                        group(MEET + k - 1, False)

                pe.wait_ge(quant_ready, 1)
                for q, quant in enumerate((rowf, colf, selff, None)):
                    ps = (psS, psI)[q % 2]
                    if q >= 2:
                        pe.wait_ge(item_out, q - 1)
                    for h in range(2):
                        for b in range(SB):
                            lhs = chunk1[:, b, :] if quant is None else quant[:, b * P:(b + 1) * P]
                            last = pe.matmul(ps[:, h, 0:HALF], lhs, picks[:, b, h * HALF:(h + 1) * HALF],
                                             start=(b == 0), stop=(b == SB - 1))
                    last.then_inc(item_sum, 1)
                pe.wait_ge(tw_ready, 1)
                for q in range(WB):
                    last = pe.matmul(psM[:, q:q + 1], twf[:, q * P:(q + 1) * P], ident[:, 0:1], start=True, stop=True)
                last.then_inc(twT_done, 1)

                def count_round(i, h, first):
                    pe.wait_ge(hot_ready, i * 2 + (h + 1))
                    if first:
                        pe.wait_ge(mm_out, TILES)
                    else:
                        pe.wait_ge(hist_out, i * 2 + (h - 1))
                    for j in range(J):
                        last = pe.matmul(psW[:, h, 2 * j:2 * j + 2], hot[:, h, j, :],
                                         pairs[:, bass.ds(i * (2 * J) + (h * J + j), 1), :].rearrange("p a s -> p (a s)"), start=True, stop=True)
                    last.then_inc(hist_mm, 1)
                for h in range(2):
                    count_round(0, h, True)
                with pe.Fori(1, ROUNDS // 2) as i:
                    for h in range(2):
                        count_round(i, h, False)
                pe.wait_ge(hist_out, ROUNDS)
                pe.wait_ge(item_out, 4)
                for m in range(2 * WB):
                    ps = psS if m < 8 else psI
                    last = pe.transpose(ps[:, m % 8 // 4, m % 4 * P:(m % 4 + 1) * P], counts[:, m // 2 * P:(m // 2 + 1) * P, m % 2], ident[:])
                last.then_inc(cnt_turned, 1)
                pe.wait_ge(cnt_set, 1)
                for s in range(2):
                    for q in range(WB):
                        last = pe.matmul(psM[:, s * P:s * P + TILES], countsT[:, 2 * q + s, :], tile_hot[:, q, :],
                                         start=(q == 0), stop=(q == WB - 1))
                last.then_inc(deg_done, 1)

            @block.vector
            def _(dve):
                count = [0]

                def step(ins):
                    count[0] += 1
                    ins.then_inc(seq, 1)

                def settle():
                    dve.wait_ge(seq, count[0])

                dve.wait_ge(edges_in, 32)
                dve.wait_ge(consts, 8)
                e_row, e_col = edges[:, 0, :], edges[:, 1, :]
                step(dve.tensor_scalar(e_row, e_row, COLBITS, NORMAL, ALU.logical_shift_left, ALU.bitwise_or))
                step(dve.tensor_scalar(part_i[:], part_i[:], 1, None, ALU.bitwise_and))
                settle()
                step(dve.tensor_tensor(keys[0][:].bitcast(I32), e_row, e_col, ALU.bitwise_or))
                step(dve.tensor_copy(sign0[:], part_i[:]))
                step(dve.tensor_scalar(bits[:], lane_i[:], 1, None, ALU.logical_shift_right))
                settle()
                step(dve.tensor_scalar(sign0[:], sign0[:], -2.0, 1.0, ALU.mult, ALU.add))
                step(dve.tensor_tensor(gray[:], lane_i[:], bits[:], ALU.bitwise_xor))
                settle()
                for k in range(7):
                    step(dve.tensor_scalar(bits[:], gray[:], k, 1, ALU.logical_shift_right, ALU.bitwise_and))
                    settle()
                    step(dve.tensor_copy(bitsf[:], bits[:]))
                    settle()
                    step(dve.tensor_scalar(turn[:, k, :], bitsf[:], -2.0, 1.0, ALU.mult, ALU.add))
                    settle()
                step(dve.tensor_scalar(keys[1][:], keys[0][:], sign0[:, 0:1], None, ALU.mult))

                buf = 1

                def compare(dist, flip):
                    nonlocal buf
                    a = keys[buf][:].rearrange("p (n two d) -> p n two d", two=2, d=dist)
                    o = keys[1 - buf][:].rearrange("p (n two d) -> p n two d", two=2, d=dist)
                    hi = a[:, :, 1, ::-1] if flip else a[:, :, 1, :]
                    settle()
                    step(dve.tensor_tensor(o[:, :, 0, :], a[:, :, 0, :], hi, ALU.min))
                    step(dve.tensor_tensor(o[:, :, 1, :], a[:, :, 0, :], hi, ALU.max))
                    buf = 1 - buf

                def level(k):
                    compare(1 << k, flip=k > 0)
                    for d in reversed(range(k)):
                        compare(1 << d, flip=False)
                for k in range(EARLY):
                    level(k)
                for g in range(G):
                    dve.wait_ge(x_in[g], 16)
                with dve.Fori(0, TILES) as t:
                    dve.bn_stats(stats[:, bass.ds(t, 1), :].rearrange("p a f -> p (a f)"),
                                 bufA[:, bass.ds(t, 1), 0:D].rearrange("p a f -> p (a f)")).then_inc(ln_seq, 1)
                dve.wait_ge(ln_seq, TILES)
                moments(dve, stats, mean, var, ln_seq, TILES)
                for k in range(EARLY, 10):
                    level(k)
                moves = 0
                for k in range(1, 8):
                    for way in range(2):
                        settle()
                        dve.sem_inc(level_sorted, 1)
                        assert source[k, way] == buf
                        for h in range(2):
                            moves += 1
                            dve.wait_ge(sort_T, moves)
                            o = keys[1 - buf][:, h * 512:(h + 1) * 512]
                            if way == 0:
                                step(dve.tensor_tensor(o.rearrange("p (b l) -> p b l", l=P), psS[:, h, :].rearrange("p (b l) -> p b l", l=P),
                                                       turn[:, k - 1:k, :].to_broadcast([P, 4, P]), ALU.mult))
                            else:
                                step(dve.tensor_copy(o, psS[:, h, :]))
                        buf = 1 - buf
                        for d in reversed(range(k if way == 0 else 10)):
                            compare(1 << d, flip=False)
                settle()
                step(dve.tensor_scalar(edges[:, 0, :], srt, COLBITS, COLMASK, ALU.logical_shift_right, ALU.bitwise_and))
                step(dve.tensor_scalar(edges[:, 1, :], srt, COLMASK, None, ALU.bitwise_and))
                settle()
                blocks = edges[:, 0, :].rearrange("p (b l) -> p b l", l=P)
                step(dve.tensor_scalar(lohi_i[:, 0, :], blocks[:, :, 0], 7, None, ALU.logical_shift_right))
                step(dve.tensor_scalar(lohi_i[:, 1, :], blocks[:, :, P - 1], 7, None, ALU.logical_shift_right))
                step(dve.tensor_copy(rowf[:], edges[:, 0, :]))
                step(dve.tensor_copy(colf[:], edges[:, 1, :]))
                settle()
                step(dve.tensor_copy(lohi[:], lohi_i[:]))
                step(dve.tensor_tensor(selff, rowf[:], colf[:], ALU.is_equal))
                settle()
                for s in range(2):
                    step(dve.tensor_tensor(lohi[:, s, :], lohi[:, s, :], chunk[:], ALU.add))
                settle()
                step(dve.scalar_tensor_tensor(rowf[:], chunk1[:].rearrange("p b l -> p (b l)"), float(P), rowf[:], ALU.mult, ALU.add))
                for b in range(SB):
                    step(dve.tensor_scalar(tmp[:], iw[:], lohi[:, 0, b:b + 1], None, ALU.is_ge))
                    settle()
                    step(dve.scalar_tensor_tensor(picks[:, b, :], iw[:], lohi[:, 1, b:b + 1], tmp[:], ALU.is_le, ALU.mult))
                    settle()
                step(dve.memset(rel[:, ITEMS:ITEMS + AHEAD], -1.0))
                step(dve.memset(twf[:, ITEMS:WB * P], -1.0))
                step(dve.memset(pairs[:], 1.0))
                step(dve.tensor_copy(lanesb[:], lanes[:]))
                step(dve.tensor_scalar(tmp[:], iw[:], float(P), float(P), ALU.mult, ALU.add))
                settle()
                dve.sem_inc(quant_ready, 1)

                def halves(t):
                    return t[:, 0:ITEMS].rearrange("p (h w) -> p h w", h=2)
                dve.wait_ge(item_sum, 1)
                dve.tensor_tensor(halves(rel), psS[:, :, 0:HALF], halves(tmp), ALU.subtract).then_inc(item_out, 1)
                dve.wait_ge(item_sum, 2)
                dve.tensor_copy(halves(col), psI[:, :, 0:HALF]).then_inc(item_out, 1)
                dve.wait_ge(item_out, 2)
                step(dve.tensor_copy(relb[:], rel[:, 0:ITEMS]))
                dve.wait_ge(item_sum, 3)
                dve.tensor_copy(pairs[:, :, 1].rearrange("p (h w) -> p h w", h=2), psS[:, :, 0:HALF]).then_inc(item_out, 1)
                dve.wait_ge(item_sum, 4)
                dve.scalar_tensor_tensor(halves(tmp), halves(iw), 1.0, psI[:, :, 0:HALF], ALU.add, ALU.subtract).then_inc(item_out, 1)
                dve.wait_ge(item_out, 4)
                step(dve.tensor_scalar(twf[:, 0:ITEMS], tmp[:], float(TILES - 1), None, ALU.min))
                step(dve.memset(counts[:, ITEMS:WB * P, :], 0.0))
                settle()
                step(dve.tensor_copy(tile_of[:], twf[0:1, 0:ITEMS]))
                dve.sem_inc(tw_ready, 1)

                def hot_round(i, h, first):
                    if not first:
                        dve.wait_ge(hist_mm, i * 2 + (h - 1))
                    dve.tensor_tensor(hot[:, h, :, :], lanesb[:].unsqueeze(1).to_broadcast([P, J, P]),
                                      relb[:, bass.ds(i * (2 * J) + h * J, J)].unsqueeze(2).to_broadcast([P, J, P]),
                                      ALU.is_equal).then_inc(hot_ready, 1)
                for h in range(2):
                    hot_round(0, h, True)
                with dve.Fori(1, ROUNDS // 2) as i:
                    for h in range(2):
                        hot_round(i, h, False)
                dve.wait_ge(twT_done, 1)
                for q in range(WB):
                    step(dve.tensor_scalar(tile_hot[:, q, :], lanes[:, 0:TILES], psM[:, q:q + 1], None, ALU.is_equal))
                dve.wait_ge(cnt_turned, 1)
                step(dve.tensor_copy(countsT[:, 0:8, :], psS[:].rearrange("p h (m r) -> p (h m) r", r=P)))
                step(dve.tensor_copy(countsT[:, 8:2 * WB, :], psI[:].rearrange("p h (m r) -> p (h m) r", r=P)[:, 0:2 * WB - 8, :]))
                settle()
                dve.sem_inc(cnt_set, 1)
                dve.wait_ge(deg_done, 1)
                dve.tensor_scalar(deg[:], psM[:, 0:TILES], 1.0, None, ALU.add).then_inc(deg_set, 1)
                step(dve.scalar_tensor_tensor(tmp[:], twf[:, 0:ITEMS], -float(J), iw[:], ALU.mult, ALU.add))
                settle()
                step(dve.tensor_reduce(latest[:], tmp[:], AX, ALU.max))
                settle()
                step(dve.tensor_scalar(redo[:], latest[0:1, :], float(LAG * J + READ), None, ALU.is_ge))
                dve.wait_ge(dis_done, 1)
                step(dve.tensor_tensor(sc2[:], dis[:], dis[:], ALU.mult))
                settle()
                step(dve.scalar_tensor_tensor(sc1[:], psM[:, P:P + TILES], 1.0, sc2[:], ALU.add, ALU.subtract))
                settle()
                step(dve.tensor_scalar(sc2[:], sc1[:], 2.0, None, ALU.mult))
                step(dve.tensor_scalar(nd1[:], dis[:], -1.0, None, ALU.mult))
                step(dve.tensor_scalar(nd2[:], dis[:], -2.0, None, ALU.mult))
                settle()
        redo_pass = nc.values_load_multi_w_load_instructions(
            redo[0:1, 0:1], engines=[DVE, PEE, mybir.EngineType.Activation, mybir.EngineType.Pool, mybir.EngineType.SP],
            min_val=0, max_val=1, skip_runtime_bounds_check_because=BOUNDED)[1][0]
        with ExitStack() as s2:
            bufC = sb(s2, "bufC", [P, TILES, D])
            gath = sb(s2, "gath", [P, J, D])
            idx = sb(s2, "idx", [P, J], U32)
            hot = sb(s2, "hot_r", [P, AHEAD, P])
            xnT = sb(s2, "xnT_s", [P, D])
            xr = sb(s2, "xr", [P, D])
            empty = sb(s2, "empty", [P, ROW])
            stat2 = sb(s2, "stat2", [P, 6])
            mv2 = sb(s2, "mv2", [P, 2])
            rstd2 = sb(s2, "rstd2", [P, 2])
            psP = pb(s2, "psP", [P, AHEAD, 512])
            psX = pb(s2, "psX", [P, 512])
            psH2 = pb(s2, "psH2", [P, 2, 512])
            psO2 = pb(s2, "psO2", [P, 512])

            PASSES = ((2, bufB, bufA, bufC, bufC, sc2, nd2),
                      (1, bufC, bufB, bufA, bufA, sc2, nd2),
                      (0, bufA, bufC, None, bufB, sc1, nd1))
            u_set = sem("u_set")
            u_first = [sem(f"u_first{g}") for g in range(G)]
            u_out = [sem(f"u_out{g}") for g in range(G)]
            next_out = sem("next_out")
            landed = [sem(f"landed{j}") for j in range(J)]
            gathering = sem("gathering")
            idx_set, hot_set, item_mm, item_added = sem("idx_set"), sem("hot_set"), sem("item_mm"), sem("item_added")
            xnT_load, xr_load = sem("xnT_load"), sem("xr_load")
            next_mm, next_diff, next_set = sem("next_mm"), sem("next_diff"), sem("next_set")
            folded = sem("folded")
            branched = sem("branched")
            empty_set, empty_out = sem("empty_set"), sem("empty_out")
            ffn_in, norm_consts = sem("ffn_in"), sem("norm_consts")
            stat_set, stat_seen, mv_set, eps_set, rstd_set = (sem(f"{a}_2") for a in ("stat_set", "stat_seen", "mv_set", "eps_set", "rstd_set"))
            z_set, turned, zT_set, hid, gelus, tails, outs = (sem(f"{a}_2") for a in ("z_set", "turned", "zT_set", "hid", "gelus", "tails", "outs"))

            def tile(buf, t):
                return buf[:, bass.ds(t, 1), 0:D].rearrange("p a f -> p (a f)")

            def over_rounds(engine, lags, body):
                marks = sorted({0, 1, ROUNDS - 1, ROUNDS} | {lag for lag in lags} | {TILES + lag for lag in lags})
                for a, b in zip(marks, marks[1:]):
                    has = {lag: lag <= a < TILES + lag for lag in lags}
                    has["items"], has["next"] = a < ROUNDS, a < ROUNDS - 1
                    if b - a < 3:
                        for i in range(a, b):
                            body(i, has, i == 0)
                    else:
                        with engine.Fori(a, b) as i:
                            body(i, has, False)
            TABLE = LAG + 1
            WHOLE, NORM, HIDDEN, GATE = LAG, LAG + 1, LAG + 2, LAG + 3

            for n, (k, acc, prev, nxt, staging, factor, minus) in enumerate(PASSES):
                last_pass = nxt is None
                lags = (0, WHOLE, NORM, HIDDEN, GATE) if last_pass else (0, TABLE)
                next_table = None if last_pass else PASSES[n + 1][4]
                with nc.Block() as block:

                    @block.sync
                    def _(sp):
                        if n == 0:
                            sp.wait_ge(empty_set, 2)
                            sp.dma_start(placed.rearrange("(t p) f -> p t f", p=P),
                                         empty[:].unsqueeze(1).to_broadcast([P, ETILES, ROW])).then_inc(empty_out, 16)
                            for g in range(G):
                                sp.wait_ge(u_first[g], G)
                                sp.dma_start(table[0][g * G * P:(g + 1) * G * P, :].rearrange("(t p) f -> p t f", p=P),
                                             staging[:, g * G:(g + 1) * G, 0:D]).then_inc(u_out[g], 16)
                        if last_pass:
                            sp.dma_start(w1_s, w1.rearrange("(c f) h -> f c h", f=P)).then_inc(ffn_in, 16)
                            sp.dma_start(b1_s[:, 0, :], b1.rearrange("(c h) -> h c", h=P), allow_slow_non_contiguous=True).then_inc(ffn_in, 16)
                            sp.dma_start(wg_s, wg.rearrange("(c h) e -> h c e", h=P)).then_inc(ffn_in, 16)
                            sp.dma_start(bg_s[0:1, 0, :], bg.rearrange("(a e) -> a e", a=1)).then_inc(ffn_in, 16)
                            return

                        def per_round(i, has, first):
                            if has[0]:
                                if not (first and n == 0):
                                    sp.wait_ge(next_set, i + n * TILES)
                                sp.dma_start(xnT[:], xnT_d[bass.ds(i, 1)].rearrange("a p f -> p (a f)")).then_inc(xnT_load, 16)
                                if k == 1:
                                    sp.dma_start(xr[:], x[bass.ds(i * P, P), :]).then_inc(xr_load, 16)
                            if has[TABLE]:
                                sp.wait_ge(u_set, i + (n * TILES - TABLE + 1))
                                sp.dma_start(table[n + 1][bass.ds((i - TABLE) * P, P), :], tile(next_table, i - TABLE)).then_inc(next_out, 16)
                        over_rounds(sp, lags, per_round)
                        sp.wait_ge(next_out, (n + 1) * TILES * 16)
                        if n == 0:
                            sp.wait_ge(empty_out, 16)

                    @block.gpsimd
                    def _(pool):
                        if n == 0:
                            pool.memset(empty[:], 0.0).then_inc(empty_set, 1)
                            pool.wait_ge(empty_set, 1)
                            pool.memset(empty[:].bitcast(I32)[:, D + 1:D + 2], NP).then_inc(empty_set, 1)
                            for g in range(G):
                                pool.wait_ge(u_out[g], 16)
                        if last_pass:
                            pool.memset(eps, EPS).then_inc(norm_consts, 1)
                            pool.memset(minus_half, -0.5).then_inc(norm_consts, 1)
                            pool.wait_ge(norm_consts, 2)

                        def per_round(i, has, first):
                            for j in range(J):
                                if last_pass and has[NORM] and j == J // 2:
                                    pool.wait_ge(mv_set, i - NORM + 1)
                                    pool.tensor_tensor(rstd2[:, 0:1], mv2[:, 1:2], eps[:, 0, :], ALU.add).then_inc(eps_set, 1)
                                    pool.wait_ge(eps_set, i - NORM + 1)
                                    pool.tensor_tensor(rstd2[:, 1:2], rstd2[:, 0:1], minus_half[:, 0, :], ALU.pow).then_inc(rstd_set, 1)
                                if not has["items"]:
                                    continue
                                if j % (J // 2) == 0:
                                    pool.wait_ge(idx_set, i * 2 + (n * 2 * ROUNDS + j // (J // 2) + 1))
                                    pool.sem_inc(gathering, 1)
                                pool.indirect_dma_start(out=gath[:, j, :], out_offset=None, in_=table[n],
                                                        in_offset=bass.IndirectOffsetOnAxis(ap=idx[:, j:j + 1], axis=0)).then_inc(landed[j], 16)
                        over_rounds(pool, lags, per_round)

                    @block.scalar
                    def _(act):
                        if n == 0:
                            for g in range(0, G, 2):
                                with act.Fori(g * G, (g + 1) * G) as t:
                                    act.mul(tile(staging, t), tile(bufA, t), dis[:, bass.ds(t, 1)]).then_inc(u_first[g], 1)
                            act.wait_ge(empty_set, 1)

                        def gelu(i, h):
                            if not (isinstance(i, int) and i == GATE):
                                act.wait_ge(tails, i - GATE)
                            act.wait_ge(hid, (i - GATE) * 2 + (h + 1))
                            for q in range(HC // 2):
                                hc = h * (HC // 2) + q
                                last = act.activation(hT[:, 0, hc, :], psH2[:, h, q * P:(q + 1) * P], ACT.Gelu, bias=b1_s[:, 0, hc:hc + 1])
                            last.then_inc(gelus, 1)

                        def per_round(i, has, first):
                            if last_pass and has[GATE]:
                                gelu(i, 0)
                                gelu(i, 1)
                            if not last_pass and has[TABLE]:
                                act.wait_ge(empty_set, 1)
                                act.wait_ge(item_added, min(i, ROUNDS) * J + n * ITEMS if isinstance(i, int) else i * J + n * ITEMS)
                                act.mul(tile(next_table, i - TABLE), tile(acc, i - TABLE), dis[:, bass.ds(i - TABLE, 1)]).then_inc(u_set, 1)
                        if last_pass:
                            act.wait_ge(ffn_in, 64)
                        over_rounds(act, lags, per_round)

                    @block.vector
                    def _(dve):
                        dve.wait_ge(empty_set, 1)

                        def one_hot(i, j):
                            dve.tensor_scalar(hot[:, j % AHEAD, :], lanes[:], rel[:, bass.ds(i * J + j, 1)], None, ALU.is_equal).then_inc(hot_set, 1)

                        def refresh(i, h):
                            c = h * (J // 2)
                            dve.tensor_copy(idx[:, c:c + J // 2], col[:, bass.ds(i * J + c, J // 2)]).then_inc(idx_set, 1)

                        def add_item(i, j, t, first):
                            if not (first and n == 0 and j == 0):
                                dve.wait_ge(item_added, i * J + (n * ITEMS + j))
                            dve.wait_ge(item_mm, i * J + (n * ITEMS + j + 1))
                            dve.scalar_tensor_tensor(out=tile(acc, t), in0=psP[:, j % AHEAD, 0:D], scalar=minus[:, bass.ds(t, 1)],
                                                     in1=tile(acc, t), op0=ALU.mult, op1=ALU.add).then_inc(item_added, 1)

                        def fold(t):
                            dve.wait_ge(item_added, t * J + (n * ITEMS + J))
                            dve.scalar_tensor_tensor(out=tile(acc, t), in0=tile(prev, t), scalar=factor[:, bass.ds(t, 1)], in1=tile(acc, t),
                                                     op0=ALU.mult, op1=ALU.add).then_inc(folded, 1)

                        def prepare(t):
                            dve.wait_ge(next_mm, t + (n * TILES + 1))
                            if k == 2:
                                dve.tensor_tensor(tile(nxt, t), psX[:, 0:D], tile(prev, t), ALU.subtract).then_inc(next_set, 1)
                            else:
                                dve.tensor_tensor(tile(nxt, t), psX[:, 0:D], tile(prev, t), ALU.subtract).then_inc(next_diff, 1)
                                dve.wait_ge(next_diff, t + 1)
                                dve.wait_ge(xr_load, (t + 1) * 16)
                                dve.tensor_tensor(tile(nxt, t), tile(nxt, t), xr[:], ALU.add).then_inc(next_set, 1)

                        def whole(i):
                            t = i - WHOLE
                            dve.wait_ge(empty_set, 1)
                            dve.wait_ge(item_added, i * J + (n * ITEMS + READ) if not isinstance(i, int) else min(i * J + READ, ITEMS) + n * ITEMS)
                            dve.bn_stats(stat2[:], tile(bufA, t)).then_inc(stat_set, 1)
                            if not (isinstance(i, int) and t == 0):
                                dve.wait_ge(z_set, t)
                            dve.wait_ge(stat_set, t + 1)
                            dve.sem_inc(stat_seen, 1)
                            dve.bn_aggr(mv2[:], stat2[:]).then_inc(mv_set, 1)

                        def norm(i):
                            t = i - NORM
                            if not (isinstance(i, int) and t == 0):
                                dve.wait_ge(turned, t)
                            dve.wait_ge(rstd_set, t + 1)
                            dve.tensor_scalar(z[:, 0, :], tile(bufA, t), mv2[:, 0:1], rstd2[:, 1:2], ALU.subtract, ALU.mult).then_inc(z_set, 1)

                        def copy_zT(i):
                            dve.wait_ge(turned, i - HIDDEN + 1)
                            dve.tensor_copy(zT[:, 0, :], psX[:, 0:D]).then_inc(zT_set, 1)

                        def keep_logits(i):
                            dve.wait_ge(empty_set, 1)
                            dve.wait_ge(tails, i - GATE + 1)
                            dve.tensor_copy(logit[:, bass.ds(i - GATE, 1), :].rearrange("p a e -> p (a e)"), psO2[:, 0:NE]).then_inc(outs, 1)

                        def per_round(i, has, first):
                            if has["items"]:
                                _, ts = nc.values_load_multi_w_load_instructions(
                                    tile_of[0:1, bass.ds(i * J, J)], engines=[DVE], min_val=0, max_val=TILES - 1, skip_runtime_bounds_check_because=BOUNDED)
                            for j in range(J):
                                if has["items"]:
                                    if j == 0 and not (first and n == 0):
                                        dve.wait_ge(folded, i + n * TILES if has[0] else (n + 1) * TILES)
                                    add_item(i, j, ts[j], first)
                                    one_hot(i, j + AHEAD)
                                    if has["next"] and j % (J // 2) == J // 2 - 1:
                                        refresh(i + 1, j // (J // 2))
                                if last_pass:
                                    if j == 3 and has[HIDDEN]:
                                        copy_zT(i)
                                    if j == 7 and has[GATE]:
                                        keep_logits(i)
                                    if j == 13 and has[NORM]:
                                        norm(i)
                                    if j == 14 and has[WHOLE]:
                                        whole(i)
                            if has[0]:
                                if nxt is not None:
                                    if first and n == 0:
                                        for g in range(G):
                                            dve.wait_ge(u_out[g], 16)
                                    prepare(i)
                                fold(i)
                        if n == 0:
                            for g in range(1, G, 2):
                                with dve.Fori(g * G, (g + 1) * G) as t:
                                    dve.tensor_scalar(tile(staging, t), tile(bufA, t), dis[:, bass.ds(t, 1)], None, ALU.mult).then_inc(u_first[g], 1)
                        if n > 0:
                            dve.wait_ge(hot_set, n * (ITEMS + AHEAD))
                        refresh(0, 0)
                        refresh(0, 1)
                        for j in range(AHEAD):
                            one_hot(0, j)
                        over_rounds(dve, lags, per_round)
                        dve.wait_ge(item_added, (n + 1) * ITEMS)

                    @block.tensor
                    def _(pe):
                        def item(i, j, first):
                            pe.wait_ge(landed[j], (i + (n * ROUNDS + 1)) * 16)
                            pe.wait_ge(hot_set, i * J + (n * (ITEMS + AHEAD) + j + 1))
                            if not (first and n == 0 and j < AHEAD):
                                pe.wait_ge(item_added, i * J + (n * ITEMS + j + 1 - AHEAD))
                            pe.matmul(psP[:, j % AHEAD, 0:D], hot[:, j % AHEAD, :], gath[:, j, :], start=True, stop=True).then_inc(item_mm, 1)

                        def prepare(t, first):
                            pe.wait_ge(xnT_load, (t + (n * TILES + 1)) * 16)
                            if not (first and n == 0):
                                pe.wait_ge(next_set, t + n * TILES)
                            for c in range(KC):
                                last = pe.matmul(psX[:, 0:D], xnT[:, c * P:(c + 1) * P], wk[:, k - 1, c, :], start=(c == 0),
                                                 stop=(c == KC - 1 and k == 2))
                            if k == 1:
                                last = pe.matmul(psX[:, 0:D], ones[0:1, :], gbrow[:], start=False, stop=True)
                            last.then_inc(next_mm, 1)

                        def turn_z(i):
                            t = i - HIDDEN
                            if not (isinstance(i, int) and t == 0):
                                pe.wait_ge(zT_set, t)
                            pe.wait_ge(z_set, t + 1)
                            for c in range(KC):
                                last = pe.transpose(psX[:, c * P:(c + 1) * P], z[:, 0, c * P:(c + 1) * P], ident[:])
                            last.then_inc(turned, 1)

                        def hidden(i, h):
                            t = i - HIDDEN
                            if h == 0:
                                pe.wait_ge(zT_set, t + 1)
                            if not (isinstance(i, int) and t == 0):
                                pe.wait_ge(gelus, t * 2 - 1 + h)
                            for q in range(HC // 2):
                                hc = h * (HC // 2) + q
                                for c in range(KC):
                                    last = pe.matmul(psH2[:, h, q * P:(q + 1) * P], w1_s[:, c, hc * P:(hc + 1) * P], zT[:, 0, c * P:(c + 1) * P],
                                                     start=(c == 0), stop=(c == KC - 1))
                            last.then_inc(hid, 1)

                        def gate(i):
                            t = i - GATE
                            if not (isinstance(i, int) and t == 0):
                                pe.wait_ge(outs, t)
                            pe.wait_ge(gelus, t * 2 + 2)
                            for c in range(HC):
                                pe.matmul(psO2[:, 0:NE], hT[:, 0, c, :], wg_s[:, c, :], start=(c == 0), stop=False)
                            pe.matmul(psO2[:, 0:NE], ones[0:1, :], bg_s[0:1, 0, :], start=False, stop=True).then_inc(tails, 1)

                        def per_round(i, has, first):
                            for j in range(J):
                                if has["items"]:
                                    item(i, j, first)
                                if last_pass:
                                    if j == 0 and has[HIDDEN]:
                                        turn_z(i)
                                    if j == 4 and has[GATE]:
                                        gate(i)
                                    if j == 7 and has[HIDDEN]:
                                        hidden(i, 0)
                                    if j == 11 and has[HIDDEN]:
                                        hidden(i, 1)
                            if has[0] and not last_pass:
                                prepare(i, first)
                        if last_pass:
                            pe.wait_ge(ffn_in, 64)
                        over_rounds(pe, lags, per_round)

                if last_pass:
                    break
                again_set, again_out = sem(f"again_set{n}"), sem(f"again_out{n}")
                with nc.If(redo_pass == 1):
                    with nc.Block() as block:

                        @block.scalar
                        def _(act):
                            with act.Fori(0, TILES) as t:
                                act.mul(tile(next_table, t), tile(acc, t), dis[:, bass.ds(t, 1)]).then_inc(again_set, 1)

                        @block.sync
                        def _(sp):
                            sp.wait_ge(again_set, TILES)
                            sp.dma_start(table[n + 1].rearrange("(t p) f -> p t f", p=P), next_table[:, :, 0:D]).then_inc(again_out, 16)
                            sp.wait_ge(again_out, 16)

                        @block.gpsimd
                        def _(pool):
                            pool.sem_inc(branched, 1)

                        @block.vector
                        def _(dve):
                            dve.sem_inc(branched, 1)

                        @block.tensor
                        def _(pe):
                            pe.sem_inc(branched, 1)
        graph.close()

        ffn = ExitStack()
        wd_s = sb(ffn, "wd_s", [P, NE, HC, D])
        bd_s = sb(ffn, "bd_s", [1, NE, D])
        expert = sb(ffn, "expert", [1, ETILES], I32)
        psT = pb(ffn, "psT", [P, 2, 512])
        psH = pb(ffn, "psH", [P, 2, 2, 512])
        psO = pb(ffn, "psO", [P, 2, 512])
        wd_in = sem("wd_in")

        def ffn_turn(pe, z_set, turned, zT_set):
            def f(n, m, _):
                pe.wait_ge(zT_set, n + 1)
                pe.wait_ge(z_set, n + 1)
                for c in range(KC):
                    last = pe.transpose(psT[:, m % 2, c * P:(c + 1) * P], z[:, m % 4, c * P:(c + 1) * P], ident[:])
                last.then_inc(turned, 1)
            return f

        def ffn_hidden(pe, zT_set, hid, gelus):
            def f(n, m, _):
                pe.wait_ge(zT_set, n + 3)
                for h in range(2):
                    pe.wait_ge(gelus, n * 2 + (h + 1))
                    for q in range(HC // 2):
                        hc = h * (HC // 2) + q
                        for c in range(KC):
                            last = pe.matmul(psH[:, m % 2, h, q * P:(q + 1) * P], w1_s[:, c, hc * P:(hc + 1) * P], zT[:, m % 2, c * P:(c + 1) * P],
                                             start=(c == 0), stop=(c == KC - 1))
                    last.then_inc(hid, 1)
            return f

        def ffn_gelu(act, hid, gelus, tails):
            def f(n, m, _):
                act.wait_ge(tails, n + 1)
                for h in range(2):
                    act.wait_ge(hid, n * 2 + (h + 1))
                    for q in range(HC // 2):
                        hc = h * (HC // 2) + q
                        last = act.activation(hT[:, m % 2, hc, :], psH[:, m % 2, h, q * P:(q + 1) * P], ACT.Gelu, bias=b1_s[:, 0, hc:hc + 1])
                    last.then_inc(gelus, 1)
            return f

        def ffn_zT(dve, turned, zT_set):
            def f(n, m, _):
                dve.wait_ge(turned, n + 1)
                dve.tensor_copy(zT[:, m % 2, :], psT[:, m % 2, 0:D]).then_inc(zT_set, 1)
            return f

        with ExitStack() as s3:
            stats = sb(s3, "stats3", [P, TILES, 6])
            mean = sb(s3, "mean3", [P, TILES])
            var = sb(s3, "var3", [P, TILES])
            rstd = sb(s3, "rstd3", [P, TILES])
            shift = sb(s3, "shift3", [P, TILES])
            ln3, rstd3_seq = sem("ln3"), sem("rstd3_seq")
            z_set, turned, zT_set, hid, gelus, tails, outs = (sem(f"{a}_3") for a in ("z_set", "turned", "zT_set", "hid", "gelus", "tails", "outs"))

            with nc.If(redo_pass == 1):
                with nc.Block() as block:

                    @block.sync
                    def _(sp):
                        sp.sem_inc(branched, 1)

                    @block.gpsimd
                    def _(pool):
                        pool.wait_ge(ln3, TILES + MOMENTS)
                        pool.tensor_scalar(rstd[:], var[:], EPS, None, ALU.add).then_inc(rstd3_seq, 1)
                        pool.wait_ge(rstd3_seq, 1)
                        pool.tensor_tensor(rstd[:], rstd[:], minus_half[:, 0, :].to_broadcast([P, TILES]), ALU.pow).then_inc(rstd3_seq, 1)
                        pool.wait_ge(rstd3_seq, 2)
                        pool.tensor_tensor(shift[:], mean[:], rstd[:], ALU.mult).then_inc(rstd3_seq, 1)
                        pool.wait_ge(rstd3_seq, 3)
                        pool.tensor_scalar(shift[:], shift[:], -0.5, None, ALU.mult).then_inc(rstd3_seq, 1)

                    @block.scalar
                    def _(act):
                        act.wait_ge(rstd3_seq, 4)
                        act.sem_inc(gelus, 4)

                        def norm(n, m, _):
                            act.activation(z[:, m % 4, :], bufA[:, bass.ds(n, 1), 0:D].rearrange("p a f -> p (a f)"), ACT.Identity,
                                           bias=shift[:, bass.ds(n, 1)], scale=rstd[:, bass.ds(n, 1)]).then_inc(z_set, 1)
                        in_turn(act, TILES, [(2, norm), (0, ffn_gelu(act, hid, gelus, tails))])

                    @block.vector
                    def _(dve):
                        with dve.Fori(0, TILES) as t:
                            dve.bn_stats(stats[:, bass.ds(t, 1), :].rearrange("p a f -> p (a f)"),
                                         bufA[:, bass.ds(t, 1), 0:D].rearrange("p a f -> p (a f)")).then_inc(ln3, 1)
                        dve.wait_ge(ln3, TILES)
                        moments(dve, stats, mean, var, ln3, TILES)
                        dve.sem_inc(zT_set, 2)
                        dve.sem_inc(outs, 2)

                        def keep_logits(n, m, _):
                            dve.wait_ge(ln3, TILES)
                            dve.wait_ge(tails, n + 3)
                            dve.tensor_copy(logit[:, bass.ds(n, 1), :].rearrange("p a e -> p (a e)"), psO[:, m % 2, 0:NE]).then_inc(outs, 1)
                        in_turn(dve, TILES, [(1, ffn_zT(dve, turned, zT_set)), (-1, keep_logits)])
                        dve.wait_ge(outs, TILES + 2)

                    @block.tensor
                    def _(pe):
                        pe.sem_inc(tails, 2)

                        def gate(n, m, _):
                            pe.wait_ge(gelus, n * 2 + 6)
                            pe.wait_ge(outs, n + 1)
                            for c in range(HC):
                                pe.matmul(psO[:, m % 2, 0:NE], hT[:, m % 2, c, :], wg_s[:, c, :], start=(c == 0), stop=False)
                            pe.matmul(psO[:, m % 2, 0:NE], ones[0:1, :], bg_s[0:1, 0, :], start=False, stop=True).then_inc(tails, 1)
                        in_turn(pe, TILES, [(1, ffn_turn(pe, z_set, turned, zT_set)), (0, ffn_hidden(pe, zT_set, hid, gelus)), (-1, gate)])

            part = sb(s3, "part", [P, 1])
            before = sb(s3, "before", [P, P])
            falling = sb(s3, "falling", [P, NE])
            etile = sb(s3, "etile", [P, ETILES])
            prob = sb(s3, "prob", [P, TILES, NE])
            mine = sb(s3, "mine", [P, TILES, NE])
            most = sb(s3, "most", [P, TILES])
            total = sb(s3, "total", [P, TILES])
            per_tile = sb(s3, "per_tile", [P, NE, TILES])
            upto = sb(s3, "upto", [P, NE, TILES])
            need = sb(s3, "need", [P, NE])
            need_i = sb(s3, "need_i", [P, NE], I32)
            start = sb(s3, "start", [P, NE])
            exf = sb(s3, "exf", [P, ETILES])
            pos = sb(s3, "pos", [P, TILES], U32)
            c3, route, exp_in, exp_out = sem("c3"), sem("route"), sem("exp_in"), sem("exp_out")
            mine_set, ranked, pos_set, scattered = sem("mine_set"), sem("ranked"), sem("pos_set"), sem("scattered")

            block = s3.enter_context(nc.Block())

            @block.sync
            def _(sp):
                sp.dma_start(bd_s[:], bd.rearrange("(a e) o -> a e o", a=1)).then_inc(wd_in, 16)
                for e in range(NE):
                    sp.dma_start(wd_s[:, e, :, :], wd[e].rearrange("(c h) o -> h c o", h=P)).then_inc(wd_in, 16)

            @block.gpsimd
            def _(pool):
                pool.memset(bufA[:, :, D:ROW], 0.0).then_inc(c3, 1)
                pool.iota(part[:], [[0, 1]], base=0, channel_multiplier=1, allow_small_or_imprecise_dtypes=True).then_inc(c3, 1)
                pool.iota(falling[:], [[-1, NE]], base=NE, channel_multiplier=0, allow_small_or_imprecise_dtypes=True).then_inc(c3, 1)
                pool.iota(etile[:], [[1, ETILES]], base=0, channel_multiplier=0, allow_small_or_imprecise_dtypes=True).then_inc(c3, 1)
                pool.wait_ge(c3, 4)
                pool.iota(bufA[:].bitcast(I32)[:, :, D + 1], [[P, TILES]], base=0, channel_multiplier=1).then_inc(c3, 1)
                pool.wait_ge(pos_set, 1)
                for t in range(TILES):
                    pool.indirect_dma_start(out=placed, out_offset=bass.IndirectOffsetOnAxis(ap=pos[:, t:t + 1], axis=0),
                                            in_=bufA[:, t, :], in_offset=None).then_inc(scattered, 16)
                pool.wait_ge(scattered, 16 * TILES)

            @block.scalar
            def _(act):
                act.wait_ge(exp_in, 1)
                act.activation(prob[:], logit, ACT.Exp).then_inc(exp_out, 1)

            @block.vector
            def _(dve):
                dve.wait_ge(c3, 5)

                count = [0]

                def step(ins):
                    count[0] += 1
                    ins.then_inc(route, 1)
                    dve.wait_ge(route, count[0])

                def over_experts(t):
                    return t[:].unsqueeze(2).to_broadcast([P, TILES, NE])
                step(dve.tensor_reduce(most[:], logit, AX, ALU.max))
                step(dve.tensor_tensor(logit, logit, over_experts(most), ALU.subtract))
                dve.sem_inc(exp_in, 1)
                step(dve.tensor_scalar(before[:], lanes[:], part[:, 0:1], None, ALU.is_gt))
                dve.wait_ge(exp_out, 1)
                step(dve.tensor_reduce(total[:], prob[:], AX, ALU.add))
                step(dve.reciprocal(total[:], total[:]))
                step(dve.tensor_tensor(prob[:], prob[:], over_experts(total), ALU.mult))
                step(dve.tensor_reduce(most[:], prob[:], AX, ALU.max))
                step(dve.tensor_copy(bufA[:, :, D], most[:]))
                step(dve.tensor_tensor(mine[:], prob[:], over_experts(most), ALU.is_equal))
                step(dve.tensor_tensor(mine[:], mine[:], falling[:].unsqueeze(1).to_broadcast([P, TILES, NE]), ALU.mult))
                step(dve.tensor_reduce(most[:], mine[:], AX, ALU.max))
                step(dve.tensor_tensor(mine[:], mine[:], over_experts(most), ALU.is_equal))
                dve.sem_inc(mine_set, 1)
                dve.wait_ge(ranked, 1)
                step(dve.tensor_copy(per_tile[:], psO[:, 1, 0:TILES * NE].rearrange("p (t e) -> p e t", e=NE)))
                for e in range(NE):
                    step(dve.tensor_tensor_scan(upto[:, e, :], ones[:, 0:TILES], per_tile[:, e, :], 0.0, ALU.mult, ALU.add))
                step(dve.tensor_scalar(need[:], upto[:, :, TILES - 1], float(P - 1), None, ALU.add))
                step(dve.tensor_copy(need_i[:], need[:]))
                step(dve.tensor_scalar(need_i[:], need_i[:], 7, None, ALU.logical_shift_right))
                step(dve.tensor_copy(need[:], need_i[:]))
                step(dve.tensor_tensor_scan(start[:], ones[:, 0:NE], need[:], 0.0, ALU.mult, ALU.add))
                step(dve.tensor_tensor(start[:], start[:], need[:], ALU.subtract))
                step(dve.tensor_tensor(upto[:], upto[:], per_tile[:], ALU.subtract))
                step(dve.scalar_tensor_tensor(upto[:], start[:].unsqueeze(2).to_broadcast([P, NE, TILES]), float(P), upto[:], ALU.mult, ALU.add))
                step(dve.tensor_tensor(prob[:], psO[:, 0, 0:TILES * NE].rearrange("p (t e) -> p t e", e=NE), upto[:].rearrange("p e t -> p t e"), ALU.add))
                step(dve.tensor_tensor(prob[:], prob[:], mine[:], ALU.mult))
                step(dve.tensor_reduce(most[:], prob[:], AX, ALU.add))
                step(dve.tensor_copy(pos[:], most[:]))
                dve.sem_inc(pos_set, 1)
                step(dve.tensor_scalar(exf[:], etile[:], start[:, 1:2], None, ALU.is_ge))
                for e in range(2, NE):
                    step(dve.scalar_tensor_tensor(exf[:], etile[:], start[:, e:e + 1], exf[:], ALU.is_ge, ALU.add))
                step(dve.tensor_copy(expert[:], exf[0:1, :]))

            @block.tensor
            def _(pe):
                pe.wait_ge(mine_set, 1)
                flat = mine[:].rearrange("p t e -> p (t e)")
                pe.matmul(psO[:, 0, 0:TILES * NE], before[:], flat, start=True, stop=True)
                pe.matmul(psO[:, 1, 0:TILES * NE], ones[:], flat, start=True, stop=True).then_inc(ranked, 1)

        with ExitStack() as s4:
            rows = sb(s4, "rows", [P, UNROLL, ROW])
            result = sb(s4, "result", [P, UNROLL, D])
            stats = sb(s4, "stats4", [P, 4, 6])
            mv = sb(s4, "mv4", [P, 4, 2])
            rstd = sb(s4, "rstd4", [P, 4, 2])

            row_in = [sem(f"row_in{j}") for j in range(UNROLL)]
            row_out = [sem(f"row_out{j}") for j in range(UNROLL)]
            stat4, stat4_seen, mv_set, eps_set, rstd_set, scatters = sem("stat4"), sem("stat4_seen"), sem("mv_set"), sem("eps_set"), sem("rstd_set"), sem("scatters")
            z_set, turned, zT_set, hid, gelus, tails, outs = (sem(f"{a}_4") for a in ("z_set", "turned", "zT_set", "hid", "gelus", "tails", "outs"))

            block = s4.enter_context(nc.Block())

            @block.sync
            def _(sp):
                def load(i, j, first):
                    if not first:
                        sp.wait_ge(row_out[j], i * 16)
                    n = i * UNROLL + j
                    sp.dma_start(rows[:, j, :], placed[bass.ds(n * P, P), :]).then_inc(row_in[j], 16)
                for j in range(UNROLL):
                    load(0, j, True)
                with sp.Fori(1, ETILES // UNROLL) as i:
                    for j in range(UNROLL):
                        load(i, j, False)
                for j in range(UNROLL):
                    sp.wait_ge(row_out[j], 16 * (ETILES // UNROLL))

            @block.gpsimd
            def _(pool):
                def root(n, m, _):
                    pool.wait_ge(mv_set, n + 1)
                    pool.tensor_tensor(rstd[:, m % 4, 0:1], mv[:, m % 4, 1:2], eps[:, 0, :], ALU.add).then_inc(eps_set, 1)
                    pool.wait_ge(eps_set, n + 1)
                    pool.tensor_tensor(rstd[:, m % 4, 1:2], rstd[:, m % 4, 0:1], minus_half[:, 0, :], ALU.pow).then_inc(rstd_set, 1)

                def scatter(n, m, _):
                    pool.wait_ge(outs, n + 3)
                    pool.sem_inc(scatters, 1)
                    pool.indirect_dma_start(out=out, out_offset=bass.IndirectOffsetOnAxis(ap=rows[:].bitcast(U32)[:, m, D + 1:D + 2], axis=0),
                                            in_=result[:, m, :], in_offset=None, bounds_check=NP - 1, oob_is_err=False).then_inc(row_out[m], 16)
                in_turn(pool, ETILES, [(3, root), (-1, scatter)])

            @block.scalar
            def _(act):
                act.sem_inc(gelus, 4)
                in_turn(act, ETILES, [(0, ffn_gelu(act, hid, gelus, tails))])

            @block.vector
            def _(dve):
                dve.sem_inc(zT_set, 2)
                dve.sem_inc(outs, 2)

                def statistics(n, m, turn):
                    dve.wait_ge(row_in[m], (turn + 1) * 16)
                    dve.bn_stats(stats[:, m % 4, :], rows[:, m, 0:D]).then_inc(stat4, 1)
                    dve.wait_ge(stat4, n + 1)
                    dve.sem_inc(stat4_seen, 1)
                    dve.bn_aggr(mv[:, m % 4, :], stats[:, m % 4, :]).then_inc(mv_set, 1)

                def norm(n, m, _):
                    dve.wait_ge(rstd_set, n + 1)
                    dve.tensor_scalar(z[:, m % 4, :], rows[:, m, 0:D], mv[:, m % 4, 0:1], rstd[:, m % 4, 1:2], ALU.subtract, ALU.mult).then_inc(z_set, 1)

                def finish(n, m, _):
                    dve.wait_ge(tails, n + 3)
                    dve.scalar_tensor_tensor(out=result[:, m, :], in0=psO[:, m % 2, 0:D], scalar=rows[:, m, D:D + 1], in1=rows[:, m, 0:D],
                                             op0=ALU.mult, op1=ALU.add).then_inc(outs, 1)
                in_turn(dve, ETILES, [(3, statistics), (2, norm), (1, ffn_zT(dve, turned, zT_set)), (-1, finish)])

            @block.tensor
            def _(pe):
                pe.wait_ge(wd_in, 16 * (NE + 1))
                pe.sem_inc(tails, 2)

                def product(n, m, _):
                    _, (e,) = nc.values_load_multi_w_load_instructions(
                        expert[0:1, bass.ds(n, 1)], engines=[PEE], min_val=0, max_val=NE - 1, skip_runtime_bounds_check_because=BOUNDED)
                    pe.wait_ge(gelus, n * 2 + 6)
                    pe.wait_ge(outs, n + 1)
                    for c in range(HC):
                        pe.matmul(psO[:, m % 2, 0:D], hT[:, m % 2, c, :], wd_s[:, bass.ds(e, 1), c, :].rearrange("p a o -> p (a o)"), start=(c == 0), stop=False)
                    pe.matmul(psO[:, m % 2, 0:D], ones[0:1, :], bd_s[:, bass.ds(e, 1), :].rearrange("p a o -> p (a o)"), start=False, stop=True).then_inc(tails, 1)
                in_turn(pe, ETILES, [(1, ffn_turn(pe, z_set, turned, zT_set)), (0, ffn_hidden(pe, zT_set, hid, gelus)), (-1, product)])
        ffn.close()


_INS = ["x", "src", "dst", "L0_gnn_weight", "L0_gnn_bias", "L0_ffn_W1", "L0_ffn_b1", "L0_ffn_Wg", "L0_ffn_bg", "L0_ffn_Wd", "L0_ffn_bd"]


def kernel(**inputs):
    import numpy as np
    import concourse.bacc as bacc
    from concourse.bass_utils import run_bass_kernel_spmd

    nodes, features = inputs["x"].shape
    padded = -(-nodes // P) * P
    nc = bacc.Bacc("TRN2", target_bir_lowering=False, num_devices=1)
    arrays, args = {}, []
    for name in _INS:
        a = np.ascontiguousarray(inputs[name])
        if name == "x":
            a = np.pad(a, ((0, padded - nodes), (0, 0)))
        arrays[f"in_{name}"] = a
        args.append(nc.dram_tensor(f"in_{name}", a.shape, mybir.dt.from_np(a.dtype), kind="ExternalInput").ap())
    out = nc.dram_tensor("out", (padded, features), F32, kind="ExternalOutput").ap()
    gnn_ffn_kernel(nc, *args, out)
    r = run_bass_kernel_spmd(nc, [arrays], core_ids=[0])
    return r.results[0]["out"][:nodes]
```

```python
from contextlib import ExitStack

import concourse.bass as bass
from concourse import mybir

F32 = mybir.dt.float32
BF16 = mybir.dt.bfloat16
F16 = mybir.dt.float16
I32 = mybir.dt.int32
U32 = mybir.dt.uint32
ALU = mybir.AluOpType
ACT = mybir.ActivationFunctionType
AX = mybir.AxisListType.X
DVE = mybir.EngineType.DVE
PEE = mybir.EngineType.PE

P = 128
MOMENTS = 5
UNROLL = 8
BOUNDED = "bounded by how the numbers are built"


def moments(dve, stats, mean, var, done, count):
    half = 128.0
    even, odd = stats[:, :, 1], stats[:, :, 4]
    dve.tensor_tensor(mean[:], even, odd, ALU.subtract).then_inc(done, 1)
    dve.wait_ge(done, count + 1)
    dve.scalar_tensor_tensor(var[:], mean[:], 0.25, mean[:], ALU.mult, ALU.mult).then_inc(done, 1)
    dve.wait_ge(done, count + 2)
    for q in (2, 5):
        dve.scalar_tensor_tensor(var[:], stats[:, :, q], 0.5 / half, var[:], ALU.mult, ALU.add).then_inc(done, 1)
        dve.wait_ge(done, count + (3 if q == 2 else 4))
    dve.tensor_tensor(mean[:], even, odd, ALU.add).then_inc(done, 1)
    dve.wait_ge(done, count + 5)


def in_turn(engine, total, steps):
    first, last = -min(lead for lead, _ in steps), total - max(lead for lead, _ in steps)
    rounds = (last - first) // UNROLL

    def one(n):
        for lead, f in steps:
            if 0 <= n + lead < total:
                f(n + lead, (n + lead) % UNROLL, (n + lead) // UNROLL)
    for n in range(-max(lead for lead, _ in steps), first):
        one(n)
    with engine.Fori(0, rounds) as i:
        for j in range(UNROLL):
            for lead, f in steps:
                m = first + j + lead
                f(i * UNROLL + m, m % UNROLL, i + m // UNROLL)
    for n in range(first + rounds * UNROLL, total - min(lead for lead, _ in steps)):
        one(n)


def gnn_ffn_kernel(nc, x, src, dst, gw, gb, w1, b1, wg, bg, wd, bd, out):
    NP, D = x.shape
    TILES = NP // P
    E = src.shape[0]
    KC = D // P
    CHUNKS = -(-E // P)
    SB = 8
    SN = SB * P
    J = 16
    EXT = 2 * TILES
    HOTS = 4
    WIN = 8
    ROUNDS = -(-(CHUNKS + EXT - 1) // (2 * J)) * 2
    ITEMS = ROUNDS * J
    HALF = ITEMS // 2
    WB = -(-ITEMS // P)
    AHEAD = 4
    COLBITS = 13
    COLMASK = (1 << COLBITS) - 1
    ROWMASK = (1 << (COLBITS + 1)) - 1
    NORMAL = 1 << 29
    EPS = 1e-5
    HID = w1.shape[1]
    HC = HID // P
    NE = wd.shape[0]
    ETILES = TILES + NE - 1
    ROW = 260
    EARLY = 4
    MEET = 3
    ESRC, EW = 125, 800
    G = 7
    FJ, FROUNDS = 12, 51
    PARTS = 4
    LAG, READ = 3, 11
    assert ESRC * EW == E and EW <= SN and SN * P >= E and NP <= COLMASK + 1
    assert CHUNKS <= SB * P and TILES == G * G and ETILES % G == 0 and D == 2 * P

    xnT_d = nc.dram_tensor("xnT", [TILES, P, D], F32, kind="Internal").ap()
    table = [nc.dram_tensor(f"table{k}", [NP, D], F32, kind="Internal").ap() for k in range(3)]
    ct_d = nc.dram_tensor("ct_d", [TILES, P, HOTS * P], BF16, kind="Internal").ap()
    placed = nc.dram_tensor("placed", [ETILES * P, ROW], F32, kind="Internal").ap()

    outer = ExitStack()
    with outer:
        def sb(ctx, name, shape, dt=F32):
            return ctx.enter_context(nc.sbuf_tensor(name, shape, dt))

        def pb(ctx, name, shape, dt=F32):
            return ctx.enter_context(nc.psum_tensor(name, shape, dt))

        def sem(name):
            return outer.enter_context(nc.semaphore(name))

        ident = sb(outer, "ident", [P, P])
        lanes = sb(outer, "lanes", [P, P])
        ones = sb(outer, "ones", [P, P])
        bufA = sb(outer, "bufA", [P, TILES, ROW])

        bufB = sb(outer, "bufB", [P, TILES, D])
        fits = sb(outer, "fits", [1, 1], I32)

        taken = [0]

        def take(*shape):
            size = 1
            for n in shape:
                size *= n
            flat = bufB[:].rearrange("p t f -> p (t f)")[:, taken[0]:taken[0] + size]
            taken[0] += size
            assert taken[0] <= TILES * D
            names = "abc"[:len(shape)]
            return flat.rearrange(f"p ({' '.join(names)}) -> p {' '.join(names)}", **dict(zip(names, shape)))
        w1_s = take(KC, HID)
        b1_s = take(1, HC)
        wg_s = take(HC, NE)
        bg_s = take(1, NE)
        z = take(4, D)
        zT = take(2, D)
        hT = take(2, HC, P)
        logit = take(TILES, NE)
        minus_half = take(1, 1)
        eps = take(1, 1)

        graph = ExitStack()
        rel = sb(graph, "rel", [P, ITEMS + AHEAD])
        col = sb(graph, "col", [P, ITEMS], U32)
        tile_of = sb(graph, "tile_of", [1, ITEMS], I32)
        wk = sb(graph, "wk", [P, 4, KC, D])
        gbrow = sb(graph, "gbrow", [1, D])
        dis = sb(graph, "dis", [P, TILES])
        sc1 = sb(graph, "sc1", [P, TILES])
        sc2 = sb(graph, "sc2", [P, TILES])
        nd1 = sb(graph, "nd1", [P, TILES])
        nd2 = sb(graph, "nd2", [P, TILES])

        rel1 = sb(graph, "rel1", [P, ITEMS + WIN], F16)
        colh = sb(graph, "colh", [P, ITEMS + WIN], F16)
        tileh = sb(graph, "tileh", [P, ITEMS + WIN], F16)
        first_item = sb(graph, "first_item", [1, TILES], I32)
        hot_tile = sb(graph, "hot_tile", [P, TILES])

        with ExitStack() as s1:
            edges = sb(s1, "edges", [P, 2, SN], I32)
            keys = [sb(s1, f"keys{i}", [P, SN]) for i in range(2)]
            sign0 = sb(s1, "sign0", [P, 1])
            lane_i = sb(s1, "lane_i", [P, P], I32)
            gray = sb(s1, "gray", [P, P], I32)
            bits = sb(s1, "bits", [P, P], I32)
            bitsf = sb(s1, "bitsf", [P, P])
            turn = sb(s1, "turn", [P, 7, P])
            part_i = sb(s1, "part_i", [P, 1], I32)
            chunk = sb(s1, "chunk", [P, SB])
            spanned = sb(s1, "spanned", [P, 2, TILES])
            excess = sb(s1, "excess", [P, 4])
            repeats = sb(s1, "repeats", [P, 1])
            lanes2 = sb(s1, "lanes2", [P, P, J], BF16)
            chunk1 = sb(s1, "chunk1", [P, SB, P])
            iw = sb(s1, "iw", [P, ITEMS])
            tmp = sb(s1, "tmp", [P, ITEMS])
            lohi_i = sb(s1, "lohi_i", [P, 2, SB], I32)
            lohi = sb(s1, "lohi", [P, 2, SB])
            pick = sb(s1, "pick", [P, SB * ITEMS])
            twf = sb(s1, "twf", [P, WB * P])
            relb = sb(s1, "relb", [P, ITEMS], BF16)
            pairs = sb(s1, "pairs", [P, ITEMS, 2], BF16)
            tile_hot = sb(s1, "tile_hot", [P, WB, EXT])
            deg = sb(s1, "deg", [P, TILES])
            stats = sb(s1, "stats", [P, TILES, 6])
            mean = sb(s1, "mean", [P, TILES])
            var = sb(s1, "var", [P, TILES])
            rstd = sb(s1, "rstd", [P, TILES])
            shift = sb(s1, "shift", [P, TILES])
            xn = pick[:, 2 * SN:2 * SN + 3 * D].rearrange("p (s f) -> p s f", s=3)
            half_neg = sb(s1, "half_neg", [P, TILES])
            xT = pick[:, 3 * SN:3 * SN + G * D].rearrange("p (s f) -> p s f", s=G)
            assert 3 * D <= SN and 3 * SN + G * D <= SB * ITEMS
            psN = pb(s1, "psN", [P, 2, 512])
            psW = pb(s1, "psW", [P, 2, 2 * D])
            psS = pb(s1, "psS", [P, 2, 512])
            psI = pb(s1, "psI", [P, 2, 512])
            psM = psN[:, 0, :]

            edges_in, wk_in = sem("edges_in"), sem("wk_in")
            x_in = [sem(f"x_in{g}") for g in range(G)]
            consts = sem("consts")
            edges_set = sem("edges_set")
            rstd_done, normed = sem("rstd_done"), sem("normed")
            ln_seq, pool_seq = sem("ln_seq"), sem("pool_seq")
            turned, xT_set, mm_done, mm_out = sem("turned"), sem("xT_set"), sem("mm_done"), sem("mm_out")
            xT_out = [sem(f"xT_out{j}") for j in range(G)]
            seq = sem("seq")
            sort_T = sem("sort_T")
            quant_ready, item_sum, item_out = sem("quant_ready"), sem("item_sum"), sem("item_out")
            tw_ready, twT_done = sem("tw_ready"), sem("twT_done")
            level_sorted = sem("level_sorted")
            hot_ready, hist_mm, hist_out = sem("hot_ready"), sem("hist_mm"), sem("hist_out")
            cnt_turned, cnt_set, deg_done = sem("cnt_turned"), sem("cnt_set"), sem("deg_done")
            deg_set, dis_done = sem("deg_set"), sem("dis_done")

            at, source = (1 + 55) % 2, {}
            for k in range(1, 8):
                for way in range(2):
                    source[k, way] = at
                    at = (at + 1 + (k if way == 0 else 10)) % 2
            srt = keys[at][:].bitcast(I32)
            rowf, colf = keys[1 - at], keys[at]
            selff = edges[:, 0, :].bitcast(F32)
            klass = pick[:, 0:SN].bitcast(I32)
            spans = pick[:, SN:SN + EXT * SB].rearrange("p (s t b) -> p s t b", s=2, b=SB)
            picks = pick[:].rearrange("p (b w) -> p b w", b=SB)
            counts = pick[:, 0:WB * P * 2].rearrange("p (w s) -> p w s", s=2)
            countsT = pick[:, WB * P * 2:WB * P * 4].rearrange("p (m r) -> p m r", r=P)
            hot = pick[:, WB * P * 4:WB * P * 4 + J * P].bitcast(BF16).rearrange("p (h r j) -> p h r j", h=2, j=J)

            block = s1.enter_context(nc.Block())

            @block.sync
            def _(sp):
                sp.wait_ge(edges_set, 1)
                sp.dma_start(edges[0:ESRC, 0, 0:EW], src.rearrange("(p f) -> p f", f=EW)).then_inc(edges_in, 16)
                sp.dma_start(edges[0:ESRC, 1, 0:EW], dst.rearrange("(p f) -> p f", f=EW)).then_inc(edges_in, 16)
                for g in range(G):
                    sp.dma_start(bufA[:, g * G:(g + 1) * G, 0:D],
                                 x[g * G * P:(g + 1) * G * P, :].rearrange("(t p) f -> p t f", p=P)).then_inc(x_in[g], 16)
                for k in range(4):
                    sp.dma_start(wk[:, k, :, :], gw[k].rearrange("(c f) o -> f c o", f=P)).then_inc(wk_in, 16)
                sp.dma_start(gbrow[:], gb.rearrange("(a o) -> a o", a=1)).then_inc(wk_in, 16)
                def store(i):
                    for j in range(G):
                        sp.wait_ge(xT_set, i * G + (j + 1))
                        sp.dma_start(xnT_d[bass.ds(i * G + j, 1)].rearrange("a p f -> p (a f)"), xT[:, j, :]).then_inc(xT_out[j], 16)
                store(0)
                with sp.Fori(1, G) as i:
                    store(i)
                for j in range(G):
                    sp.wait_ge(xT_out[j], 16 * G)

            @block.gpsimd
            def _(pool):
                pool.memset(edges[:, 0, :], NP - 1).then_inc(pool_seq, 1)
                pool.memset(edges[:, 1, :], 0).then_inc(pool_seq, 1)
                pool.wait_ge(pool_seq, 2)
                pool.sem_inc(edges_set, 1)
                pool.iota(lane_i[:], [[1, P]], base=0, channel_multiplier=0).then_inc(consts, 1)
                pool.iota(part_i[:], [[0, 1]], base=0, channel_multiplier=1).then_inc(consts, 1)
                pool.iota(lanes[:], [[1, P]], base=0, channel_multiplier=0, allow_small_or_imprecise_dtypes=True).then_inc(consts, 1)
                pool.iota(iw[:], [[1, ITEMS]], base=0, channel_multiplier=0, allow_small_or_imprecise_dtypes=True).then_inc(consts, 1)
                pool.iota(chunk[:], [[1, SB]], base=0, channel_multiplier=SB, allow_small_or_imprecise_dtypes=True).then_inc(consts, 1)
                pool.iota(chunk1[:], [[1, SB], [0, P]], base=1, channel_multiplier=SB, allow_small_or_imprecise_dtypes=True).then_inc(consts, 1)
                pool.memset(ident[:], 0.0).then_inc(pool_seq, 1)
                pool.memset(ones[:], 1.0).then_inc(consts, 1)
                pool.memset(half_neg[:], -0.5).then_inc(pool_seq, 1)
                pool.memset(pairs[:], 1.0).then_inc(consts, 1)
                pool.iota(lanes2[:], [[1, P], [0, J]], base=0, channel_multiplier=0, allow_small_or_imprecise_dtypes=True).then_inc(consts, 1)
                pool.iota(hot_tile[:], [[1, TILES]], base=TILES, channel_multiplier=0, allow_small_or_imprecise_dtypes=True).then_inc(consts, 1)
                pool.wait_ge(pool_seq, 4)
                pool.affine_select(out=ident[:], in_=ident[:], compare_op=ALU.not_equal, fill=1.0, base=0,
                                   pattern=[[-1, P]], channel_multiplier=1).then_inc(consts, 1)
                pool.wait_ge(ln_seq, TILES + MOMENTS)
                pool.tensor_scalar(rstd[:], var[:], EPS, None, ALU.add).then_inc(pool_seq, 1)
                pool.wait_ge(pool_seq, 5)
                pool.tensor_tensor(rstd[:], rstd[:], half_neg[:], ALU.pow).then_inc(pool_seq, 1)
                pool.wait_ge(pool_seq, 6)
                pool.tensor_tensor(shift[:], mean[:], rstd[:], ALU.mult).then_inc(pool_seq, 1)
                pool.wait_ge(pool_seq, 7)
                pool.tensor_scalar(shift[:], shift[:], -0.5, None, ALU.mult).then_inc(rstd_done, 1)
                pool.wait_ge(deg_set, 1)
                pool.tensor_tensor(dis[:], deg[:], half_neg[:], ALU.pow).then_inc(dis_done, 1)

            @block.scalar
            def _(act):
                def norm(i, j):
                    act.activation(xn[:, j % 3, :], bufA[:, bass.ds(i * G + j, 1), 0:D].rearrange("p a f -> p (a f)"), ACT.Identity,
                                   bias=shift[:, bass.ds(i * G + j, 1)], scale=rstd[:, bass.ds(i * G + j, 1)]).then_inc(normed, 1)

                def xT_evac(i, j, first):
                    act.wait_ge(turned, i * G + (j + 1))
                    if not first:
                        act.wait_ge(xT_out[j], i * 16)
                    act.copy(xT[:, j, :], psN[:, j % 2, 0:D]).then_inc(xT_set, 1)

                def mm_evac(i, j):
                    act.wait_ge(rstd_done, 1)
                    act.wait_ge(mm_done, i * G + (j + 1))
                    act.copy(bufA[:, bass.ds(i * G + j, 1), 0:D].rearrange("p a f -> p (a f)"), psW[:, j % 2, 0:D])
                    act.copy(bufB[:, bass.ds(i * G + j, 1), :].rearrange("p a f -> p (a f)"), psW[:, j % 2, D:2 * D]).then_inc(mm_out, 1)

                def group(i, first):
                    norm(i, 0)
                    norm(i, 1)
                    xT_evac(i, 0, first)
                    for j in range(G):
                        if j + 2 < G:
                            norm(i, j + 2)
                        if j + 1 < G:
                            xT_evac(i, j + 1, first)
                        mm_evac(i, j)
                act.wait_ge(rstd_done, 1)
                group(0, True)
                with act.Fori(1, G) as i:
                    group(i, False)

                with act.Fori(0, ROUNDS // 2) as i:
                    for h in range(2):
                        act.wait_ge(rstd_done, 1)
                        act.wait_ge(hist_mm, i * 2 + (h + 1))
                        act.copy(counts[:, bass.ds(i * (2 * J) + h * J, J), :], psW[:, h, 0:2 * J].rearrange("p (j s) -> p j s", s=2)).then_inc(hist_out, 1)

            @block.tensor
            def _(pe):
                pe.wait_ge(consts, 11)

                def turn_tile(i, j, first):
                    pe.wait_ge(normed, i * G + (j + 1))
                    if not (first and j == 0) and j != 1:
                        pe.wait_ge(xT_set, i * G + max(j - 1, 0))
                    for c in range(KC):
                        last = pe.transpose(psN[:, j % 2, c * P:(c + 1) * P],
                                            xn[:, j % 3, c * P:(c + 1) * P], ident[:])
                    last.then_inc(turned, 1)

                def mm_tile(i, j, first):
                    pe.wait_ge(xT_set, i * G + (j + 1))
                    if not (first and j == 0) and j != 1:
                        pe.wait_ge(mm_out, i * G + max(j - 1, 0))
                    for q, k in enumerate((3, 2)):
                        for c in range(KC):
                            last = pe.matmul(psW[:, j % 2, q * D:(q + 1) * D], xT[:, j, c * P:(c + 1) * P], wk[:, k, c, :],
                                             start=(c == 0), stop=(c == KC - 1))
                    last.then_inc(mm_done, 1)

                def group(i, first):
                    turn_tile(i, 0, first)
                    for j in range(G):
                        if j + 1 < G:
                            turn_tile(i, j + 1, first)
                        mm_tile(i, j, first)

                def sort_level(k):
                    for way in range(2):
                        pe.wait_ge(level_sorted, 2 * (k - 1) + way + 1)
                        for b in range(SB):
                            last = pe.transpose(psS[:, b // 4, (b % 4) * P:(b % 4 + 1) * P],
                                                keys[source[k, way]][:, b * P:(b + 1) * P], ident[:])
                            if b % 4 == 3:
                                last.then_inc(sort_T, 1)

                pe.wait_ge(wk_in, 16 * 5)
                group(0, True)
                with pe.Fori(1, MEET) as i:
                    group(i, False)
                for k in range(1, 8):
                    sort_level(k)
                    if MEET + k - 1 < G:
                        group(MEET + k - 1, False)

                for q, quant in enumerate((rowf, colf, selff, None)):
                    ps = (psS, psI)[q % 2]
                    if q >= 2:
                        pe.wait_ge(item_out, q - 1)
                    for b in range(SB):
                        if q == 0:
                            pe.wait_ge(quant_ready, b + 1)
                        lhs = chunk1[:, b, :] if quant is None else quant[:, b * P:(b + 1) * P]
                        for h in range(2):
                            last = pe.matmul(ps[:, h, 0:HALF], lhs, picks[:, b, h * HALF:(h + 1) * HALF],
                                             start=(b == 0), stop=(b == SB - 1))
                    last.then_inc(item_sum, 1)
                pe.wait_ge(tw_ready, 1)
                for q in range(WB):
                    last = pe.matmul(psM[:, q:q + 1], twf[:, q * P:(q + 1) * P], ident[:, 0:1], start=True, stop=True)
                last.then_inc(twT_done, 1)

                def count_round(i, h, first):
                    pe.wait_ge(hot_ready, i * 2 + (h + 1))
                    if first:
                        pe.wait_ge(mm_out, TILES)
                    else:
                        pe.wait_ge(hist_out, i * 2 + (h - 1))
                    for j in range(J):
                        last = pe.matmul(psW[:, h, 2 * j:2 * j + 2], hot[:, h, :, j],
                                         pairs[:, bass.ds(i * (2 * J) + (h * J + j), 1), :].rearrange("p a s -> p (a s)"), start=True, stop=True)
                    last.then_inc(hist_mm, 1)
                for h in range(2):
                    count_round(0, h, True)
                with pe.Fori(1, ROUNDS // 2) as i:
                    for h in range(2):
                        count_round(i, h, False)
                pe.wait_ge(hist_out, ROUNDS)
                pe.wait_ge(item_out, 4)
                for m in range(2 * WB):
                    ps = psS if m < 8 else psI
                    last = pe.transpose(ps[:, m % 8 // 4, m % 4 * P:(m % 4 + 1) * P], counts[:, m // 2 * P:(m // 2 + 1) * P, m % 2], ident[:])
                last.then_inc(cnt_turned, 1)
                pe.wait_ge(cnt_set, 1)
                for s in range(2):
                    for q in range(WB):
                        last = pe.matmul(psM[:, s * P:s * P + EXT], countsT[:, 2 * q + s, :], tile_hot[:, q, :],
                                         start=(q == 0), stop=(q == WB - 1))
                pe.matmul(psM[:, 2 * P:2 * P + EXT], ones[:], spanned[:].rearrange("p s t -> p (s t)"), start=True, stop=True)
                last = pe.matmul(psM[:, 3 * P:3 * P + 1], ones[:], repeats[:], start=True, stop=True)
                last.then_inc(deg_done, 1)

            @block.vector
            def _(dve):
                count = [0]

                def step(ins):
                    count[0] += 1
                    ins.then_inc(seq, 1)

                def settle():
                    dve.wait_ge(seq, count[0])

                dve.wait_ge(edges_in, 32)
                dve.wait_ge(consts, 11)
                e_row, e_col = edges[:, 0, :], edges[:, 1, :]
                step(dve.tensor_scalar(klass, e_col, float(HOTS * P), float(NP), ALU.is_lt, ALU.mult))
                settle()
                step(dve.tensor_tensor(e_row, e_row, klass, ALU.add))
                settle()
                step(dve.tensor_scalar(e_row, e_row, COLBITS, NORMAL, ALU.logical_shift_left, ALU.bitwise_or))
                step(dve.tensor_scalar(part_i[:], part_i[:], 1, None, ALU.bitwise_and))
                settle()
                step(dve.tensor_tensor(keys[0][:].bitcast(I32), e_row, e_col, ALU.bitwise_or))
                step(dve.tensor_copy(sign0[:], part_i[:]))
                step(dve.tensor_scalar(bits[:], lane_i[:], 1, None, ALU.logical_shift_right))
                settle()
                step(dve.tensor_scalar(sign0[:], sign0[:], -2.0, 1.0, ALU.mult, ALU.add))
                step(dve.tensor_tensor(gray[:], lane_i[:], bits[:], ALU.bitwise_xor))
                settle()
                for k in range(7):
                    step(dve.tensor_scalar(bits[:], gray[:], k, 1, ALU.logical_shift_right, ALU.bitwise_and))
                    settle()
                    step(dve.tensor_copy(bitsf[:], bits[:]))
                    settle()
                    step(dve.tensor_scalar(turn[:, k, :], bitsf[:], -2.0, 1.0, ALU.mult, ALU.add))
                    settle()
                step(dve.tensor_scalar(keys[1][:], keys[0][:], sign0[:, 0:1], None, ALU.mult))

                buf = 1

                def compare(dist, flip):
                    nonlocal buf
                    a = keys[buf][:].rearrange("p (n two d) -> p n two d", two=2, d=dist)
                    o = keys[1 - buf][:].rearrange("p (n two d) -> p n two d", two=2, d=dist)
                    hi = a[:, :, 1, ::-1] if flip else a[:, :, 1, :]
                    settle()
                    step(dve.tensor_tensor(o[:, :, 0, :], a[:, :, 0, :], hi, ALU.min))
                    step(dve.tensor_tensor(o[:, :, 1, :], a[:, :, 0, :], hi, ALU.max))
                    buf = 1 - buf

                def level(k):
                    compare(1 << k, flip=k > 0)
                    for d in reversed(range(k)):
                        compare(1 << d, flip=False)
                for k in range(EARLY):
                    level(k)
                for g in range(G):
                    dve.wait_ge(x_in[g], 16)
                with dve.Fori(0, TILES) as t:
                    dve.bn_stats(stats[:, bass.ds(t, 1), :].rearrange("p a f -> p (a f)"),
                                 bufA[:, bass.ds(t, 1), 0:D].rearrange("p a f -> p (a f)")).then_inc(ln_seq, 1)
                dve.wait_ge(ln_seq, TILES)
                moments(dve, stats, mean, var, ln_seq, TILES)
                for k in range(EARLY, 10):
                    level(k)
                moves = 0
                for k in range(1, 8):
                    for way in range(2):
                        settle()
                        dve.sem_inc(level_sorted, 1)
                        assert source[k, way] == buf
                        for h in range(2):
                            moves += 1
                            dve.wait_ge(sort_T, moves)
                            o = keys[1 - buf][:, h * 512:(h + 1) * 512]
                            if way == 0:
                                step(dve.tensor_tensor(o.rearrange("p (b l) -> p b l", l=P), psS[:, h, :].rearrange("p (b l) -> p b l", l=P),
                                                       turn[:, k - 1:k, :].to_broadcast([P, 4, P]), ALU.mult))
                            else:
                                step(dve.tensor_copy(o, psS[:, h, :]))
                        buf = 1 - buf
                        for d in reversed(range(k if way == 0 else 10)):
                            compare(1 << d, flip=False)
                settle()
                step(dve.tensor_scalar(edges[:, 0, :], srt, COLBITS, ROWMASK, ALU.logical_shift_right, ALU.bitwise_and))
                step(dve.tensor_scalar(edges[:, 1, :], srt, COLMASK, None, ALU.bitwise_and))
                settle()
                blocks = edges[:, 0, :].rearrange("p (b l) -> p b l", l=P)
                step(dve.tensor_scalar(lohi_i[:, 0, :], blocks[:, :, 0], 7, None, ALU.logical_shift_right))
                step(dve.tensor_scalar(lohi_i[:, 1, :], blocks[:, :, P - 1], 7, None, ALU.logical_shift_right))
                step(dve.tensor_copy(rowf[:], edges[:, 0, :]))
                step(dve.tensor_tensor(klass[:, 0:SN - P], keys[at][:, 0:SN - P], keys[at][:, P:SN], ALU.is_equal))
                settle()
                step(dve.scalar_tensor_tensor(klass[:, 0:SN - P], edges[:, 0, 0:SN - P], float(2 * NP - 1), klass[:, 0:SN - P], ALU.is_lt, ALU.mult))
                settle()
                step(dve.tensor_reduce(repeats[:], klass[:, 0:SN - P], AX, ALU.max))
                step(dve.tensor_copy(colf[:], edges[:, 1, :]))
                settle()
                step(dve.tensor_copy(lohi[:], lohi_i[:]))
                step(dve.tensor_scalar(selff, rowf[:], float(NP), -float(NP), ALU.is_ge, ALU.mult))
                settle()
                step(dve.tensor_tensor(selff, selff, rowf[:], ALU.add))
                for q, op in enumerate((ALU.is_gt, ALU.is_ge)):
                    step(dve.tensor_tensor(spans[:, q], hot_tile[:].unsqueeze(2).to_broadcast([P, TILES, SB]),
                                           lohi[:, 1 - q, :].unsqueeze(1).to_broadcast([P, TILES, SB]), op))
                settle()
                step(dve.tensor_tensor(selff, selff, colf[:], ALU.is_equal))
                step(dve.tensor_reduce(spanned[:], spans[:], AX, ALU.add))
                settle()
                for s in range(2):
                    step(dve.tensor_tensor(lohi[:, s, :], lohi[:, s, :], chunk[:], ALU.add))
                settle()
                step(dve.scalar_tensor_tensor(rowf[:], chunk1[:].rearrange("p b l -> p (b l)"), float(P), rowf[:], ALU.mult, ALU.add))
                for j in range(G):
                    dve.wait_ge(xT_out[j], 16 * G)
                dve.wait_ge(mm_out, TILES)
                for b in range(SB):
                    step(dve.tensor_scalar(tmp[:], iw[:], lohi[:, 0, b:b + 1], None, ALU.is_ge))
                    settle()
                    step(dve.scalar_tensor_tensor(picks[:, b, :], iw[:], lohi[:, 1, b:b + 1], tmp[:], ALU.is_le, ALU.mult))
                    settle()
                    dve.sem_inc(quant_ready, 1)
                step(dve.memset(rel[:, ITEMS:ITEMS + AHEAD], -1.0))
                if ITEMS < WB * P:
                    step(dve.memset(twf[:, ITEMS:WB * P], -1.0))
                for t in (rel1, colh, tileh):
                    step(dve.memset(t[:, ITEMS:ITEMS + WIN], 0.0))
                step(dve.tensor_scalar(tmp[:], iw[:], float(P), float(P), ALU.mult, ALU.add))
                settle()

                def halves(t):
                    return t[:, 0:ITEMS].rearrange("p (h w) -> p h w", h=2)
                dve.wait_ge(item_sum, 1)
                dve.tensor_tensor(halves(rel), psS[:, :, 0:HALF], halves(tmp), ALU.subtract).then_inc(item_out, 1)
                dve.wait_ge(item_sum, 2)
                dve.tensor_copy(halves(col), psI[:, :, 0:HALF]).then_inc(item_out, 1)
                dve.wait_ge(item_out, 2)
                step(dve.tensor_copy(relb[:], rel[:, 0:ITEMS]))
                dve.wait_ge(item_sum, 3)
                dve.tensor_copy(pairs[:, :, 1].rearrange("p (h w) -> p h w", h=2), psS[:, :, 0:HALF]).then_inc(item_out, 1)
                dve.wait_ge(item_sum, 4)
                dve.scalar_tensor_tensor(halves(tmp), halves(iw), 1.0, psI[:, :, 0:HALF], ALU.add, ALU.subtract).then_inc(item_out, 1)
                dve.wait_ge(item_out, 4)
                step(dve.tensor_scalar(twf[:, 0:ITEMS], tmp[:], float(EXT - 1), None, ALU.min))
                if ITEMS < WB * P:
                    step(dve.memset(counts[:, ITEMS:WB * P, :], 0.0))
                settle()
                dve.sem_inc(tw_ready, 1)

                def hot_round(i, h, first):
                    if not first:
                        dve.wait_ge(hist_mm, i * 2 + (h - 1))
                    dve.tensor_tensor(hot[:, h, :, :], lanes2[:],
                                      relb[:, bass.ds(i * (2 * J) + h * J, J)].unsqueeze(1).to_broadcast([P, P, J]),
                                      ALU.is_equal).then_inc(hot_ready, 1)
                for h in range(2):
                    hot_round(0, h, True)
                with dve.Fori(1, ROUNDS // 2) as i:
                    for h in range(2):
                        hot_round(i, h, False)
                dve.wait_ge(twT_done, 1)
                for q in range(WB):
                    step(dve.tensor_scalar(tile_hot[:, q, :], lanes[:, 0:EXT], psM[:, q:q + 1], None, ALU.is_equal))
                dve.wait_ge(cnt_turned, 1)
                step(dve.tensor_copy(countsT[:, 0:8, :], psS[:].rearrange("p h (m r) -> p (h m) r", r=P)))
                step(dve.tensor_copy(countsT[:, 8:2 * WB, :], psI[:].rearrange("p h (m r) -> p (h m) r", r=P)[:, 0:2 * WB - 8, :]))
                settle()
                dve.sem_inc(cnt_set, 1)
                dve.wait_ge(deg_done, 1)
                step(dve.tensor_scalar(deg[:], psM[:, 0:TILES], 1.0, None, ALU.add))
                settle()
                dve.tensor_tensor(deg[:], deg[:], psM[:, TILES:EXT], ALU.add).then_inc(deg_set, 1)
                step(dve.tensor_scalar(rel1[:, 0:ITEMS], rel[:, 0:ITEMS], 1.0, 0.0, ALU.add, ALU.max))
                step(dve.tensor_copy(colh[:, 0:ITEMS], col[:]))
                step(dve.tensor_copy(tileh[:, 0:ITEMS], twf[:, 0:ITEMS]))
                step(dve.tensor_tensor(first_item[:], psM[0:1, 2 * P:2 * P + TILES], hot_tile[0:1, :], ALU.add))
                step(dve.tensor_scalar(spanned[:, 1, :], psM[:, 2 * P + TILES:2 * P + EXT], float(CHUNKS), None, ALU.min))
                settle()
                step(dve.tensor_tensor(spanned[:, 1, :], spanned[:, 1, :], psM[:, 2 * P:2 * P + TILES], ALU.subtract))
                cold, late = pick[:, 0:ITEMS], pick[:, ITEMS:2 * ITEMS]
                step(dve.scalar_tensor_tensor(cold, twf[:, 0:ITEMS], float(TILES), iw[:], ALU.is_lt, ALU.mult))
                step(dve.scalar_tensor_tensor(late, twf[:, 0:ITEMS], -float(FJ), iw[:], ALU.mult, ALU.add))
                settle()
                step(dve.scalar_tensor_tensor(late, twf[:, 0:ITEMS], float(TILES), late, ALU.is_lt, ALU.mult))
                settle()
                step(dve.tensor_reduce(excess[:, 0:1], spanned[:, 1, :], AX, ALU.max))
                step(dve.tensor_reduce(excess[:, 1:2], cold, AX, ALU.max))
                step(dve.tensor_reduce(excess[:, 2:3], late, AX, ALU.max))
                step(dve.tensor_copy(excess[:, 3:4], psM[:, 3 * P:3 * P + 1]))
                settle()
                for q, most_held in enumerate((WIN, FJ * FROUNDS - 1, LAG * FJ + READ - 1, 0)):
                    step(dve.tensor_scalar(excess[:, q:q + 1], excess[:, q:q + 1], float(most_held), None, ALU.is_gt))
                settle()
                step(dve.tensor_reduce(repeats[:], excess[:], AX, ALU.max))
                step(dve.tensor_scalar(tmp[:], twf[:, 0:ITEMS], float(TILES), -float(TILES), ALU.is_ge, ALU.mult))
                settle()
                step(dve.tensor_scalar(fits[:], repeats[0:1, :], 0.5, None, ALU.is_lt))
                step(dve.tensor_tensor(tile_of[:], tmp[0:1, :], twf[0:1, 0:ITEMS], ALU.add))
                dve.wait_ge(dis_done, 1)
                step(dve.tensor_tensor(sc2[:], dis[:], dis[:], ALU.mult))
                settle()
                step(dve.scalar_tensor_tensor(sc1[:], psM[:, P:P + TILES], 1.0, sc2[:], ALU.add, ALU.subtract))
                settle()
                step(dve.tensor_tensor(sc1[:], sc1[:], psM[:, P + TILES:P + EXT], ALU.add))
                settle()
                step(dve.tensor_scalar(sc2[:], sc1[:], 2.0, None, ALU.mult))
                step(dve.tensor_scalar(nd1[:], dis[:], -1.0, None, ALU.mult))
                step(dve.tensor_scalar(nd2[:], dis[:], -2.0, None, ALU.mult))
                settle()

        path = nc.values_load_multi_w_load_instructions(
            fits[0:1, 0:1], engines=[DVE, PEE, mybir.EngineType.Activation, mybir.EngineType.Pool, mybir.EngineType.SP],
            min_val=0, max_val=1, skip_runtime_bounds_check_because=BOUNDED)[1][0]
        with ExitStack() as s2:
            bufC = sb(s2, "bufC", [P, TILES, D])
            gath = sb(s2, "gath", [P, J, D])
            idx = sb(s2, "idx", [P, J], U32)
            hot = sb(s2, "hot_r", [P, AHEAD, P])
            xnT = sb(s2, "xnT_s", [P, D])
            xr = sb(s2, "xr", [P, D])
            empty = sb(s2, "empty", [P, ROW])
            ct = sb(s2, "ct", [P, HOTS * P], BF16)
            uh = sb(s2, "uh", [P, HOTS, 3, D], BF16)
            rest = gath[:, FJ:FJ + HOTS, :]
            relm = sb(s2, "relm", [P, WIN], F16)
            rowhot = sb(s2, "rowhot", [P, WIN // 2, P, 2], F16)
            cols2 = sb(s2, "cols2", [P, HOTS * P, 2], F16)
            rows2 = xr[:, 0:P].bitcast(F16).rearrange("p (r b) -> p r b", b=2)
            colhot = [part.rearrange("p (a c b) -> p a c b", a=WIN // 4, b=2) for part in (
                gath[:, FJ:J, :].rearrange("p j f -> p (j f)").bitcast(F16), wk[:, 2:4].rearrange("p k c o -> p (k c o)").bitcast(F16))]
            assert FJ + HOTS <= J and WIN * HOTS * P == 4 * (J - FJ) * D
            stat2, mv2, rstd2 = xr[:, 0:6], xr[:, 6:8], xr[:, 8:10]
            psP = pb(s2, "psP", [P, AHEAD, 512])
            psX = pb(s2, "psX", [P, 512])
            psH2 = pb(s2, "psH2", [P, 2, 512])
            psO2 = pb(s2, "psO2", [P, 512])

            PASSES = ((2, bufB, bufA, bufC, bufC, sc2, nd2),
                      (1, bufC, bufB, bufA, bufA, sc2, nd2),
                      (0, bufA, bufC, None, bufB, sc1, nd1))
            u_set = sem("u_set")
            u_first = sem("u_first")
            next_out = sem("next_out")
            landed = [sem(f"landed{j}") for j in range(J)]
            gathering = sem("gathering")
            idx_set, hot_set, item_mm, item_added = sem("idx_set"), sem("hot_set"), sem("item_mm"), sem("item_added")
            xnT_load, xr_load = sem("xnT_load"), sem("xr_load")
            next_mm, next_diff, next_set = sem("next_mm"), sem("next_diff"), sem("next_set")
            folded = sem("folded")
            branched = sem("branched")
            block_consts, masked, relm_set, blk_hot, blk_mm, blk_out = (sem(a) for a in ("block_consts", "masked", "relm_set", "blk_hot", "blk_mm", "blk_out"))
            blk_stored, u_first_odd = sem("blk_stored"), sem("u_first_odd")
            first_out, uh_set, ct_in, dense_mm, dense_added = sem("first_out"), sem("uh_set"), sem("ct_in"), sem("dense_mm"), sem("dense_added")
            again_set, again_out = sem("again_set"), sem("again_out")
            empty_set, empty_out = sem("empty_set"), sem("empty_out")
            ffn_in, norm_consts = sem("ffn_in"), sem("norm_consts")
            stat_set, stat_seen, mv_set, eps_set, rstd_set = (sem(f"{a}_2") for a in ("stat_set", "stat_seen", "mv_set", "eps_set", "rstd_set"))
            z_set, turned, zT_set, hid, gelus, tails, outs = (sem(f"{a}_2") for a in ("z_set", "turned", "zT_set", "hid", "gelus", "tails", "outs"))

            def tile(buf, t):
                return buf[:, bass.ds(t, 1), 0:D].rearrange("p a f -> p (a f)")

            def over_rounds(engine, rounds, lags, body):
                marks = sorted({0, 1, 2, rounds - 1, rounds, max(lags) + 1} | {lag for lag in lags} | {TILES + lag for lag in lags})
                for a, b in zip(marks, marks[1:]):
                    has = {lag: lag <= a < TILES + lag for lag in lags}
                    has["items"], has["next"] = a < rounds, a < rounds - 1
                    if b - a < 3 or a >= rounds:
                        for i in range(a, b):
                            body(i, has, i == 0)
                    else:
                        with engine.Fori(a, b) as i:
                            body(i, has, False)
            COLS_AT, COUNT_AT, DENSE_AT_0, DENSE_AT = (2, 4), (7, 10), (3, 5), (10, 11)
            BY_ACT = (G + 1) // 2
            TABLE = LAG + 1
            WHOLE, NORM, HIDDEN, GATE = LAG, LAG + 1, LAG + 2, LAG + 3

            def sparse(fast):
                width, rounds = (FJ, FROUNDS) if fast else (J, ROUNDS)
                count = width * rounds
                for n, (k, acc, prev, nxt, staging, factor, minus) in enumerate(PASSES):
                    last_pass = nxt is None
                    DENSE = 1 if fast and n == 0 else 0
                    lags = (0,) if not fast else (0, WHOLE, NORM, HIDDEN, GATE) if last_pass else (0, DENSE, TABLE)
                    next_table = None if last_pass else PASSES[n + 1][4]

                    def items_before(i, j):
                        return min(i * width + j, count) + n * count if isinstance(i, int) else i * width + (n * count + j)

                    with nc.Block() as block:

                        @block.sync
                        def _(sp):
                            if n == 0:
                                sp.wait_ge(empty_set, 2)
                                sp.dma_start(placed.rearrange("(t p) f -> p t f", p=P),
                                             empty[:].unsqueeze(1).to_broadcast([P, ETILES, ROW])).then_inc(empty_out, 16)
                                for q in range(G):
                                    g = q // 2 if q % 2 == 0 else BY_ACT + q // 2
                                    sp.wait_ge(u_first if q % 2 == 0 else u_first_odd, (q // 2 + 1) * G)
                                    sp.dma_start(table[0][g * G * P:(g + 1) * G * P, :].rearrange("(t p) f -> p t f", p=P),
                                                 staging[:, g * G:(g + 1) * G, 0:D]).then_inc(first_out, 16)
                            if last_pass:
                                if fast:
                                    sp.wait_ge(uh_set, 5 * (n + 1))
                                sp.dma_start(w1_s, w1.rearrange("(c f) h -> f c h", f=P)).then_inc(ffn_in, 16)
                                sp.dma_start(b1_s[:, 0, :], b1.rearrange("(c h) -> h c", h=P), allow_slow_non_contiguous=True).then_inc(ffn_in, 16)
                                sp.dma_start(wg_s, wg.rearrange("(c h) e -> h c e", h=P)).then_inc(ffn_in, 16)
                                sp.dma_start(bg_s[0:1, 0, :], bg.rearrange("(a e) -> a e", a=1)).then_inc(ffn_in, 16)

                            def per_round(i, has, first):
                                if has[0] and fast and n > 0:
                                    sp.wait_ge(dense_mm, i + n * TILES)
                                    sp.dma_start(ct[:], ct_d[bass.ds(i, 1)].rearrange("a p f -> p (a f)")).then_inc(ct_in, 16)
                                if has[0] and not last_pass:
                                    if not (first and n == 0):
                                        sp.wait_ge(next_set, i + n * TILES)
                                    sp.dma_start(xnT[:], xnT_d[bass.ds(i, 1)].rearrange("a p f -> p (a f)")).then_inc(xnT_load, 16)
                                    if k == 1:
                                        sp.dma_start(xr[:], x[bass.ds(i * P, P), :]).then_inc(xr_load, 16)
                                if has[0] and fast and n == 0:
                                    sp.wait_ge(blk_out, i + 1)
                                    sp.dma_start(ct_d[bass.ds(i, 1)].rearrange("a p f -> p (a f)"), ct[:]).then_inc(blk_stored, 16)
                                if has.get(TABLE) and not last_pass:
                                    sp.wait_ge(u_set, i + (n * TILES - TABLE + 1))
                                    sp.dma_start(table[n + 1][bass.ds((i - TABLE) * P, P), :], tile(next_table, i - TABLE)).then_inc(next_out, 16)
                            over_rounds(sp, rounds, lags, per_round)
                            if fast and not last_pass:
                                sp.wait_ge(next_out, (n + 1) * TILES * 16)
                            if n == 0:
                                sp.wait_ge(empty_out, 16)

                        @block.gpsimd
                        def _(pool):
                            if n == 0:
                                pool.memset(empty[:], 0.0).then_inc(empty_set, 1)
                                pool.wait_ge(empty_set, 1)
                                pool.memset(empty[:].bitcast(I32)[:, D + 1:D + 2], NP).then_inc(empty_set, 1)
                                if fast:
                                    pool.iota(cols2[:], [[1, HOTS * P], [0, 2]], base=0, channel_multiplier=0, allow_small_or_imprecise_dtypes=True).then_inc(block_consts, 1)
                                    pool.iota(rows2, [[1, P], [0, 2]], base=1, channel_multiplier=0, allow_small_or_imprecise_dtypes=True).then_inc(block_consts, 1)
                                pool.wait_ge(first_out, 16 * G)
                            if last_pass:
                                pool.memset(eps, EPS).then_inc(norm_consts, 1)
                                pool.memset(minus_half, -0.5).then_inc(norm_consts, 1)
                                pool.wait_ge(norm_consts, 2)

                            def per_round(i, has, first):
                                for j in range(width):
                                    if last_pass and has.get(NORM) and j == width // 2:
                                        pool.wait_ge(mv_set, i - NORM + 1)
                                        pool.tensor_tensor(rstd2[:, 1:2], rstd2[:, 0:1], minus_half[:, 0, :], ALU.pow).then_inc(rstd_set, 1)
                                    if not has["items"]:
                                        continue
                                    if j % (width // PARTS) == 0:
                                        pool.wait_ge(idx_set, i * PARTS + (n * PARTS * rounds + j // (width // PARTS) + 1))
                                        pool.sem_inc(gathering, 1)
                                    pool.indirect_dma_start(out=gath[:, j, :], out_offset=None, in_=table[n],
                                                            in_offset=bass.IndirectOffsetOnAxis(ap=idx[:, j:j + 1], axis=0)).then_inc(landed[j], 16)
                            over_rounds(pool, rounds, lags, per_round)

                        @block.scalar
                        def _(act):
                            if n == 0:
                                with act.Fori(0, BY_ACT * G) as t:
                                    act.mul(tile(staging, t), tile(bufA, t), dis[:, bass.ds(t, 1)]).then_inc(u_first, 1)

                            def gelu(i, h):
                                if not (isinstance(i, int) and i == GATE):
                                    act.wait_ge(tails, i - GATE)
                                act.wait_ge(hid, (i - GATE) * 2 + (h + 1))
                                for q in range(HC // 2):
                                    hc = h * (HC // 2) + q
                                    last = act.activation(hT[:, 0, hc, :], psH2[:, h, q * P:(q + 1) * P], ACT.Gelu, bias=b1_s[:, 0, hc:hc + 1])
                                last.then_inc(gelus, 1)

                            def per_round(i, has, first):
                                if last_pass and has.get(GATE):
                                    gelu(i, 0)
                                    gelu(i, 1)
                                if not last_pass and has.get(TABLE):
                                    act.wait_ge(empty_set, 1)
                                    act.wait_ge(item_added, items_before(i, 0))
                                    act.mul(tile(next_table, i - TABLE), tile(acc, i - TABLE), dis[:, bass.ds(i - TABLE, 1)]).then_inc(u_set, 1)
                                if fast and n == 0 and has[0]:
                                    if not first:
                                        act.wait_ge(blk_stored, i * 16)
                                        act.wait_ge(dense_mm, i)
                                    act.wait_ge(blk_mm, i + 1)
                                    act.copy(ct[:], psH2[:, 0, :]).then_inc(blk_out, 1)
                            if last_pass:
                                act.wait_ge(ffn_in, 64)
                            over_rounds(act, rounds, lags, per_round)

                        @block.vector
                        def _(dve):
                            dve.wait_ge(empty_set, 1)

                            def one_hot(i, j):
                                dve.tensor_scalar(hot[:, j % AHEAD, :], lanes[:], rel[:, bass.ds(i * width + j, 1)], None, ALU.is_equal).then_inc(hot_set, 1)

                            def refresh(i, h):
                                c = h * (width // PARTS)
                                dve.tensor_copy(idx[:, c:c + width // PARTS], col[:, bass.ds(i * width + c, width // PARTS)]).then_inc(idx_set, 1)

                            def block_rows(i, w, first):
                                dve.scalar_tensor_tensor(out=relm[:], in0=tileh[:, bass.ds(w, WIN)], scalar=hot_tile[:, bass.ds(i, 1)],
                                                         in1=rel1[:, bass.ds(w, WIN)], op0=ALU.is_equal, op1=ALU.mult).then_inc(relm_set, 1)
                                if not first:
                                    dve.wait_ge(blk_mm, i)
                                dve.wait_ge(relm_set, i + 1)
                                dve.tensor_tensor(rowhot[:], rows2.unsqueeze(1).to_broadcast([P, WIN // 2, P, 2]),
                                                  relm[:].rearrange("p (a b) -> p a b", b=2).unsqueeze(2).to_broadcast([P, WIN // 2, P, 2]),
                                                  ALU.is_equal).then_inc(blk_hot, 1)

                            def block_cols(i, w, h):
                                cols = colh[:, bass.ds(w + h * (WIN // 2), WIN // 2)].rearrange("p (a b) -> p a b", b=2)
                                dve.tensor_tensor(colhot[h], cols2[:].unsqueeze(1).to_broadcast([P, WIN // 4, HOTS * P, 2]),
                                                  cols.unsqueeze(2).to_broadcast([P, WIN // 4, HOTS * P, 2]), ALU.is_equal).then_inc(blk_hot, 1)

                            def add_item(i, j, t, first):
                                if not (first and n == 0 and j == 0):
                                    dve.wait_ge(item_added, i * width + (n * count + j))
                                dve.wait_ge(item_mm, i * width + (n * count + j + 1))
                                dve.scalar_tensor_tensor(out=tile(acc, t), in0=psP[:, j % AHEAD, 0:D], scalar=minus[:, bass.ds(t, 1)],
                                                         in1=tile(acc, t), op0=ALU.mult, op1=ALU.add).then_inc(item_added, 1)

                            def split_hot():
                                done = 5 * n
                                for part in range(3):
                                    whole_part = staging[:, 0:HOTS, 0:D] if part == 0 else rest
                                    dve.tensor_copy(uh[:, :, part, :], whole_part).then_inc(uh_set, 1)
                                    done += 1
                                    dve.wait_ge(uh_set, done)
                                    if part < 2:
                                        dve.tensor_tensor(rest, whole_part, uh[:, :, part, :], ALU.subtract).then_inc(uh_set, 1)
                                        done += 1
                                        dve.wait_ge(uh_set, done)

                            def fold(i):
                                t = i - DENSE
                                dve.wait_ge(item_added, items_before(i, width))
                                if fast:
                                    dve.wait_ge(dense_mm, t + (n * TILES + 1))
                                    dve.scalar_tensor_tensor(out=tile(acc, t), in0=psO2[:, 0:D], scalar=minus[:, bass.ds(t, 1)], in1=tile(acc, t),
                                                             op0=ALU.mult, op1=ALU.add).then_inc(dense_added, 1)
                                    dve.wait_ge(dense_added, t + (n * TILES + 1))
                                dve.scalar_tensor_tensor(out=tile(acc, t), in0=tile(prev, t), scalar=factor[:, bass.ds(t, 1)], in1=tile(acc, t),
                                                         op0=ALU.mult, op1=ALU.add).then_inc(folded, 1)

                            def prepare(t):
                                dve.wait_ge(next_mm, t + (n * TILES + 1))
                                if k == 2:
                                    dve.tensor_tensor(tile(nxt, t), psX[:, 0:D], tile(prev, t), ALU.subtract).then_inc(next_set, 1)
                                else:
                                    dve.tensor_tensor(tile(nxt, t), psX[:, 0:D], tile(prev, t), ALU.subtract).then_inc(next_diff, 1)
                                    dve.wait_ge(next_diff, t + 1)
                                    dve.wait_ge(xr_load, (t + 1) * 16)
                                    dve.tensor_tensor(tile(nxt, t), tile(nxt, t), xr[:], ALU.add).then_inc(next_set, 1)

                            def whole(i):
                                t = i - WHOLE
                                dve.wait_ge(empty_set, 1)
                                dve.wait_ge(item_added, items_before(i, READ))
                                dve.bn_stats(stat2[:], tile(bufA, t)).then_inc(stat_set, 1)
                                if not (isinstance(i, int) and t == 0):
                                    dve.wait_ge(z_set, t)
                                dve.wait_ge(stat_set, t + 1)
                                dve.sem_inc(stat_seen, 1)
                                dve.bn_aggr(mv2[:], stat2[:]).then_inc(eps_set, 1)
                                dve.wait_ge(eps_set, t + 1)
                                dve.tensor_scalar(rstd2[:, 0:1], mv2[:, 1:2], EPS, None, ALU.add).then_inc(mv_set, 1)

                            def norm(i):
                                t = i - NORM
                                if not (isinstance(i, int) and t == 0):
                                    dve.wait_ge(turned, t)
                                dve.wait_ge(item_added, items_before(i, READ - 1))
                                dve.wait_ge(rstd_set, t + 1)
                                dve.tensor_scalar(z[:, 0, :], tile(bufA, t), mv2[:, 0:1], rstd2[:, 1:2], ALU.subtract, ALU.mult).then_inc(z_set, 1)

                            def copy_zT(i):
                                dve.wait_ge(turned, i - HIDDEN + 1)
                                dve.tensor_copy(zT[:, 0, :], psX[:, 0:D]).then_inc(zT_set, 1)

                            def keep_logits(i):
                                dve.wait_ge(empty_set, 1)
                                dve.wait_ge(tails, i - GATE + 1)
                                dve.tensor_copy(logit[:, bass.ds(i - GATE, 1), :].rearrange("p a e -> p (a e)"), psO2[:, 0:NE]).then_inc(outs, 1)

                            def per_round(i, has, first):
                                if has["items"]:
                                    _, ts = nc.values_load_multi_w_load_instructions(
                                        tile_of[0:1, bass.ds(i * width, width)], engines=[DVE], min_val=0, max_val=TILES - 1, skip_runtime_bounds_check_because=BOUNDED)
                                if fast and n == 0 and has[0]:
                                    _, (w,) = nc.values_load_multi_w_load_instructions(
                                        first_item[0:1, bass.ds(i, 1)], engines=[DVE], min_val=0, max_val=ITEMS - 1, skip_runtime_bounds_check_because=BOUNDED)
                                for j in range(width):
                                    if fast and n == 0 and has[0]:
                                        if j == 1:
                                            block_rows(i, w, first)
                                        if j in COLS_AT:
                                            block_cols(i, w, COLS_AT.index(j))
                                    if has["items"]:
                                        if j == 0 and not (isinstance(i, int) and i <= DENSE and n == 0):
                                            dve.wait_ge(folded, i + (n * TILES - DENSE) if has[DENSE] else (n + 1) * TILES)
                                        if j == 0 and not last_pass and has.get(TABLE):
                                            dve.wait_ge(u_set, i + (n * TILES - TABLE + 1))
                                        add_item(i, j, ts[j], first)
                                        one_hot(i, j + AHEAD)
                                        if has["next"] and j % (width // PARTS) == width // PARTS - 1:
                                            refresh(i + 1, j // (width // PARTS))
                                    if last_pass:
                                        if j == 2 and has.get(HIDDEN):
                                            copy_zT(i)
                                        if j == 6 and has.get(GATE):
                                            keep_logits(i)
                                        if j == READ - 2 and has.get(NORM):
                                            norm(i)
                                        if j == READ - 1 and has.get(WHOLE):
                                            whole(i)
                                if has[0] and nxt is not None:
                                    if first and n == 0:
                                        dve.wait_ge(first_out, 16 * G)
                                    prepare(i)
                                if has[DENSE]:
                                    fold(i)
                            if n == 0:
                                with dve.Fori(BY_ACT * G, TILES) as t:
                                    dve.tensor_scalar(tile(staging, t), tile(bufA, t), dis[:, bass.ds(t, 1)], None, ALU.mult).then_inc(u_first_odd, 1)
                            if n == 0 and fast:
                                part = ITEMS // 2
                                assert part <= AHEAD * P
                                scratch = hot[:].rearrange("p j r -> p (j r)")[:, 0:part]
                                for h in range(2):
                                    mine_of = slice(h * part, (h + 1) * part)
                                    dve.tensor_scalar(scratch, tileh[:, mine_of], float(TILES), -4.0 * P, ALU.is_ge, ALU.mult).then_inc(masked, 1)
                                    dve.wait_ge(masked, 2 * h + 1)
                                    dve.tensor_tensor(rel[:, mine_of], rel[:, mine_of], scratch, ALU.add).then_inc(masked, 1)
                                    dve.wait_ge(masked, 2 * h + 2)
                                dve.wait_ge(block_consts, 2)
                                dve.wait_ge(u_first, BY_ACT * G)
                            if n > 0:
                                dve.wait_ge(hot_set, n * (count + AHEAD))
                            for h in range(PARTS):
                                refresh(0, h)
                            for j in range(AHEAD):
                                one_hot(0, j)
                            if fast:
                                split_hot()
                            over_rounds(dve, rounds, lags, per_round)
                            dve.wait_ge(item_added, (n + 1) * count)

                        @block.tensor
                        def _(pe):
                            def item(i, j, first):
                                pe.wait_ge(landed[j], (i + (n * rounds + 1)) * 16)
                                pe.wait_ge(hot_set, i * width + (n * (count + AHEAD) + j + 1))
                                if not (first and n == 0 and j < AHEAD):
                                    pe.wait_ge(item_added, i * width + (n * count + j + 1 - AHEAD))
                                pe.matmul(psP[:, j % AHEAD, 0:D], hot[:, j % AHEAD, :], gath[:, j, :], start=True, stop=True).then_inc(item_mm, 1)

                            def prepare(t, first):
                                pe.wait_ge(xnT_load, (t + (n * TILES + 1)) * 16)
                                if not (first and n == 0):
                                    pe.wait_ge(next_set, t + n * TILES)
                                for c in range(KC):
                                    last = pe.matmul(psX[:, 0:D], xnT[:, c * P:(c + 1) * P], wk[:, k - 1, c, :], start=(c == 0),
                                                     stop=(c == KC - 1 and k == 2))
                                if k == 1:
                                    last = pe.matmul(psX[:, 0:D], ones[0:1, :], gbrow[:], start=False, stop=True)
                                last.then_inc(next_mm, 1)

                            def block_counts(i, half, first):
                                if half == 0:
                                    pe.wait_ge(blk_hot, i * 3 + 3)
                                    if not first:
                                        pe.wait_ge(blk_out, i)
                                for c in range(half * (HOTS // 2), (half + 1) * (HOTS // 2)):
                                    for w in range(WIN):
                                        last = pe.matmul(psH2[:, 0, c * P:(c + 1) * P], colhot[w // (WIN // 2)][:, w // 2 % (WIN // 4), c * P:(c + 1) * P, w % 2],
                                                         rowhot[:, w // 2, :, w % 2], start=(w == 0), stop=(w == WIN - 1))
                                if half == 1:
                                    last.then_inc(blk_mm, 1)

                            def dense(i, half, has):
                                t = i - DENSE
                                if half == 0:
                                    if n == 0:
                                        pe.wait_ge(blk_out, t + 1)
                                    else:
                                        pe.wait_ge(ct_in, (t + ((n - 1) * TILES + 1)) * 16)
                                    if isinstance(i, int) and t == 0:
                                        pe.wait_ge(uh_set, 5 * (n + 1))
                                    if not (isinstance(i, int) and t == 0 and n == 0):
                                        pe.wait_ge(dense_added, t + n * TILES)
                                    if has.get(GATE):
                                        pe.wait_ge(outs, i - GATE + 1)
                                for c in range(half * (HOTS // 2), (half + 1) * (HOTS // 2)):
                                    for part in range(3):
                                        last = pe.matmul(psO2[:, 0:D], ct[:, c * P:(c + 1) * P], uh[:, c, part, :],
                                                         start=(c == 0 and part == 0), stop=(c == HOTS - 1 and part == 2))
                                if half == 1:
                                    last.then_inc(dense_mm, 1)

                            def turn_z(i):
                                t = i - HIDDEN
                                if not (isinstance(i, int) and t == 0):
                                    pe.wait_ge(zT_set, t)
                                pe.wait_ge(z_set, t + 1)
                                for c in range(KC):
                                    last = pe.transpose(psX[:, c * P:(c + 1) * P], z[:, 0, c * P:(c + 1) * P], ident[:])
                                last.then_inc(turned, 1)

                            def hidden(i, h):
                                t = i - HIDDEN
                                if h == 0:
                                    pe.wait_ge(zT_set, t + 1)
                                if not (isinstance(i, int) and t == 0):
                                    pe.wait_ge(gelus, t * 2 - 1 + h)
                                for q in range(HC // 2):
                                    hc = h * (HC // 2) + q
                                    for c in range(KC):
                                        last = pe.matmul(psH2[:, h, q * P:(q + 1) * P], w1_s[:, c, hc * P:(hc + 1) * P], zT[:, 0, c * P:(c + 1) * P],
                                                         start=(c == 0), stop=(c == KC - 1))
                                last.then_inc(hid, 1)

                            def gate(i, has):
                                t = i - GATE
                                if not (isinstance(i, int) and t == 0):
                                    pe.wait_ge(outs, t)
                                pe.wait_ge(dense_added, i + n * TILES if has[0] else (n + 1) * TILES)
                                pe.wait_ge(gelus, t * 2 + 2)
                                for c in range(HC):
                                    pe.matmul(psO2[:, 0:NE], hT[:, 0, c, :], wg_s[:, c, :], start=(c == 0), stop=False)
                                pe.matmul(psO2[:, 0:NE], ones[0:1, :], bg_s[0:1, 0, :], start=False, stop=True).then_inc(tails, 1)

                            def per_round(i, has, first):
                                for j in range(width):
                                    if has["items"]:
                                        item(i, j, first)
                                    if last_pass:
                                        if j == 0 and has.get(HIDDEN):
                                            turn_z(i)
                                        if j == 3 and has.get(GATE):
                                            gate(i, has)
                                        if j == 5 and has.get(HIDDEN):
                                            hidden(i, 0)
                                        if j == 9 and has.get(HIDDEN):
                                            hidden(i, 1)
                                    for half in range(2):
                                        if fast and has[0] and n == 0 and j == COUNT_AT[half]:
                                            block_counts(i, half, first)
                                        if fast and has[DENSE] and j == (DENSE_AT_0 if DENSE else DENSE_AT)[half]:
                                            dense(i, half, has)
                                if has[0] and not last_pass:
                                    prepare(i, first)
                            if last_pass:
                                pe.wait_ge(ffn_in, 64)
                            over_rounds(pe, rounds, lags, per_round)

                    if last_pass:
                        break
                    if fast:
                        continue
                    with nc.Block() as block:

                        @block.scalar
                        def _(act):
                            with act.Fori(0, TILES) as t:
                                act.mul(tile(next_table, t), tile(acc, t), dis[:, bass.ds(t, 1)]).then_inc(again_set, 1)

                        @block.sync
                        def _(sp):
                            sp.wait_ge(again_set, (n + 1) * TILES)
                            sp.dma_start(table[n + 1].rearrange("(t p) f -> p t f", p=P), next_table[:, :, 0:D]).then_inc(again_out, 16)
                            sp.wait_ge(again_out, (n + 1) * 16)

                        @block.gpsimd
                        def _(pool):
                            pool.sem_inc(branched, 1)

                        @block.vector
                        def _(dve):
                            dve.sem_inc(branched, 1)

                        @block.tensor
                        def _(pe):
                            pe.sem_inc(branched, 1)

            with nc.If(path == 1):
                sparse(True)
            with nc.Else():
                sparse(False)
        graph.close()

        ffn = ExitStack()
        wd_s = sb(ffn, "wd_s", [P, NE, HC, D])
        bd_s = sb(ffn, "bd_s", [1, NE, D])
        expert = sb(ffn, "expert", [1, ETILES], I32)
        psT = pb(ffn, "psT", [P, 2, 512])
        psH = pb(ffn, "psH", [P, 2, 2, 512])
        psO = pb(ffn, "psO", [P, 2, 512])
        wd_in = sem("wd_in")

        def ffn_turn(pe, z_set, turned, zT_set):
            def f(n, m, _):
                pe.wait_ge(zT_set, n + 1)
                pe.wait_ge(z_set, n + 1)
                for c in range(KC):
                    last = pe.transpose(psT[:, m % 2, c * P:(c + 1) * P], z[:, m % 4, c * P:(c + 1) * P], ident[:])
                last.then_inc(turned, 1)
            return f

        def ffn_hidden(pe, zT_set, hid, gelus):
            def f(n, m, _):
                pe.wait_ge(zT_set, n + 3)
                for h in range(2):
                    pe.wait_ge(gelus, n * 2 + (h + 1))
                    for q in range(HC // 2):
                        hc = h * (HC // 2) + q
                        for c in range(KC):
                            last = pe.matmul(psH[:, m % 2, h, q * P:(q + 1) * P], w1_s[:, c, hc * P:(hc + 1) * P], zT[:, m % 2, c * P:(c + 1) * P],
                                             start=(c == 0), stop=(c == KC - 1))
                    last.then_inc(hid, 1)
            return f

        def ffn_gelu(act, hid, gelus, tails):
            def f(n, m, _):
                act.wait_ge(tails, n + 1)
                for h in range(2):
                    act.wait_ge(hid, n * 2 + (h + 1))
                    for q in range(HC // 2):
                        hc = h * (HC // 2) + q
                        last = act.activation(hT[:, m % 2, hc, :], psH[:, m % 2, h, q * P:(q + 1) * P], ACT.Gelu, bias=b1_s[:, 0, hc:hc + 1])
                    last.then_inc(gelus, 1)
            return f

        def ffn_zT(dve, turned, zT_set):
            def f(n, m, _):
                dve.wait_ge(turned, n + 1)
                dve.tensor_copy(zT[:, m % 2, :], psT[:, m % 2, 0:D]).then_inc(zT_set, 1)
            return f

        with ExitStack() as s3:
            stats = sb(s3, "stats3", [P, TILES, 6])
            mean = sb(s3, "mean3", [P, TILES])
            var = sb(s3, "var3", [P, TILES])
            rstd = sb(s3, "rstd3", [P, TILES])
            shift = sb(s3, "shift3", [P, TILES])
            ln3, rstd3_seq = sem("ln3"), sem("rstd3_seq")
            z_set, turned, zT_set, hid, gelus, tails, outs = (sem(f"{a}_3") for a in ("z_set", "turned", "zT_set", "hid", "gelus", "tails", "outs"))

            with nc.If(path == 0):
                with nc.Block() as block:

                    @block.sync
                    def _(sp):
                        sp.sem_inc(branched, 1)

                    @block.gpsimd
                    def _(pool):
                        pool.wait_ge(ln3, TILES + MOMENTS)
                        pool.tensor_scalar(rstd[:], var[:], EPS, None, ALU.add).then_inc(rstd3_seq, 1)
                        pool.wait_ge(rstd3_seq, 1)
                        pool.tensor_tensor(rstd[:], rstd[:], minus_half[:, 0, :].to_broadcast([P, TILES]), ALU.pow).then_inc(rstd3_seq, 1)
                        pool.wait_ge(rstd3_seq, 2)
                        pool.tensor_tensor(shift[:], mean[:], rstd[:], ALU.mult).then_inc(rstd3_seq, 1)
                        pool.wait_ge(rstd3_seq, 3)
                        pool.tensor_scalar(shift[:], shift[:], -0.5, None, ALU.mult).then_inc(rstd3_seq, 1)

                    @block.scalar
                    def _(act):
                        act.wait_ge(rstd3_seq, 4)
                        act.sem_inc(gelus, 4)

                        def norm(n, m, _):
                            act.activation(z[:, m % 4, :], bufA[:, bass.ds(n, 1), 0:D].rearrange("p a f -> p (a f)"), ACT.Identity,
                                           bias=shift[:, bass.ds(n, 1)], scale=rstd[:, bass.ds(n, 1)]).then_inc(z_set, 1)
                        in_turn(act, TILES, [(2, norm), (0, ffn_gelu(act, hid, gelus, tails))])

                    @block.vector
                    def _(dve):
                        with dve.Fori(0, TILES) as t:
                            dve.bn_stats(stats[:, bass.ds(t, 1), :].rearrange("p a f -> p (a f)"),
                                         bufA[:, bass.ds(t, 1), 0:D].rearrange("p a f -> p (a f)")).then_inc(ln3, 1)
                        dve.wait_ge(ln3, TILES)
                        moments(dve, stats, mean, var, ln3, TILES)
                        dve.sem_inc(zT_set, 2)
                        dve.sem_inc(outs, 2)

                        def keep_logits(n, m, _):
                            dve.wait_ge(ln3, TILES)
                            dve.wait_ge(tails, n + 3)
                            dve.tensor_copy(logit[:, bass.ds(n, 1), :].rearrange("p a e -> p (a e)"), psO[:, m % 2, 0:NE]).then_inc(outs, 1)
                        in_turn(dve, TILES, [(1, ffn_zT(dve, turned, zT_set)), (-1, keep_logits)])
                        dve.wait_ge(outs, TILES + 2)

                    @block.tensor
                    def _(pe):
                        pe.sem_inc(tails, 2)

                        def gate(n, m, _):
                            pe.wait_ge(gelus, n * 2 + 6)
                            pe.wait_ge(outs, n + 1)
                            for c in range(HC):
                                pe.matmul(psO[:, m % 2, 0:NE], hT[:, m % 2, c, :], wg_s[:, c, :], start=(c == 0), stop=False)
                            pe.matmul(psO[:, m % 2, 0:NE], ones[0:1, :], bg_s[0:1, 0, :], start=False, stop=True).then_inc(tails, 1)
                        in_turn(pe, TILES, [(1, ffn_turn(pe, z_set, turned, zT_set)), (0, ffn_hidden(pe, zT_set, hid, gelus)), (-1, gate)])

            part = sb(s3, "part", [P, 1])
            before = sb(s3, "before", [P, P])
            falling = sb(s3, "falling", [P, NE])
            etile = sb(s3, "etile", [P, ETILES])
            prob = sb(s3, "prob", [P, TILES, NE])
            mine = sb(s3, "mine", [P, TILES, NE])
            most = sb(s3, "most", [P, TILES])
            total = sb(s3, "total", [P, TILES])
            per_tile = sb(s3, "per_tile", [P, NE, TILES])
            upto = sb(s3, "upto", [P, NE, TILES])
            need = sb(s3, "need", [P, NE])
            need_i = sb(s3, "need_i", [P, NE], I32)
            start = sb(s3, "start", [P, NE])
            exf = sb(s3, "exf", [P, ETILES])
            pos = sb(s3, "pos", [P, TILES], U32)
            c3, route, exp_in, exp_out = sem("c3"), sem("route"), sem("exp_in"), sem("exp_out")
            mine_set, ranked, pos_set, scattered = sem("mine_set"), sem("ranked"), sem("pos_set"), sem("scattered")

            block = s3.enter_context(nc.Block())

            @block.sync
            def _(sp):
                sp.dma_start(bd_s[:], bd.rearrange("(a e) o -> a e o", a=1)).then_inc(wd_in, 16)
                for e in range(NE):
                    sp.dma_start(wd_s[:, e, :, :], wd[e].rearrange("(c h) o -> h c o", h=P)).then_inc(wd_in, 16)

            @block.gpsimd
            def _(pool):
                pool.memset(bufA[:, :, D:ROW], 0.0).then_inc(c3, 1)
                pool.iota(part[:], [[0, 1]], base=0, channel_multiplier=1, allow_small_or_imprecise_dtypes=True).then_inc(c3, 1)
                pool.iota(falling[:], [[-1, NE]], base=NE, channel_multiplier=0, allow_small_or_imprecise_dtypes=True).then_inc(c3, 1)
                pool.iota(etile[:], [[1, ETILES]], base=0, channel_multiplier=0, allow_small_or_imprecise_dtypes=True).then_inc(c3, 1)
                pool.wait_ge(c3, 4)
                pool.iota(bufA[:].bitcast(I32)[:, :, D + 1], [[P, TILES]], base=0, channel_multiplier=1).then_inc(c3, 1)
                pool.wait_ge(pos_set, 1)
                for t in range(TILES):
                    pool.indirect_dma_start(out=placed, out_offset=bass.IndirectOffsetOnAxis(ap=pos[:, t:t + 1], axis=0),
                                            in_=bufA[:, t, :], in_offset=None).then_inc(scattered, 16)
                pool.wait_ge(scattered, 16 * TILES)

            @block.scalar
            def _(act):
                act.wait_ge(exp_in, 1)
                act.activation(prob[:], logit, ACT.Exp).then_inc(exp_out, 1)

            @block.vector
            def _(dve):
                dve.wait_ge(c3, 5)

                count = [0]

                def step(ins):
                    count[0] += 1
                    ins.then_inc(route, 1)
                    dve.wait_ge(route, count[0])

                def over_experts(t):
                    return t[:].unsqueeze(2).to_broadcast([P, TILES, NE])
                step(dve.tensor_reduce(most[:], logit, AX, ALU.max))
                step(dve.tensor_tensor(logit, logit, over_experts(most), ALU.subtract))
                dve.sem_inc(exp_in, 1)
                step(dve.tensor_scalar(before[:], lanes[:], part[:, 0:1], None, ALU.is_gt))
                dve.wait_ge(exp_out, 1)
                step(dve.tensor_reduce(total[:], prob[:], AX, ALU.add))
                step(dve.reciprocal(total[:], total[:]))
                step(dve.tensor_tensor(prob[:], prob[:], over_experts(total), ALU.mult))
                step(dve.tensor_reduce(most[:], prob[:], AX, ALU.max))
                step(dve.tensor_copy(bufA[:, :, D], most[:]))
                step(dve.tensor_tensor(mine[:], prob[:], over_experts(most), ALU.is_equal))
                step(dve.tensor_tensor(mine[:], mine[:], falling[:].unsqueeze(1).to_broadcast([P, TILES, NE]), ALU.mult))
                step(dve.tensor_reduce(most[:], mine[:], AX, ALU.max))
                step(dve.tensor_tensor(mine[:], mine[:], over_experts(most), ALU.is_equal))
                dve.sem_inc(mine_set, 1)
                dve.wait_ge(ranked, 1)
                step(dve.tensor_copy(per_tile[:], psO[:, 1, 0:TILES * NE].rearrange("p (t e) -> p e t", e=NE)))
                for e in range(NE):
                    step(dve.tensor_tensor_scan(upto[:, e, :], ones[:, 0:TILES], per_tile[:, e, :], 0.0, ALU.mult, ALU.add))
                step(dve.tensor_scalar(need[:], upto[:, :, TILES - 1], float(P - 1), None, ALU.add))
                step(dve.tensor_copy(need_i[:], need[:]))
                step(dve.tensor_scalar(need_i[:], need_i[:], 7, None, ALU.logical_shift_right))
                step(dve.tensor_copy(need[:], need_i[:]))
                step(dve.tensor_tensor_scan(start[:], ones[:, 0:NE], need[:], 0.0, ALU.mult, ALU.add))
                step(dve.tensor_tensor(start[:], start[:], need[:], ALU.subtract))
                step(dve.tensor_tensor(upto[:], upto[:], per_tile[:], ALU.subtract))
                step(dve.scalar_tensor_tensor(upto[:], start[:].unsqueeze(2).to_broadcast([P, NE, TILES]), float(P), upto[:], ALU.mult, ALU.add))
                step(dve.tensor_tensor(prob[:], psO[:, 0, 0:TILES * NE].rearrange("p (t e) -> p t e", e=NE), upto[:].rearrange("p e t -> p t e"), ALU.add))
                step(dve.tensor_tensor(prob[:], prob[:], mine[:], ALU.mult))
                step(dve.tensor_reduce(most[:], prob[:], AX, ALU.add))
                step(dve.tensor_copy(pos[:], most[:]))
                dve.sem_inc(pos_set, 1)
                step(dve.tensor_scalar(exf[:], etile[:], start[:, 1:2], None, ALU.is_ge))
                for e in range(2, NE):
                    step(dve.scalar_tensor_tensor(exf[:], etile[:], start[:, e:e + 1], exf[:], ALU.is_ge, ALU.add))
                step(dve.tensor_copy(expert[:], exf[0:1, :]))

            @block.tensor
            def _(pe):
                pe.wait_ge(mine_set, 1)
                flat = mine[:].rearrange("p t e -> p (t e)")
                pe.matmul(psO[:, 0, 0:TILES * NE], before[:], flat, start=True, stop=True)
                pe.matmul(psO[:, 1, 0:TILES * NE], ones[:], flat, start=True, stop=True).then_inc(ranked, 1)

        with ExitStack() as s4:
            rows = sb(s4, "rows", [P, UNROLL, ROW])
            result = sb(s4, "result", [P, UNROLL, D])
            stats = sb(s4, "stats4", [P, 4, 6])
            mv = sb(s4, "mv4", [P, 4, 2])
            rstd = sb(s4, "rstd4", [P, 4, 2])

            row_in = [sem(f"row_in{j}") for j in range(UNROLL)]
            row_out = [sem(f"row_out{j}") for j in range(UNROLL)]
            stat4, stat4_seen, mv_set, eps_set, rstd_set, scatters = sem("stat4"), sem("stat4_seen"), sem("mv_set"), sem("eps_set"), sem("rstd_set"), sem("scatters")
            z_set, turned, zT_set, hid, gelus, tails, outs = (sem(f"{a}_4") for a in ("z_set", "turned", "zT_set", "hid", "gelus", "tails", "outs"))

            block = s4.enter_context(nc.Block())

            @block.sync
            def _(sp):
                def load(i, j, first):
                    if not first:
                        sp.wait_ge(row_out[j], i * 16)
                    n = i * UNROLL + j
                    sp.dma_start(rows[:, j, :], placed[bass.ds(n * P, P), :]).then_inc(row_in[j], 16)
                for j in range(UNROLL):
                    load(0, j, True)
                with sp.Fori(1, ETILES // UNROLL) as i:
                    for j in range(UNROLL):
                        load(i, j, False)
                for j in range(UNROLL):
                    sp.wait_ge(row_out[j], 16 * (ETILES // UNROLL))

            @block.gpsimd
            def _(pool):
                def root(n, m, _):
                    pool.wait_ge(mv_set, n + 1)
                    pool.tensor_tensor(rstd[:, m % 4, 0:1], mv[:, m % 4, 1:2], eps[:, 0, :], ALU.add).then_inc(eps_set, 1)
                    pool.wait_ge(eps_set, n + 1)
                    pool.tensor_tensor(rstd[:, m % 4, 1:2], rstd[:, m % 4, 0:1], minus_half[:, 0, :], ALU.pow).then_inc(rstd_set, 1)

                def scatter(n, m, _):
                    pool.wait_ge(outs, n + 3)
                    pool.sem_inc(scatters, 1)
                    pool.indirect_dma_start(out=out, out_offset=bass.IndirectOffsetOnAxis(ap=rows[:].bitcast(U32)[:, m, D + 1:D + 2], axis=0),
                                            in_=result[:, m, :], in_offset=None, bounds_check=NP - 1, oob_is_err=False).then_inc(row_out[m], 16)
                in_turn(pool, ETILES, [(3, root), (-1, scatter)])

            @block.scalar
            def _(act):
                act.sem_inc(gelus, 4)
                in_turn(act, ETILES, [(0, ffn_gelu(act, hid, gelus, tails))])

            @block.vector
            def _(dve):
                dve.sem_inc(zT_set, 2)
                dve.sem_inc(outs, 2)

                def statistics(n, m, turn):
                    dve.wait_ge(row_in[m], (turn + 1) * 16)
                    dve.bn_stats(stats[:, m % 4, :], rows[:, m, 0:D]).then_inc(stat4, 1)
                    dve.wait_ge(stat4, n + 1)
                    dve.sem_inc(stat4_seen, 1)
                    dve.bn_aggr(mv[:, m % 4, :], stats[:, m % 4, :]).then_inc(mv_set, 1)

                def norm(n, m, _):
                    dve.wait_ge(rstd_set, n + 1)
                    dve.tensor_scalar(z[:, m % 4, :], rows[:, m, 0:D], mv[:, m % 4, 0:1], rstd[:, m % 4, 1:2], ALU.subtract, ALU.mult).then_inc(z_set, 1)

                def finish(n, m, _):
                    dve.wait_ge(tails, n + 3)
                    dve.scalar_tensor_tensor(out=result[:, m, :], in0=psO[:, m % 2, 0:D], scalar=rows[:, m, D:D + 1], in1=rows[:, m, 0:D],
                                             op0=ALU.mult, op1=ALU.add).then_inc(outs, 1)
                in_turn(dve, ETILES, [(3, statistics), (2, norm), (1, ffn_zT(dve, turned, zT_set)), (-1, finish)])

            @block.tensor
            def _(pe):
                pe.wait_ge(wd_in, 16 * (NE + 1))
                pe.sem_inc(tails, 2)

                def product(n, m, _):
                    _, (e,) = nc.values_load_multi_w_load_instructions(
                        expert[0:1, bass.ds(n, 1)], engines=[PEE], min_val=0, max_val=NE - 1, skip_runtime_bounds_check_because=BOUNDED)
                    pe.wait_ge(gelus, n * 2 + 6)
                    pe.wait_ge(outs, n + 1)
                    for c in range(HC):
                        pe.matmul(psO[:, m % 2, 0:D], hT[:, m % 2, c, :], wd_s[:, bass.ds(e, 1), c, :].rearrange("p a o -> p (a o)"), start=(c == 0), stop=False)
                    pe.matmul(psO[:, m % 2, 0:D], ones[0:1, :], bd_s[:, bass.ds(e, 1), :].rearrange("p a o -> p (a o)"), start=False, stop=True).then_inc(tails, 1)
                in_turn(pe, ETILES, [(1, ffn_turn(pe, z_set, turned, zT_set)), (0, ffn_hidden(pe, zT_set, hid, gelus)), (-1, product)])
        ffn.close()


_INS = ["x", "src", "dst", "L0_gnn_weight", "L0_gnn_bias", "L0_ffn_W1", "L0_ffn_b1", "L0_ffn_Wg", "L0_ffn_bg", "L0_ffn_Wd", "L0_ffn_bd"]


def kernel(**inputs):
    import numpy as np
    import concourse.bacc as bacc
    from concourse.bass_utils import run_bass_kernel_spmd

    nodes, features = inputs["x"].shape
    padded = -(-nodes // P) * P
    nc = bacc.Bacc("TRN2", target_bir_lowering=False, num_devices=1)
    arrays, args = {}, []
    for name in _INS:
        a = np.ascontiguousarray(inputs[name])
        if name == "x":
            a = np.pad(a, ((0, padded - nodes), (0, 0)))
        arrays[f"in_{name}"] = a
        args.append(nc.dram_tensor(f"in_{name}", a.shape, mybir.dt.from_np(a.dtype), kind="ExternalInput").ap())
    out = nc.dram_tensor("out", (padded, features), F32, kind="ExternalOutput").ap()
    gnn_ffn_kernel(nc, *args, out)
    r = run_bass_kernel_spmd(nc, [arrays], core_ids=[0])
    return r.results[0]["out"][:nodes]
```
